# Optimizing a Trainium2 kernel written in Bass

```python
import numpy as np
import jax
import jax.numpy as jnp

def _softmax(x, axis=-1):
    return jax.nn.softmax(x, axis=axis)

def _gelu(x):
    return jax.nn.gelu(x, approximate=True)

def _silu(x):
    return jax.nn.silu(x)

def _sigmoid(x):
    return jax.nn.sigmoid(x)

def _layernorm(x, axis=-1, eps=1e-05):
    m = jnp.mean(x, axis=axis, keepdims=True)
    v = jnp.var(x, axis=axis, keepdims=True)
    return (x - m) / jnp.sqrt(v + eps)

def _scatter_add(tgt, idx, src, axis=0):
    return tgt.at[idx].add(src)

def _segment_sum(src, seg, n):
    return jax.ops.segment_sum(src, seg, n)
kernel_name = 'mk_vit_tower_postln_d4_tok_img256_r4_02247c'

def setup_inputs(seed: int=0):
    np.random.seed(seed)
    _w = jnp.asarray

    def _rec_inputs():
        import jax
        import jax.numpy as jnp
        _rk = jax.random.key(seed)
        x = -0.000520686 + 1.00062 * jax.random.normal(jax.random.fold_in(_rk, 1), (64, 64, 64, 4), jnp.float32)
        return x
    x = _rec_inputs()

    def _L0_tok_setup():
        import jax, jax.numpy as jnp
        import numpy as np
        HIDDEN_DIM = 128
        key = jax.random.key(seed)
        k_geom, k_w, k_b = jax.random.split(key, 3)
        B, N, F = (8, 64, 4)
        geom = jax.random.normal(k_geom, (B, N, N, F), dtype=jnp.float32)
        bound = 1.0 / np.sqrt(F)
        W = jax.random.uniform(k_w, (HIDDEN_DIM, F), dtype=jnp.float32, minval=-bound, maxval=bound)
        b = jax.random.uniform(k_b, (HIDDEN_DIM,), dtype=jnp.float32, minval=-bound, maxval=bound)
        return {'geom': geom, 'W': W, 'b': b}
    _L0_tok_all = _L0_tok_setup()
    _L0_tok_in = {k: v for k, v in _L0_tok_all.items() if k in ('W', 'b')}
    del _L0_tok_all

    def _L0_attn_setup():
        import jax, jax.numpy as jnp
        import numpy as np
        U_DECAY = 0.97
        X_DECAY = 0.97
        LN_EPS = 1e-05
        L1_EPS = 1e-12

        def _ln(x):
            m = jnp.mean(x, axis=-1, keepdims=True)
            v = jnp.mean((x - m) ** 2, axis=-1, keepdims=True)
            return (x - m) * jax.lax.rsqrt(v + LN_EPS)
        key = jax.random.key(seed)
        k0, k1, k2, k3 = jax.random.split(key, 4)
        B, T, d, n = (8, 64, 64, 256)
        embeddings = jax.random.normal(k0, (B, T, d), dtype=jnp.float32)
        E = jax.random.normal(k1, (d, n), dtype=jnp.float32) / n ** 0.5
        Dx = jax.random.normal(k2, (n, d), dtype=jnp.float32) / d ** 0.5
        Dy = jax.random.normal(k3, (n, d), dtype=jnp.float32) / d ** 0.5
        return {'embeddings': embeddings, 'E': E, 'Dx': Dx, 'Dy': Dy}
    _L0_attn_all = _L0_attn_setup()
    _L0_attn_in = {k: v for k, v in _L0_attn_all.items() if k in ('E', 'Dx', 'Dy')}
    del _L0_attn_all

    def _L0_ffn_setup():
        import jax, jax.numpy as jnp
        import numpy as np
        TOP_K = 2
        LN_EPS = 1e-05
        key = jax.random.key(seed)
        ks = jax.random.split(key, 8)
        B, S, D, E, H = (16, 256, 64, 8, 256)
        x = jax.random.normal(ks[0], (B, S, D), dtype=jnp.float32)
        Wr = jax.random.normal(ks[1], (D, E), dtype=jnp.float32) * 0.1
        br = jnp.zeros((E,), dtype=jnp.float32)
        ln_g = jnp.ones((E, D), dtype=jnp.float32)
        ln_b = jnp.zeros((E, D), dtype=jnp.float32)
        W1 = jax.random.normal(ks[2], (E, D, H), dtype=jnp.float32) * (1.0 / np.sqrt(D))
        b1 = jnp.zeros((E, H), dtype=jnp.float32)
        W2 = jax.random.normal(ks[3], (E, H, D), dtype=jnp.float32) * (1.0 / np.sqrt(H))
        b2 = jnp.zeros((E, D), dtype=jnp.float32)
        return {'x': x, 'Wr': Wr, 'br': br, 'ln_g': ln_g, 'ln_b': ln_b, 'W1': W1, 'b1': b1, 'W2': W2, 'b2': b2}
    _L0_ffn_all = _L0_ffn_setup()
    _L0_ffn_in = {k: v for k, v in _L0_ffn_all.items() if k in ('Wr', 'br', 'ln_g', 'ln_b', 'W1', 'b1', 'W2', 'b2')}
    del _L0_ffn_all

    def _L1_attn_setup():
        import jax, jax.numpy as jnp
        import numpy as np
        NHEAD = 8
        ATT_EPS = 1e-06
        LN_EPS = 1e-05

        def _layernorm(x, g, b):
            mu = jnp.mean(x, axis=-1, keepdims=True)
            var = jnp.mean(jnp.square(x - mu), axis=-1, keepdims=True)
            return (x - mu) * jax.lax.rsqrt(var + LN_EPS) * g + b
        key = jax.random.key(seed)
        ks = jax.random.split(key, 7)
        N, L, C = (4, 4096, 64)
        s = 1.0 / np.sqrt(C)
        return {'x': jax.random.normal(ks[0], (N, L, C), jnp.float32), 'Wq': jax.random.normal(ks[1], (C, C), jnp.float32) * s, 'Wk': jax.random.normal(ks[2], (C, C), jnp.float32) * s, 'Wv': jax.random.normal(ks[3], (C, C), jnp.float32) * s, 'Wm': jax.random.normal(ks[4], (C, C), jnp.float32) * s, 'W1': jax.random.normal(ks[5], (2 * C, 2 * C), jnp.float32) * (1.0 / np.sqrt(2 * C)), 'W2': jax.random.normal(ks[6], (2 * C, C), jnp.float32) * (1.0 / np.sqrt(2 * C)), 'g1': jnp.ones((C,), jnp.float32), 'b1': jnp.zeros((C,), jnp.float32), 'g2': jnp.ones((C,), jnp.float32), 'b2': jnp.zeros((C,), jnp.float32)}
    _L1_attn_all = _L1_attn_setup()
    _L1_attn_in = {k: v for k, v in _L1_attn_all.items() if k in ('Wq', 'Wk', 'Wv', 'Wm', 'W1', 'W2', 'g1', 'b1', 'g2', 'b2')}
    del _L1_attn_all

    def _L1_ffn_setup():
        import jax, jax.numpy as jnp
        import numpy as np
        B, T, IN_DIM = (64, 64, 64)
        HID, OUT_DIM = (128, 64)
        N_LAYERS, N_EXPERTS, N_SHARED = (2, 16, 1)
        key = jax.random.key(seed)
        ks = jax.random.split(key, 10)
        s = 0.02
        x = jax.random.normal(ks[0], (B, T, IN_DIM), dtype=jnp.float32)
        route_id = jax.random.randint(ks[1], (B,), 0, N_EXPERTS)
        Wi = jax.random.normal(ks[2], (HID, IN_DIM), dtype=jnp.float32) * s
        bi = jnp.zeros((HID,), dtype=jnp.float32)
        Wr = jax.random.normal(ks[3], (N_LAYERS, N_EXPERTS, HID, HID), dtype=jnp.float32) * s
        br = jax.random.normal(ks[4], (N_LAYERS, N_EXPERTS, HID), dtype=jnp.float32) * s
        Ws = jax.random.normal(ks[5], (N_LAYERS, N_SHARED, HID, HID), dtype=jnp.float32) * s
        bs = jax.random.normal(ks[6], (N_LAYERS, N_SHARED, HID), dtype=jnp.float32) * s
        Wo = jax.random.normal(ks[7], (OUT_DIM, HID), dtype=jnp.float32) * s
        bo = jnp.zeros((OUT_DIM,), dtype=jnp.float32)
        return {'x': x, 'route_id': route_id, 'Wi': Wi, 'bi': bi, 'Wr': Wr, 'br': br, 'Ws': Ws, 'bs': bs, 'Wo': Wo, 'bo': bo}
    _L1_ffn_all = _L1_ffn_setup()
    _L1_ffn_in = {k: v for k, v in _L1_ffn_all.items() if k in ('route_id', 'Wi', 'bi', 'Wr', 'br', 'Ws', 'bs', 'Wo', 'bo')}
    del _L1_ffn_all

    def _L2_attn_setup():
        import jax, jax.numpy as jnp
        import numpy as np
        B, L, H, C, D = (16, 1024, 64, 1, 64)

        def krylov(L, A, b, c):
            x = b[..., None]
            A_ = A
            while x.shape[-1] < L:
                x = jnp.concatenate([x, jnp.einsum('chij,chjt->chit', A_, x)], axis=-1)
                A_ = jnp.einsum('chij,chjk->chik', A_, A_)
            x = x[..., :L]
            return jnp.einsum('chd,chdl->chl', c, x)
        key = jax.random.key(seed)
        k1, k2 = jax.random.split(key)
        u = jax.random.normal(k1, (B, L, H), dtype=jnp.float32)
        c = jax.random.normal(k2, (C, H, D), dtype=jnp.float32)
        return {'u': u, 'c': c}
    _L2_attn_all = _L2_attn_setup()
    _L2_attn_in = {k: v for k, v in _L2_attn_all.items() if k in ('c',)}
    del _L2_attn_all

    def _L2_ffn_setup():
        import jax, jax.numpy as jnp
        import numpy as np
        D_MODEL = 64
        EXPERT_DIM = 128
        NUM_EXPERTS = 8
        TOP_K = 2
        SEQ_LEN = 512
        BATCH = 2
        key = jax.random.key(seed)
        ks = jax.random.split(key, 8)
        s = 0.02
        x = jax.random.normal(ks[0], (SEQ_LEN, BATCH, D_MODEL), dtype=jnp.float32)
        Wg = jax.random.normal(ks[1], (D_MODEL, NUM_EXPERTS), dtype=jnp.float32) * s
        bg = jax.random.normal(ks[2], (NUM_EXPERTS,), dtype=jnp.float32) * s
        bias = jnp.zeros((NUM_EXPERTS,), dtype=jnp.float32)
        W1 = jax.random.normal(ks[3], (NUM_EXPERTS, D_MODEL, EXPERT_DIM), dtype=jnp.float32) * s
        b1 = jax.random.normal(ks[4], (NUM_EXPERTS, EXPERT_DIM), dtype=jnp.float32) * s
        W2 = jax.random.normal(ks[5], (NUM_EXPERTS, EXPERT_DIM, D_MODEL), dtype=jnp.float32) * s
        b2 = jax.random.normal(ks[6], (NUM_EXPERTS, D_MODEL), dtype=jnp.float32) * s
        return {'x': x, 'Wg': Wg, 'bg': bg, 'bias': bias, 'W1': W1, 'b1': b1, 'W2': W2, 'b2': b2}
    _L2_ffn_all = _L2_ffn_setup()
    _L2_ffn_in = {k: v for k, v in _L2_ffn_all.items() if k in ('Wg', 'bg', 'bias', 'W1', 'b1', 'W2', 'b2')}
    del _L2_ffn_all

    def _L3_attn_setup():
        import jax, jax.numpy as jnp
        import numpy as np
        from jax import lax

        def _solve_im(u, a, W_B, b_B, dt):
            s = 1.0 / (1.0 + dt * dt * a)
            Bu = jnp.einsum('bnq,pq->bnp', u, W_B) + b_B
            f_x = dt * s * Bu
            f_z = dt * dt * s * Bu
            dsa = dt * s * a
            ds = dt * s

            def step(carry, f):
                x, z = carry
                fx, fz = f
                x_new = s * x - dsa * z + fx
                z_new = ds * x + s * z + fz
                return ((x_new, z_new), z_new)
            Bsz, _, q = u.shape
            init = (jnp.zeros((Bsz, q), u.dtype), jnp.zeros((Bsz, q), u.dtype))
            _, z_t = lax.scan(step, init, (jnp.moveaxis(f_x, 1, 0), jnp.moveaxis(f_z, 1, 0)))
            return jnp.moveaxis(z_t, 0, 1)

        def _reference_tuple_inner(u, a, W_B, b_B, W_C, b_C, W_D, b_D):
            N = u.shape[1]
            dt = 1.0 / N
            y = _solve_im(u, a, W_B, b_B, dt)
            x = jnp.einsum('bnq,pq->bnp', y, W_C) + b_C + (jnp.einsum('bnq,pq->bnp', u, W_D) + b_D)
            x = jax.nn.gelu(x, approximate=False)
            out = x * jax.nn.sigmoid(x) + u
            return (out, y)
        key = jax.random.key(seed)
        ks = jax.random.split(key, 8)
        B, N, q = (16, 1024, 64)
        sc = float(1.0 / np.sqrt(q))
        return {'u': jax.random.normal(ks[0], (B, N, q), jnp.float32), 'a': jax.random.normal(ks[1], (q,), jnp.float32), 'W_B': jax.random.normal(ks[2], (q, q), jnp.float32) * sc, 'b_B': jax.random.normal(ks[3], (q,), jnp.float32) * sc, 'W_C': jax.random.normal(ks[4], (q, q), jnp.float32) * sc, 'b_C': jax.random.normal(ks[5], (q,), jnp.float32) * sc, 'W_D': jax.random.normal(ks[6], (q, q), jnp.float32) * sc, 'b_D': jax.random.normal(ks[7], (q,), jnp.float32) * sc}
    _L3_attn_all = _L3_attn_setup()
    _L3_attn_in = {k: v for k, v in _L3_attn_all.items() if k in ('a', 'W_B', 'b_B', 'W_C', 'b_C', 'W_D', 'b_D')}
    del _L3_attn_all

    def _L3_ffn_setup():
        import jax, jax.numpy as jnp
        import numpy as np
        B, N, D = (16, 1024, 64)
        NUM_EXPERTS, TOP_K, HEADS = (4, 2, 4)
        N_EDGES = 262144
        LN_EPS = 1e-05

        def _layernorm(x, g, b):
            mu = x.mean(-1, keepdims=True)
            var = ((x - mu) ** 2).mean(-1, keepdims=True)
            return (x - mu) * jax.lax.rsqrt(var + LN_EPS) * g + b

        def _forward(x, edge_index, W_gat, att_src, att_dst, b_gat, ln_gamma, ln_beta, W1, b1, W2, b2):
            Bc, Nc, Dc = x.shape
            M = Bc * Nc
            x_flat = x.reshape(M, Dc)
            h = (x_flat @ W_gat).reshape(M, HEADS, NUM_EXPERTS)
            loops = jnp.arange(M, dtype=edge_index.dtype)
            src = jnp.concatenate([edge_index[0], loops])
            dst = jnp.concatenate([edge_index[1], loops])
            a_src = (h * att_src).sum(-1)
            a_dst = (h * att_dst).sum(-1)
            e = jax.nn.leaky_relu(a_src[src] + a_dst[dst], negative_slope=0.2)
            e_max = jax.ops.segment_max(e, dst, num_segments=M)
            ee = jnp.exp(e - e_max[dst])
            denom = jax.ops.segment_sum(ee, dst, num_segments=M)
            alpha = ee / (denom[dst] + 1e-16)
            msg = h[src] * alpha[:, :, None]
            agg = jax.ops.segment_sum(msg, dst, num_segments=M).reshape(M, HEADS * NUM_EXPERTS) + b_gat
            scores = _layernorm(agg, ln_gamma, ln_beta).reshape(M, HEADS, NUM_EXPERTS).mean(1)
            scores = scores.reshape(Bc, Nc, NUM_EXPERTS)
            topk_s, topk_i = jax.lax.top_k(scores, TOP_K)
            w = jax.nn.softmax(topk_s, axis=-1)
            out = jnp.zeros_like(x)
            for ei in range(NUM_EXPERTS):
                g = jnp.where(topk_i == ei, w, 0.0).sum(-1)
                hh = jax.nn.gelu(x @ W1[ei] + b1[ei], approximate=False)
                out = out + g[..., None] * (hh @ W2[ei] + b2[ei])
            return out
        key = jax.random.key(seed)
        ks = jax.random.split(key, 8)
        s = 0.05
        return {'x': jax.random.normal(ks[0], (B, N, D), jnp.float32), 'W_gat': jax.random.normal(ks[1], (D, HEADS * NUM_EXPERTS), jnp.float32) * s, 'att_src': jax.random.normal(ks[2], (HEADS, NUM_EXPERTS), jnp.float32) * s, 'att_dst': jax.random.normal(ks[3], (HEADS, NUM_EXPERTS), jnp.float32) * s, 'b_gat': jnp.zeros((HEADS * NUM_EXPERTS,), jnp.float32), 'ln_gamma': jnp.ones((HEADS * NUM_EXPERTS,), jnp.float32), 'ln_beta': jnp.zeros((HEADS * NUM_EXPERTS,), jnp.float32), 'W1': jax.random.normal(ks[4], (NUM_EXPERTS, D, 2 * D), jnp.float32) * s, 'b1': jnp.zeros((NUM_EXPERTS, 2 * D), jnp.float32), 'W2': jax.random.normal(ks[5], (NUM_EXPERTS, 2 * D, D), jnp.float32) * s, 'b2': jnp.zeros((NUM_EXPERTS, D), jnp.float32), 'edge_index': jax.random.randint(ks[6], (2, N_EDGES), 0, B * N, jnp.int32)}
    _L3_ffn_all = _L3_ffn_setup()
    _L3_ffn_in = {k: v for k, v in _L3_ffn_all.items() if k in ('W_gat', 'att_src', 'att_dst', 'b_gat', 'ln_gamma', 'ln_beta', 'W1', 'b1', 'W2', 'b2', 'edge_index')}
    del _L3_ffn_all
    return {'x': x, 'L0_tok_W': _L0_tok_in['W'], 'L0_tok_b': _L0_tok_in['b'], 'L0_attn_E': _L0_attn_in['E'], 'L0_attn_Dx': _L0_attn_in['Dx'], 'L0_attn_Dy': _L0_attn_in['Dy'], 'L0_ffn_Wr': _L0_ffn_in['Wr'], 'L0_ffn_br': _L0_ffn_in['br'], 'L0_ffn_ln_g': _L0_ffn_in['ln_g'], 'L0_ffn_ln_b': _L0_ffn_in['ln_b'], 'L0_ffn_W1': _L0_ffn_in['W1'], 'L0_ffn_b1': _L0_ffn_in['b1'], 'L0_ffn_W2': _L0_ffn_in['W2'], 'L0_ffn_b2': _L0_ffn_in['b2'], 'L1_attn_Wq': _L1_attn_in['Wq'], 'L1_attn_Wk': _L1_attn_in['Wk'], 'L1_attn_Wv': _L1_attn_in['Wv'], 'L1_attn_Wm': _L1_attn_in['Wm'], 'L1_attn_W1': _L1_attn_in['W1'], 'L1_attn_W2': _L1_attn_in['W2'], 'L1_attn_g1': _L1_attn_in['g1'], 'L1_attn_b1': _L1_attn_in['b1'], 'L1_attn_g2': _L1_attn_in['g2'], 'L1_attn_b2': _L1_attn_in['b2'], 'L1_ffn_route_id': _L1_ffn_in['route_id'], 'L1_ffn_Wi': _L1_ffn_in['Wi'], 'L1_ffn_bi': _L1_ffn_in['bi'], 'L1_ffn_Wr': _L1_ffn_in['Wr'], 'L1_ffn_br': _L1_ffn_in['br'], 'L1_ffn_Ws': _L1_ffn_in['Ws'], 'L1_ffn_bs': _L1_ffn_in['bs'], 'L1_ffn_Wo': _L1_ffn_in['Wo'], 'L1_ffn_bo': _L1_ffn_in['bo'], 'L2_attn_c': _L2_attn_in['c'], 'L2_ffn_Wg': _L2_ffn_in['Wg'], 'L2_ffn_bg': _L2_ffn_in['bg'], 'L2_ffn_bias': _L2_ffn_in['bias'], 'L2_ffn_W1': _L2_ffn_in['W1'], 'L2_ffn_b1': _L2_ffn_in['b1'], 'L2_ffn_W2': _L2_ffn_in['W2'], 'L2_ffn_b2': _L2_ffn_in['b2'], 'L3_attn_a': _L3_attn_in['a'], 'L3_attn_W_B': _L3_attn_in['W_B'], 'L3_attn_b_B': _L3_attn_in['b_B'], 'L3_attn_W_C': _L3_attn_in['W_C'], 'L3_attn_b_C': _L3_attn_in['b_C'], 'L3_attn_W_D': _L3_attn_in['W_D'], 'L3_attn_b_D': _L3_attn_in['b_D'], 'L3_ffn_W_gat': _L3_ffn_in['W_gat'], 'L3_ffn_att_src': _L3_ffn_in['att_src'], 'L3_ffn_att_dst': _L3_ffn_in['att_dst'], 'L3_ffn_b_gat': _L3_ffn_in['b_gat'], 'L3_ffn_ln_gamma': _L3_ffn_in['ln_gamma'], 'L3_ffn_ln_beta': _L3_ffn_in['ln_beta'], 'L3_ffn_W1': _L3_ffn_in['W1'], 'L3_ffn_b1': _L3_ffn_in['b1'], 'L3_ffn_W2': _L3_ffn_in['W2'], 'L3_ffn_b2': _L3_ffn_in['b2'], 'L3_ffn_edge_index': _L3_ffn_in['edge_index']}

def reference(x, L0_tok_W, L0_tok_b, L0_attn_E, L0_attn_Dx, L0_attn_Dy, L0_ffn_Wr, L0_ffn_br, L0_ffn_ln_g, L0_ffn_ln_b, L0_ffn_W1, L0_ffn_b1, L0_ffn_W2, L0_ffn_b2, L1_attn_Wq, L1_attn_Wk, L1_attn_Wv, L1_attn_Wm, L1_attn_W1, L1_attn_W2, L1_attn_g1, L1_attn_b1, L1_attn_g2, L1_attn_b2, L1_ffn_route_id, L1_ffn_Wi, L1_ffn_bi, L1_ffn_Wr, L1_ffn_br, L1_ffn_Ws, L1_ffn_bs, L1_ffn_Wo, L1_ffn_bo, L2_attn_c, L2_ffn_Wg, L2_ffn_bg, L2_ffn_bias, L2_ffn_W1, L2_ffn_b1, L2_ffn_W2, L2_ffn_b2, L3_attn_a, L3_attn_W_B, L3_attn_b_B, L3_attn_W_C, L3_attn_b_C, L3_attn_W_D, L3_attn_b_D, L3_ffn_W_gat, L3_ffn_att_src, L3_ffn_att_dst, L3_ffn_b_gat, L3_ffn_ln_gamma, L3_ffn_ln_beta, L3_ffn_W1, L3_ffn_b1, L3_ffn_W2, L3_ffn_b2, L3_ffn_edge_index):
    import jax
    import jax.numpy as jnp

    def _L0_tok_ref(geom, W, b):
        import jax, jax.numpy as jnp
        import numpy as np
        HIDDEN_DIM = 128
        bias = jnp.einsum('bijf,hf->bijh', geom, W) + b
        return bias.mean(-1)

    def _L0_attn_ref(embeddings, E, Dx, Dy):
        import jax, jax.numpy as jnp
        import numpy as np
        U_DECAY = 0.97
        X_DECAY = 0.97
        LN_EPS = 1e-05
        L1_EPS = 1e-12

        def _ln(x):
            m = jnp.mean(x, axis=-1, keepdims=True)
            v = jnp.mean((x - m) ** 2, axis=-1, keepdims=True)
            return (x - m) * jax.lax.rsqrt(v + LN_EPS)
        B, T, d = embeddings.shape
        n = E.shape[1]

        def step(carry, v_prev):
            x_state, rho = carry
            x_update = jax.nn.relu(v_prev @ Dx.T)
            x_t = X_DECAY * x_state + x_update
            x_t = x_t / jnp.maximum(jnp.sum(jnp.abs(x_t), axis=-1, keepdims=True), L1_EPS)
            a_star = jnp.einsum('bdn,bn->bd', rho, x_t)
            y_core = _ln(a_star) @ Dy.T
            y_t = jax.nn.relu(y_core) * jax.nn.relu(x_t)
            v_star = _ln(y_t @ E.T)
            rho_t = U_DECAY * rho + _ln(v_prev)[:, :, None] * x_t[:, None, :]
            return ((x_t, rho_t), v_star)
        x0 = jnp.zeros((B, n), dtype=embeddings.dtype)
        rho0 = jnp.zeros((B, d, n), dtype=embeddings.dtype)
        _, vs = jax.lax.scan(step, (x0, rho0), jnp.swapaxes(embeddings, 0, 1))
        return jnp.swapaxes(vs, 0, 1)

    def _L0_ffn_ref(x, Wr, br, ln_g, ln_b, W1, b1, W2, b2):
        import jax, jax.numpy as jnp
        import numpy as np
        TOP_K = 2
        LN_EPS = 1e-05
        B, S, D = x.shape
        N = B * S
        xt = x.reshape(N, D)
        logits = xt @ Wr + br
        probs = jax.nn.softmax(logits, axis=-1)
        top_p, top_idx = jax.lax.top_k(probs, TOP_K)
        weights = top_p / top_p.sum(axis=-1, keepdims=True)
        mu = xt.mean(axis=-1, keepdims=True)
        var = ((xt - mu) ** 2).mean(axis=-1, keepdims=True)
        xn = (xt - mu) * jax.lax.rsqrt(var + LN_EPS)
        xe = xn[None, :, :] * ln_g[:, None, :] + ln_b[:, None, :]
        h = jax.nn.gelu(jnp.einsum('end,edh->enh', xe, W1) + b1[:, None, :], approximate=False)
        y = jnp.einsum('enh,ehd->end', h, W2) + b2[:, None, :]
        y_tok = jnp.transpose(y, (1, 0, 2))
        sel = jnp.take_along_axis(y_tok, top_idx[:, :, None], axis=1)
        out = (weights[:, :, None] * sel).sum(axis=1)
        return out.reshape(B, S, D)

    def _L1_attn_ref(x, Wq, Wk, Wv, Wm, W1, W2, g1, b1, g2, b2):
        import jax, jax.numpy as jnp
        import numpy as np
        NHEAD = 8
        ATT_EPS = 1e-06
        LN_EPS = 1e-05

        def _layernorm(x, g, b):
            mu = jnp.mean(x, axis=-1, keepdims=True)
            var = jnp.mean(jnp.square(x - mu), axis=-1, keepdims=True)
            return (x - mu) * jax.lax.rsqrt(var + LN_EPS) * g + b
        N, L, C = x.shape
        H = NHEAD
        D = C // H
        q = (x @ Wq).reshape(N, L, H, D)
        k = (x @ Wk).reshape(N, L, H, D)
        v = (x @ Wv).reshape(N, L, H, D)
        Q = jax.nn.elu(q) + 1.0
        K = jax.nn.elu(k) + 1.0
        v = v / L
        KV = jnp.einsum('nshd,nshv->nhdv', K, v)
        Z = 1.0 / (jnp.einsum('nlhd,nhd->nlh', Q, K.sum(axis=1)) + ATT_EPS)
        msg = jnp.einsum('nlhd,nhdv,nlh->nlhv', Q, KV, Z) * L
        msg = msg.reshape(N, L, C) @ Wm
        msg = _layernorm(msg, g1, b1)
        h = jnp.concatenate([x, msg], axis=-1) @ W1
        h = jax.nn.relu(h) @ W2
        msg = _layernorm(h, g2, b2)
        return x + msg

    def _L1_ffn_ref(x, route_id, Wi, bi, Wr, br, Ws, bs, Wo, bo):
        import jax, jax.numpy as jnp
        import numpy as np
        B, T, IN_DIM = (64, 64, 64)
        HID, OUT_DIM = (128, 64)
        N_LAYERS, N_EXPERTS, N_SHARED = (2, 16, 1)
        flat = x.reshape(-1, x.shape[-1])
        n_tok = flat.shape[0]
        route = jnp.repeat(route_id, n_tok // route_id.shape[0])
        h = jax.nn.relu(flat @ Wi.T + bi)
        n_layers, n_experts = (Wr.shape[0], Wr.shape[1])
        for l in range(n_layers):
            shared = (jnp.einsum('nd,shd->snh', h, Ws[l]) + bs[l][:, None, :]).mean(axis=0)
            routed = jnp.zeros_like(h)
            for e in range(n_experts):
                ye = h @ Wr[l, e].T + br[l, e]
                routed = routed + jnp.where((route == e)[:, None], ye, 0.0)
            h = jax.nn.relu(shared + routed + h)
        out = h @ Wo.T + bo
        return out.reshape(*x.shape[:-1], out.shape[-1])

    def _L2_attn_ref(u, c):
        import jax, jax.numpy as jnp
        import numpy as np
        B, L, H, C, D = (16, 1024, 64, 1, 64)

        def krylov(L, A, b, c):
            x = b[..., None]
            A_ = A
            while x.shape[-1] < L:
                x = jnp.concatenate([x, jnp.einsum('chij,chjt->chit', A_, x)], axis=-1)
                A_ = jnp.einsum('chij,chjk->chik', A_, A_)
            x = x[..., :L]
            return jnp.einsum('chd,chdl->chl', c, x)
        Cc, Hh, Dd = c.shape
        A = jnp.zeros((Dd, Dd), c.dtype).at[1:, :-1].set(jnp.eye(Dd - 1, dtype=c.dtype))
        A = jnp.broadcast_to(A, (Cc, Hh, Dd, Dd))
        b = jnp.zeros((Dd,), c.dtype).at[0].set(1.0)
        b = jnp.broadcast_to(b, (Cc, Hh, Dd))
        ub = jnp.transpose(u, (0, 2, 1))
        l = ub.shape[-1]
        f = krylov(l, A, b, c)
        n = 2 * l
        u_f = jnp.fft.rfft(ub, n=n)
        v_f = jnp.fft.rfft(f, n=n)
        y_f = jnp.einsum('bhl,chl->bchl', u_f, v_f)
        y = jnp.fft.irfft(y_f, n=n)[..., :l]
        y = y.reshape(y.shape[0], -1, l)
        return jnp.transpose(y, (0, 2, 1))

    def _L2_ffn_ref(x, Wg, bg, bias, W1, b1, W2, b2):
        import jax, jax.numpy as jnp
        import numpy as np
        D_MODEL = 64
        EXPERT_DIM = 128
        NUM_EXPERTS = 8
        TOP_K = 2
        SEQ_LEN = 512
        BATCH = 2
        x_flat = x.reshape(-1, D_MODEL)
        gate_logits = x_flat @ Wg + bg + bias
        topk_vals, topk_idx = jax.lax.top_k(gate_logits, TOP_K)
        topk_w = jax.nn.softmax(topk_vals, axis=-1)
        combine = (jax.nn.one_hot(topk_idx, NUM_EXPERTS, dtype=x.dtype) * topk_w[..., None]).sum(axis=1)
        h = jax.nn.relu(jnp.einsum('td,edh->teh', x_flat, W1) + b1)
        y = jnp.einsum('teh,ehd->ted', h, W2) + b2
        out = jnp.einsum('ted,te->td', y, combine)
        return out.reshape(x.shape)

    def _L3_attn_ref(u, a, W_B, b_B, W_C, b_C, W_D, b_D):
        import jax, jax.numpy as jnp
        import numpy as np
        from jax import lax

        def _solve_im(u, a, W_B, b_B, dt):
            s = 1.0 / (1.0 + dt * dt * a)
            Bu = jnp.einsum('bnq,pq->bnp', u, W_B) + b_B
            f_x = dt * s * Bu
            f_z = dt * dt * s * Bu
            dsa = dt * s * a
            ds = dt * s

            def step(carry, f):
                x, z = carry
                fx, fz = f
                x_new = s * x - dsa * z + fx
                z_new = ds * x + s * z + fz
                return ((x_new, z_new), z_new)
            Bsz, _, q = u.shape
            init = (jnp.zeros((Bsz, q), u.dtype), jnp.zeros((Bsz, q), u.dtype))
            _, z_t = lax.scan(step, init, (jnp.moveaxis(f_x, 1, 0), jnp.moveaxis(f_z, 1, 0)))
            return jnp.moveaxis(z_t, 0, 1)

        def _reference_tuple_inner(u, a, W_B, b_B, W_C, b_C, W_D, b_D):
            N = u.shape[1]
            dt = 1.0 / N
            y = _solve_im(u, a, W_B, b_B, dt)
            x = jnp.einsum('bnq,pq->bnp', y, W_C) + b_C + (jnp.einsum('bnq,pq->bnp', u, W_D) + b_D)
            x = jax.nn.gelu(x, approximate=False)
            out = x * jax.nn.sigmoid(x) + u
            return (out, y)
        return _reference_tuple_inner(u, a, W_B, b_B, W_C, b_C, W_D, b_D)[0]

    def _L3_ffn_ref(x, W_gat, att_src, att_dst, b_gat, ln_gamma, ln_beta, W1, b1, W2, b2, edge_index):
        import jax, jax.numpy as jnp
        import numpy as np
        B, N, D = (16, 1024, 64)
        NUM_EXPERTS, TOP_K, HEADS = (4, 2, 4)
        N_EDGES = 262144
        LN_EPS = 1e-05

        def _layernorm(x, g, b):
            mu = x.mean(-1, keepdims=True)
            var = ((x - mu) ** 2).mean(-1, keepdims=True)
            return (x - mu) * jax.lax.rsqrt(var + LN_EPS) * g + b

        def _forward(x, edge_index, W_gat, att_src, att_dst, b_gat, ln_gamma, ln_beta, W1, b1, W2, b2):
            Bc, Nc, Dc = x.shape
            M = Bc * Nc
            x_flat = x.reshape(M, Dc)
            h = (x_flat @ W_gat).reshape(M, HEADS, NUM_EXPERTS)
            loops = jnp.arange(M, dtype=edge_index.dtype)
            src = jnp.concatenate([edge_index[0], loops])
            dst = jnp.concatenate([edge_index[1], loops])
            a_src = (h * att_src).sum(-1)
            a_dst = (h * att_dst).sum(-1)
            e = jax.nn.leaky_relu(a_src[src] + a_dst[dst], negative_slope=0.2)
            e_max = jax.ops.segment_max(e, dst, num_segments=M)
            ee = jnp.exp(e - e_max[dst])
            denom = jax.ops.segment_sum(ee, dst, num_segments=M)
            alpha = ee / (denom[dst] + 1e-16)
            msg = h[src] * alpha[:, :, None]
            agg = jax.ops.segment_sum(msg, dst, num_segments=M).reshape(M, HEADS * NUM_EXPERTS) + b_gat
            scores = _layernorm(agg, ln_gamma, ln_beta).reshape(M, HEADS, NUM_EXPERTS).mean(1)
            scores = scores.reshape(Bc, Nc, NUM_EXPERTS)
            topk_s, topk_i = jax.lax.top_k(scores, TOP_K)
            w = jax.nn.softmax(topk_s, axis=-1)
            out = jnp.zeros_like(x)
            for ei in range(NUM_EXPERTS):
                g = jnp.where(topk_i == ei, w, 0.0).sum(-1)
                hh = jax.nn.gelu(x @ W1[ei] + b1[ei], approximate=False)
                out = out + g[..., None] * (hh @ W2[ei] + b2[ei])
            return out
        return _forward(x, edge_index, W_gat, att_src, att_dst, b_gat, ln_gamma, ln_beta, W1, b1, W2, b2)
    h = _L0_tok_ref(x, L0_tok_W, L0_tok_b)
    h = _layernorm(h + _L0_attn_ref(h, L0_attn_E, L0_attn_Dx, L0_attn_Dy), axis=-1)
    h = _layernorm(h + _L0_ffn_ref(h, L0_ffn_Wr, L0_ffn_br, L0_ffn_ln_g, L0_ffn_ln_b, L0_ffn_W1, L0_ffn_b1, L0_ffn_W2, L0_ffn_b2), axis=-1)
    h = _layernorm(h + _L1_attn_ref(h, L1_attn_Wq, L1_attn_Wk, L1_attn_Wv, L1_attn_Wm, L1_attn_W1, L1_attn_W2, L1_attn_g1, L1_attn_b1, L1_attn_g2, L1_attn_b2), axis=-1)
    h = _layernorm(h + _L1_ffn_ref(h, L1_ffn_route_id, L1_ffn_Wi, L1_ffn_bi, L1_ffn_Wr, L1_ffn_br, L1_ffn_Ws, L1_ffn_bs, L1_ffn_Wo, L1_ffn_bo), axis=-1)
    h = _layernorm(h + _L2_attn_ref(h, L2_attn_c), axis=-1)
    h = _layernorm(h + _L2_ffn_ref(h, L2_ffn_Wg, L2_ffn_bg, L2_ffn_bias, L2_ffn_W1, L2_ffn_b1, L2_ffn_W2, L2_ffn_b2), axis=-1)
    h = _layernorm(h + _L3_attn_ref(h, L3_attn_a, L3_attn_W_B, L3_attn_b_B, L3_attn_W_C, L3_attn_b_C, L3_attn_W_D, L3_attn_b_D), axis=-1)
    h = _layernorm(h + _L3_ffn_ref(h, L3_ffn_W_gat, L3_ffn_att_src, L3_ffn_att_dst, L3_ffn_b_gat, L3_ffn_ln_gamma, L3_ffn_ln_beta, L3_ffn_W1, L3_ffn_b1, L3_ffn_W2, L3_ffn_b2, L3_ffn_edge_index), axis=-1)
    return h

_drawn_inputs = setup_inputs


def setup_inputs(seed=0):
    import zlib

    import numpy as np

    out = dict(_drawn_inputs(seed))
    spreads = {'L0_ffn_br': (0.0, 0.1),
     'L0_ffn_ln_g': (1.0, 0.2),
     'L0_ffn_ln_b': (0.0, 0.1),
     'L0_ffn_b1': (0.0, 0.1),
     'L0_ffn_b2': (0.0, 0.1),
     'L1_attn_g1': (1.0, 0.2),
     'L1_attn_b1': (0.0, 0.1),
     'L1_attn_g2': (1.0, 0.2),
     'L1_attn_b2': (0.0, 0.1),
     'L1_ffn_bi': (0.0, 0.1),
     'L1_ffn_bo': (0.0, 0.1),
     'L2_ffn_bias': (0.0, 0.1),
     'L3_ffn_b_gat': (0.0, 0.1),
     'L3_ffn_ln_gamma': (1.0, 0.2),
     'L3_ffn_ln_beta': (0.0, 0.1),
     'L3_ffn_b1': (0.0, 0.342),
     'L3_ffn_b2': (0.0, 0.1)}
    factors = {'L0_tok_b': 200.0,
     'L1_ffn_Wr': 3.276,
     'L1_ffn_br': 5.098,
     'L1_ffn_Ws': 3.946,
     'L1_ffn_bs': 3.933,
     'L2_ffn_bg': 7.051,
     'L2_ffn_W1': 3.106,
     'L2_ffn_b1': 22.535,
     'L3_attn_a': 3.274,
     'L3_ffn_att_src': 24.505,
     'L3_ffn_att_dst': 79.944,
     'L2_ffn_b2': 2.824,
     'L3_attn_b_B': 3.101,
     'L1_attn_Wq': 3.442}
    for name, (base, spread) in spreads.items():
        noise = np.random.default_rng([zlib.crc32(name.encode()), seed]).standard_normal(out[name].shape)
        drawn = base * np.exp(spread * noise) if base else spread * noise
        out[name] = jnp.asarray(drawn.astype(out[name].dtype))
    for name, factor in factors.items():
        out[name] = (out[name] * factor).astype(out[name].dtype)
    return out
```

```python
from contextlib import ExitStack

import concourse.bass as bass
from concourse import mybir
from concourse.alu_op_type import AluOpType as ALU

F32 = mybir.dt.float32
I32 = mybir.dt.int32
U32 = mybir.dt.uint32
ACT = mybir.ActivationFunctionType
AX = mybir.AxisListType.X

P = 128
B, T, D = 64, 64, 64
TOK = B * T
HALF = TOK // 2
GC = 512
G = HALF // GC
TJ = GC // P
GB = GC // T
NH = 256
EPS = 1e-5
STAGES = 99


class Stage:

    def __init__(self, nc, name):
        self.nc, self.name, self.ctx, self.all = nc, name, ExitStack(), []

    def sem(self, what):
        s = self.nc.alloc_semaphore(f"{self.name}_{what}")
        self.all.append(s)
        return s

    def sems(self, names):
        return [self.sem(n) for n in names.split()]

    def sb(self, what, shape, dt=F32):
        return self.ctx.enter_context(self.nc.sbuf_tensor(f"{self.name}_{what}", shape, dt))

    def ps(self, what, shape):
        return self.ctx.enter_context(self.nc.psum_tensor(f"{self.name}_{what}", shape, F32))

    def end(self):
        self.ctx.close()
        self.nc.clear_and_free_semaphores(self.all)
        self.nc.all_engine_barrier()


class Norm:

    def __init__(self, st, name, con, centred_ps, var_ps, sq, std):
        self.con, self.cp, self.vp, self.sq, self.std = con, centred_ps, var_ps, sq, std
        self.centred, self.squared, self.averaged, self.rooted, self.inverted, self.normed = st.sems(
            " ".join(f"{name}_{x}" for x in "centred squared averaged rooted inverted normed".split()))

    def tensor_centre(self, pe, src, src_ready, g):
        pe.wait_ge(src_ready, g + 1)
        pe.matmul(self.cp, self.con["centre"], src, start=True, stop=True).then_inc(self.centred, 1)

    def tensor_average(self, pe, g):
        pe.wait_ge(self.squared, g + 1)
        pe.matmul(self.vp, self.con["average"], self.sq, start=True, stop=True).then_inc(self.averaged, 1)

    def scalar(self, act, g):
        act.wait_ge(self.centred, g + 1)
        act.activation(self.sq, self.cp, ACT.Square).then_inc(self.squared, 1)
        act.wait_ge(self.averaged, g + 1)
        act.activation(self.std, self.vp, ACT.Sqrt, bias=self.con["eps"]).then_inc(self.rooted, 1)

    def vector(self, v, out, g):
        v.wait_ge(self.rooted, g + 1)
        v.reciprocal(self.std, self.std).then_inc(self.inverted, 1)
        v.wait_ge(self.inverted, g + 1)
        v.tensor_tensor(out, self.cp, self.std, ALU.mult).then_inc(self.normed, 1)


def group(t, g):
    return t[:, bass.ds(g * GC, GC)]


def tokenizer(nc, con, X, a):
    st = Stage(nc, "tok")
    F = 4
    wb = st.sb("wb", [P, F + 1])
    mean = st.sb("mean", [P, F + 1])
    xin = [st.sb(f"xin{k}", [P, TJ, 2, D * F]) for k in range(G)]
    tm = [st.sb(f"tm{k}", [P, GC]) for k in range(G)]
    mean_ps = st.ps("mean_ps", [P, F + 1])
    turn_ps = [st.ps(f"turn_ps{k}", [P, GC]) for k in range(G)]
    consts_in, w_in, meaned, mean_kept, summed, turned, kept = st.sems(
        "consts_in w_in meaned mean_kept summed turned kept")
    x_in = [st.sem(f"x_in{k}") for k in range(G)]
    xr = a["x"].rearrange("(h k j p) c -> k p j h c", h=2, k=G, j=TJ, p=P)
    block = st.ctx.enter_context(nc.Block())

    @block.sync
    def _(sp):
        sp.dma_start(con["consts"], a["consts"]).then_inc(consts_in, 16)
        sp.dma_start(wb[:, :], a["tok"]).then_inc(w_in, 16)
        for k in range(G):
            for j in range(TJ):
                sp.dma_start(xin[k][:, j, :, :], xr[k][:, j, :, :]).then_inc(x_in[k], 16)

    @block.tensor
    def _(pe):
        pe.wait_ge(consts_in, 16)
        pe.wait_ge(w_in, 16)
        pe.matmul(mean_ps[:, :], con["mean128"], wb[:, :], start=True, stop=True).then_inc(meaned, 1)
        for k in range(G):
            pe.wait_ge(summed, F * k + F)
            for j in range(TJ):
                mm = pe.transpose(turn_ps[k][:, j * P:(j + 1) * P], tm[k][:, j * P:(j + 1) * P], con["ident"])
            mm.then_inc(turned, 1)

    @block.vector
    def _(v):
        v.wait_ge(meaned, 1)
        v.tensor_copy(mean[:, :], mean_ps[:, :]).then_inc(mean_kept, 1)
        v.wait_ge(mean_kept, 1)
        for k in range(G):
            v.wait_ge(x_in[k], 16 * TJ)
            xf = xin[k][:, :, :, :].rearrange("p j h (d f) -> p (j h d) f", f=F)
            v.tensor_scalar(tm[k][:, :], xf[:, :, 0], mean[:, 0:1], mean[:, F:F + 1], ALU.mult,
                            ALU.add).then_inc(summed, 1)
            for f in range(1, F):
                v.wait_ge(summed, F * k + f)
                v.scalar_tensor_tensor(tm[k][:, :], xf[:, :, f], mean[:, f:f + 1], tm[k][:, :],
                                       ALU.mult, ALU.add).then_inc(summed, 1)

    @block.scalar
    def _(act):
        for k in range(G):
            act.wait_ge(turned, k + 1)
            act.activation(X[:, k * GC:(k + 1) * GC], turn_ps[k][:, :], ACT.Copy).then_inc(kept, 1)

    st.end()


def first_attention(nc, con, X, a):
    st = Stage(nc, "att0")
    A = 0.97
    BIG = 1e12
    dx = st.sb("dx", [P, 2, NH])
    dy = st.sb("dy", [P, 2, NH])
    et = st.sb("et", [P, 2, 2, P])
    decay = st.sb("decay", [P, GC])
    later = st.sb("later", [P, 2 * GC])
    xg, nv, u = st.sb("xg", [P, GC]), st.sb("nv", [P, GC]), st.sb("u", [P, 4, GC])
    sq, std = st.sb("sq", [P, GC]), st.sb("std", [P, GC])
    run, q, sig, r, keep = [st.sb(n, [P, 2 * GC]) for n in ("run", "q", "sig", "r", "keep")]
    ur, xs = st.sb("ur", [P, 4, GC]), st.sb("xs", [P, 4, GC])
    gm, nvt = st.sb("gm", [P, 2, GC]), st.sb("nvt", [P, GC])
    an, asum, y, vs, hsum = st.sb("an", [P, GC]), st.sb("asum", [P, GC]), st.sb("y", [P, 4, GC]), st.sb("vs", [P, GC]), st.sb("hsum", [P, GC])
    big = st.ps("big", [P, 4, GC])
    sums = st.ps("sums", [P, 2, GC])
    cp, vp = st.ps("cp", [P, GC]), st.ps("vp", [P, GC])
    weights_in, grouped, u_made, u_kept, u_summed = st.sems("weights_in grouped u_made u_kept u_summed")
    ran, capped, q_raw, q_first, q_made, s_raw, s_first, sig_made = st.sems("ran capped q_raw q_first q_made s_raw s_first sig_made")
    raw, raw_first, guarded, inverted, kept, scaled, scanned = st.sems("raw raw_first guarded inverted kept scaled scanned")
    grams, masked, v_turned, v_kept, attended, a_kept, y_made, gated, v_made, vs_kept, added = st.sems(
        "grams masked v_turned v_kept attended a_kept y_made gated v_made vs_kept added")
    n_v = Norm(st, "nv", con, cp[:, :], vp[:, :], sq[:, :], std[:, :])
    n_a = Norm(st, "na", con, cp[:, :], vp[:, :], sq[:, :], std[:, :])
    n_s = Norm(st, "ns", con, cp[:, :], vp[:, :], sq[:, :], std[:, :])
    n_o = Norm(st, "no", con, cp[:, :], vp[:, :], sq[:, :], std[:, :])
    steps = lambda t: t[:, :].rearrange("p (b t) -> p b t", t=T)
    flat_sums = sums[:, :, :].rearrange("p h c -> p (h c)")
    block = st.ctx.enter_context(nc.Block())

    @block.sync
    def _(sp):
        for dst, src in ((dx[:, :, :], "dx"), (dy[:, :, :], "dy"), (et[:, :, :, :], "et"),
                         (decay[:, :], "decay"), (later[:, :], "later")):
            sp.dma_start(dst, a[src]).then_inc(weights_in, 16)

    @block.tensor
    def _(pe):
        pe.wait_ge(weights_in, 80)
        with pe.Fori(0, G) as g:
            n_v.tensor_centre(pe, xg[:, :], grouped, g)
            for h in range(2):
                for c in range(2):
                    mm = pe.matmul(big[:, 2 * h + c, :], dx[:, h, c * P:(c + 1) * P], xg[:, :], start=True, stop=True)
            mm.then_inc(u_made, 1)
            n_v.tensor_average(pe, g)
            pe.wait_ge(u_kept, g + 1)
            for h in range(2):
                for c in range(2):
                    mm = pe.matmul(sums[:, h, :], con["ones"], u[:, 2 * h + c, :], start=c == 0, stop=c == 1)
            mm.then_inc(u_summed, 1)
            pe.wait_ge(n_v.normed, g + 1)
            for j in range(TJ):
                mm = pe.transpose(big[:, 2, j * P:(j + 1) * P], nv[:, j * P:(j + 1) * P], con["ident"])
            mm.then_inc(v_turned, 1)
            pe.wait_ge(scanned, 4 * g + 4)
            for h in range(2):
                for j in range(TJ):
                    for c in range(2):
                        xt = xs[:, 2 * h + c, j * P:(j + 1) * P]
                        mm = pe.matmul(big[:, h, j * P:(j + 1) * P], xt, xt, start=c == 0, stop=c == 1)
            mm.then_inc(grams, 1)
            pe.wait_ge(masked, g + 1)
            pe.wait_ge(v_kept, g + 1)
            for h in range(2):
                for j in range(TJ):
                    mm = pe.matmul(big[h * D:(h + 1) * D, 3, j * P:(j + 1) * P], nvt[:, j * P + h * D:j * P + (h + 1) * D],
                                   gm[:, h, j * P:(j + 1) * P], start=True, stop=True)
            mm.then_inc(attended, 1)
            n_a.tensor_centre(pe, asum[:, :], a_kept, g)
            n_a.tensor_average(pe, g)
            pe.wait_ge(n_a.normed, g + 1)
            for h in range(2):
                for c in range(2):
                    mm = pe.matmul(big[:, 2 * h + c, :], dy[:, h, c * P:(c + 1) * P], an[:, :], start=True, stop=True)
            mm.then_inc(y_made, 1)
            pe.wait_ge(gated, g + 1)
            for n in range(4):
                mm = pe.matmul(sums[:, 0, :], et[:, n // 2, n % 2, :], y[:, n, :], start=n == 0, stop=n == 3)
            mm.then_inc(v_made, 1)
            n_s.tensor_centre(pe, vs[:, :], vs_kept, g)
            n_s.tensor_average(pe, g)
            n_o.tensor_centre(pe, hsum[:, :], added, g)
            n_o.tensor_average(pe, g)

    @block.scalar
    def _(act):
        with act.Fori(0, G) as g:
            act.wait_ge(u_made, g + 1)
            act.activation(u[:, :, :], big[:, :, :], ACT.Relu).then_inc(u_kept, 1)
            n_v.scalar(act, g)
            act.wait_ge(v_turned, g + 1)
            act.activation(nvt[:, :], big[:, 2, :], ACT.Copy).then_inc(v_kept, 1)
            act.wait_ge(attended, g + 1)
            act.activation(asum[:, :], big[:, 3, :], ACT.Copy).then_inc(a_kept, 1)
            n_a.scalar(act, g)
            act.wait_ge(v_made, g + 1)
            act.activation(vs[:, :], sums[:, 0, :], ACT.Copy).then_inc(vs_kept, 1)
            n_s.scalar(act, g)
            n_o.scalar(act, g)

    @block.vector
    def _(v):
        v.wait_ge(weights_in, 80)
        with v.Fori(0, G) as g:
            v.tensor_copy(xg[:, :], group(X, g)).then_inc(grouped, 1)
            n_v.vector(v, nv[:, :], g)
            v.wait_ge(u_summed, g + 1)
            v.tensor_tensor_scan(run[:, :], later[:, :], flat_sums, 0.0, ALU.mult, ALU.max).then_inc(ran, 1)
            v.wait_ge(ran, g + 1)
            v.tensor_scalar(run[:, :], run[:, :], BIG, 1.0, ALU.mult, ALU.min).then_inc(capped, 1)
            v.wait_ge(capped, g + 1)
            v.tensor_copy(steps(q)[:, :, 0], steps(run)[:, :, 0]).then_inc(q_first, 1)
            v.scalar_tensor_tensor(steps(q)[:, :, 1:T], steps(run)[:, :, 0:T - 1], A * BIG, steps(run)[:, :, 1:T],
                                   ALU.mult, ALU.add).then_inc(q_raw, 1)
            v.wait_ge(q_first, g + 1)
            v.wait_ge(q_raw, g + 1)
            v.tensor_scalar(q[:, :], q[:, :], 1.0, None, ALU.min).then_inc(q_made, 1)
            v.wait_ge(q_made, g + 1)
            v.tensor_copy(steps(sig)[:, :, 0], steps(run)[:, :, 0]).then_inc(s_first, 1)
            v.scalar_tensor_tensor(steps(sig)[:, :, 1:T], steps(q)[:, :, 0:T - 1], A * BIG, steps(run)[:, :, 1:T],
                                   ALU.mult, ALU.add).then_inc(s_raw, 1)
            v.wait_ge(s_first, g + 1)
            v.wait_ge(s_raw, g + 1)
            v.tensor_scalar(sig[:, :], sig[:, :], 1.0, None, ALU.min).then_inc(sig_made, 1)
            v.wait_ge(sig_made, g + 1)
            sb3 = flat_sums.rearrange("p (b t) -> p b t", t=T)
            v.tensor_copy(steps(r)[:, :, 0], sb3[:, :, 0]).then_inc(raw_first, 1)
            v.scalar_tensor_tensor(steps(r)[:, :, 1:T], steps(sig)[:, :, 0:T - 1], A, sb3[:, :, 1:T],
                                   ALU.mult, ALU.add).then_inc(raw, 1)
            v.wait_ge(raw_first, g + 1)
            v.wait_ge(raw, g + 1)
            v.tensor_scalar(r[:, :], r[:, :], 1.0 / BIG, None, ALU.max).then_inc(guarded, 1)
            v.wait_ge(guarded, g + 1)
            v.reciprocal(r[:, :], r[:, :]).then_inc(inverted, 1)
            v.wait_ge(inverted, g + 1)
            v.scalar_tensor_tensor(keep[:, :], r[:, :], A, later[:, :], ALU.mult, ALU.mult).then_inc(kept, 1)
            for n in range(4):
                rh = r[:, (n // 2) * GC:(n // 2 + 1) * GC]
                v.tensor_tensor(ur[:, n, :], u[:, n, :], rh, ALU.mult).then_inc(scaled, 1)
            v.wait_ge(kept, g + 1)
            for n in range(4):
                v.wait_ge(scaled, 4 * g + n + 1)
                v.tensor_tensor_scan(xs[:, n, :], keep[:, (n // 2) * GC:(n // 2 + 1) * GC], ur[:, n, :], 0.0,
                                     ALU.mult, ALU.add).then_inc(scanned, 1)
            v.wait_ge(grams, g + 1)
            for h in range(2):
                ins = v.tensor_tensor(gm[:, h, :], big[:, h, :], decay[:, :], ALU.mult)
            ins.then_inc(masked, 1)
            n_a.vector(v, an[:, :], g)
            v.wait_ge(y_made, g + 1)
            v.scalar_tensor_tensor(y[:, :, :].rearrange("p n c -> p (n c)"), big[:, :, :].rearrange("p n c -> p (n c)"), 0.0,
                                   xs[:, :, :].rearrange("p n c -> p (n c)"), ALU.max, ALU.mult).then_inc(gated, 1)
            n_s.vector(v, vs[:, :], g)
            v.wait_ge(n_s.normed, g + 1)
            v.tensor_tensor(hsum[:, :], xg[:, :], vs[:, :], ALU.add).then_inc(added, 1)
            n_o.vector(v, group(X, g), g)

    st.end()


def finish(nc, con, X, out):
    st = Stage(nc, "out")
    rows = [st.sb(f"rows{k}", [P, TJ, P]) for k in range(G)]
    turn_ps = [st.ps(f"turn_ps{k}", [P, GC]) for k in range(G)]
    turned, kept = st.sems("turned kept")
    stored = [st.sem(f"stored{k}") for k in range(G)]
    ov = out.rearrange("(h k j p) d -> k h p j d", h=2, k=G, j=TJ, p=P)
    block = st.ctx.enter_context(nc.Block())

    @block.tensor
    def _(pe):
        for k in range(G):
            for j in range(TJ):
                c = k * GC + j * P
                mm = pe.transpose(turn_ps[k][:, j * P:(j + 1) * P], X[:, c:c + P], con["ident"])
            mm.then_inc(turned, 1)

    @block.vector
    def _(v):
        for k in range(G):
            v.wait_ge(turned, k + 1)
            v.tensor_copy(rows[k][:, :, :].rearrange("p j c -> p (j c)"), turn_ps[k][:, :]).then_inc(kept, 1)

    @block.sync
    def _(sp):
        for k in range(G):
            sp.wait_ge(kept, k + 1)
            for h in range(2):
                sp.dma_start(ov[k][h], rows[k][:, :, h * D:(h + 1) * D]).then_inc(stored[k], 16)
        for k in range(G):
            sp.wait_ge(stored[k], 32)

    st.end()

def experts(nc, con, X, a, name, E, HC, act_fn, scored=None, prenorm=False, background=None):
    st = Stage(nc, name)
    TH = TJ * 2
    N = E * 2 * HC
    w1 = st.sb("w1", [P, 2, E, HC * P])
    w2 = st.sb("w2", [P, E, HC, 2, P])
    b1 = st.sb("b1", [P, E, HC])
    b2 = st.sb("b2", [2 * E, P])
    sel = st.sb("sel", [2 * E, E, P])
    index = st.sb("index", [P, TH, E])
    loads = [(w1[:, :, :, :], "w1"), (w2[:, :, :, :, :], "w2"), (b1[:, :, :], "b1"), (b2[:, :], "b2"),
             (sel[:, :, :], "sel"), (index[:, :, :], "index")]
    if scored is None:
        wr = st.sb("wr", [P, 2 * E])
        br = st.sb("br", [P, 2, TH, E])
        loads += [(wr[:, :], "wr"), (br[:, :, :, :], "br")]
    if prenorm:
        scale, shift = st.sb("scale", [P, E]), st.sb("shift", [P, E])
        loads += [(scale[:, :], "scale"), (shift[:, :], "shift")]
    xg, sq, std, acc = [st.sb(n, [P, GC]) for n in ("xg", "sq", "std", "acc")]
    xn = st.sb("xn", [P, GC])
    xe = [st.sb(f"xe{k}", [P, GC]) for k in range(2)]
    hid = [st.sb(f"hid{k}", [P, GC]) for k in range(3)]
    spread = [st.sb(f"spread{k}", [P, GC]) for k in range(2)]
    part = [st.sb(f"part{k}", [P, GC]) for k in range(2)]
    lo, eq, low, m1, m2, gate = [st.sb(n, [P, TH, E]) for n in ("lo", "eq", "low", "m1", "m2", "gate")]
    top1, top2, first, e2, den, wgt1, wgt2 = [st.sb(n, [P, TH]) for n in ("top1", "top2", "first", "e2", "den", "wgt1", "wgt2")]
    gt = st.sb("gt", [2 * E, GC])
    misc = st.ps("misc", [P, GC])
    hid_ps = [st.ps(f"hid_ps{k}", [P, GC]) for k in range(3)]
    spread_ps = [st.ps(f"spread_ps{k}", [P, GC]) for k in range(2)]
    out_ps = [st.ps(f"out_ps{k}", [P, GC]) for k in range(2)]
    weights_in, grouped, scored_ps, biased1, biased2 = st.sems("weights_in grouped scored_ps biased1 biased2")
    best1, is1, cand1, first1, mark1, masked, best2, is2, cand2, first2, mark2, diff, exped = st.sems(
        "best1 is1 cand1 first1 mark1 masked best2 is2 cand2 first2 mark2 diff exped")
    summed, weight1, weight2, half_gate, gate2, gated, turned, turned_kept, bias_out, bias_kept = st.sems(
        "summed weight1 weight2 half_gate gate2 gated turned turned_kept bias_out bias_kept")
    hidden, activated, spread_made, spread_kept, out_made, weighed, accumulated, added, tuned = st.sems(
        "hidden activated spread_made spread_kept out_made weighed accumulated added tuned")
    n_i = Norm(st, "ni", con, hid_ps[0][:, :], hid_ps[1][:, :], sq[:, :], std[:, :]) if prenorm else None
    n_o = Norm(st, "no", con, hid_ps[0][:, :], hid_ps[1][:, :], sq[:, :], std[:, :])
    bc = lambda t: t[:, :, None].to_broadcast((P, TH, E))
    block = st.ctx.enter_context(nc.Block())

    @block.sync
    def _(sp):
        for dst, src in loads:
            sp.dma_start(dst, a[f"{name}_{src}" if src not in ("sel", "index") else f"{src}{E}"]).then_inc(weights_in, 16)
        if background is not None:
            background(sp)

    @block.tensor
    def _(pe):
        pe.wait_ge(weights_in, 16 * len(loads))
        with pe.Fori(0, G) as g:
            pe.wait_ge(grouped, g + 1)
            if scored is None:
                for j in range(TJ):
                    mm = pe.matmul(misc[:, j * 2 * E:(j + 1) * 2 * E], xg[:, j * P:(j + 1) * P], wr[:, :], start=True, stop=True)
                mm.then_inc(scored_ps, 1)
            if prenorm:
                n_i.tensor_centre(pe, xg[:, :], grouped, g)
                n_i.tensor_average(pe, g)

            def hidden_of(n):
                e, h, c = n // (2 * HC), n // HC % 2, n % HC
                if prenorm:
                    pe.wait_ge(tuned, g * E + e + 1)
                src = xe[e % 2] if prenorm else xg
                pe.matmul(hid_ps[n % 3][:, :], w1[:, h, e, c * P:(c + 1) * P], src[:, :], start=True, stop=True).then_inc(hidden, 1)

            def output_of(n):
                e, h, c = n // (2 * HC), n // HC % 2, n % HC
                if n % (2 * HC) == 0 and e >= 2:
                    pe.wait_ge(weighed, g * E + e - 1)
                pe.wait_ge(activated, g * N + n + 1)
                mm = pe.matmul(out_ps[e % 2][:, :], w2[:, e, c, h, :], hid[n % 3][:, :],
                               start=n % (2 * HC) == 0, stop=n % (2 * HC) == 2 * HC - 1)
                if n % (2 * HC) == 2 * HC - 1:
                    mm.then_inc(out_made, 1)

            def spread_of(e):
                if e >= 2:
                    pe.wait_ge(spread_kept, g * E + e - 1)
                pe.matmul(spread_ps[e % 2][:, :], sel[:, e, :], gt[:, :], start=True, stop=True).then_inc(spread_made, 1)

            hidden_of(0)
            hidden_of(1)
            pe.wait_ge(gated, g + 1)
            for j in range(TJ):
                mm = pe.transpose(misc[0:2 * E, j * P:(j + 1) * P], gate[:, 2 * j:2 * j + 2, :].rearrange("p h e -> p (h e)"), con["ident"])
            mm.then_inc(turned, 1)
            pe.wait_ge(turned_kept, g + 1)
            pe.matmul(misc[:, :], b2[:, :], gt[:, :], start=True, stop=True).then_inc(bias_out, 1)
            for n in range(N):
                if n % (2 * HC) == 0:
                    spread_of(n // (2 * HC))
                output_of(n)
                if n + 2 < N:
                    hidden_of(n + 2)
            n_o.tensor_centre(pe, acc[:, :], added, g)
            n_o.tensor_average(pe, g)

    @block.scalar
    def _(act):
        act.wait_ge(weights_in, 16 * len(loads))
        with act.Fori(0, G) as g:
            if prenorm:
                n_i.scalar(act, g)
            act.wait_ge(diff, g + 1)
            act.activation(e2[:, :], top2[:, :], ACT.Exp).then_inc(exped, 1)
            for n in range(N):
                if n % (2 * HC) == 0:
                    e = n // (2 * HC)
                    act.wait_ge(spread_made, g * E + e + 1)
                    if e >= 2:
                        act.wait_ge(weighed, g * E + e - 1)
                    act.activation(spread[e % 2][:, :], spread_ps[e % 2][:, :], ACT.Copy).then_inc(spread_kept, 1)
                act.wait_ge(hidden, g * N + n + 1)
                act.activation(hid[n % 3][:, :], hid_ps[n % 3][:, :], act_fn,
                               bias=b1[:, n // (2 * HC), n % HC:n % HC + 1]).then_inc(activated, 1)
            n_o.scalar(act, g)

    @block.vector
    def _(v):
        v.wait_ge(weights_in, 16 * len(loads))
        with v.Fori(0, G) as g:
            v.tensor_copy(xg[:, :], group(X, g)).then_inc(grouped, 1)
            if prenorm:
                n_i.vector(v, xn[:, :], g)

            def tune(e):
                v.tensor_scalar(xe[e % 2][:, :], xn[:, :], scale[:, e:e + 1], shift[:, e:e + 1], ALU.mult, ALU.add).then_inc(tuned, 1)

            if prenorm:
                v.wait_ge(n_i.normed, g + 1)
                tune(0)
                tune(1)
            if scored is None:
                v.wait_ge(scored_ps, g + 1)
                lg = misc[:, 0:TH * E].rearrange("p (t e) -> p t e", e=E)
                v.tensor_tensor(lo[:, :, :], lg, br[:, 0, :, :], ALU.add).then_inc(biased1, 1)
                v.wait_ge(biased1, g + 1)
                v.tensor_tensor(lo[:, :, :], lo[:, :, :], br[:, 1, :, :], ALU.add).then_inc(biased2, 1)
            else:
                v.tensor_copy(lo[:, :, :].rearrange("p t e -> p (t e)"), scored[:, bass.ds(g * TH * E, TH * E)]).then_inc(biased2, 1)
            v.wait_ge(biased2, g + 1)
            v.tensor_reduce(top1[:, :], lo[:, :, :], AX, ALU.max).then_inc(best1, 1)
            v.wait_ge(best1, g + 1)
            v.tensor_tensor(eq[:, :, :], lo[:, :, :], bc(top1), ALU.is_equal).then_inc(is1, 1)
            v.wait_ge(is1, g + 1)
            v.scalar_tensor_tensor(low[:, :, :], eq[:, :, :], -float(E), index[:, :, :], ALU.mult, ALU.add).then_inc(cand1, 1)
            v.wait_ge(cand1, g + 1)
            v.tensor_reduce(first[:, :], low[:, :, :], AX, ALU.min).then_inc(first1, 1)
            v.wait_ge(first1, g + 1)
            v.tensor_tensor(m1[:, :, :], low[:, :, :], bc(first), ALU.is_equal).then_inc(mark1, 1)
            v.wait_ge(mark1, g + 1)
            v.scalar_tensor_tensor(lo[:, :, :], m1[:, :, :], -3.0e38, lo[:, :, :], ALU.mult, ALU.add).then_inc(masked, 1)
            v.wait_ge(masked, g + 1)
            v.tensor_reduce(top2[:, :], lo[:, :, :], AX, ALU.max).then_inc(best2, 1)
            v.wait_ge(best2, g + 1)
            v.tensor_tensor(eq[:, :, :], lo[:, :, :], bc(top2), ALU.is_equal).then_inc(is2, 1)
            v.wait_ge(is2, g + 1)
            v.scalar_tensor_tensor(low[:, :, :], eq[:, :, :], -float(E), index[:, :, :], ALU.mult, ALU.add).then_inc(cand2, 1)
            v.tensor_tensor(top2[:, :], top2[:, :], top1[:, :], ALU.subtract).then_inc(diff, 1)
            v.wait_ge(cand2, g + 1)
            v.tensor_reduce(first[:, :], low[:, :, :], AX, ALU.min).then_inc(first2, 1)
            v.wait_ge(first2, g + 1)
            v.tensor_tensor(m2[:, :, :], low[:, :, :], bc(first), ALU.is_equal).then_inc(mark2, 1)
            v.wait_ge(exped, g + 1)
            v.tensor_scalar(den[:, :], e2[:, :], 1.0, None, ALU.add).then_inc(summed, 1)
            v.wait_ge(summed, g + 1)
            v.reciprocal(wgt1[:, :], den[:, :]).then_inc(weight1, 1)
            v.wait_ge(weight1, g + 1)
            v.tensor_tensor(wgt2[:, :], e2[:, :], wgt1[:, :], ALU.mult).then_inc(weight2, 1)
            v.tensor_tensor(gate[:, :, :], m1[:, :, :], bc(wgt1), ALU.mult).then_inc(half_gate, 1)
            v.wait_ge(weight2, g + 1)
            v.wait_ge(mark2, g + 1)
            v.tensor_tensor(m2[:, :, :], m2[:, :, :], bc(wgt2), ALU.mult).then_inc(gate2, 1)
            v.wait_ge(half_gate, g + 1)
            v.wait_ge(gate2, g + 1)
            v.tensor_tensor(gate[:, :, :], gate[:, :, :], m2[:, :, :], ALU.add).then_inc(gated, 1)
            v.wait_ge(turned, g + 1)
            v.tensor_copy(gt[:, :], misc[0:2 * E, :]).then_inc(turned_kept, 1)
            v.wait_ge(bias_out, g + 1)
            v.tensor_tensor(acc[:, :], misc[:, :], xg[:, :], ALU.add).then_inc(bias_kept, 1)
            v.wait_ge(bias_kept, g + 1)
            for e in range(E):
                v.wait_ge(out_made, g * E + e + 1)
                v.wait_ge(spread_kept, g * E + e + 1)
                v.tensor_tensor(part[e % 2][:, :], out_ps[e % 2][:, :], spread[e % 2][:, :], ALU.mult).then_inc(weighed, 1)
                if prenorm and e + 2 < E:
                    tune(e + 2)
                v.wait_ge(weighed, g * E + e + 1)
                if e:
                    v.wait_ge(accumulated, g * (E - 1) + e)
                ins = v.tensor_tensor(acc[:, :], acc[:, :], part[e % 2][:, :], ALU.add)
                ins.then_inc(accumulated if e < E - 1 else added, 1)
            n_o.vector(v, group(X, g), g)

    st.end()


def first_experts(nc, con, X, a):
    experts(nc, con, X, a, "ffn0", 8, 2, ACT.Gelu, prenorm=True)


def third_experts(nc, con, X, a):
    experts(nc, con, X, a, "ffn2", 8, 1, ACT.Relu)


def second_attention(nc, con, X, a):
    st = Stage(nc, "att1")
    wq, wkv, wm = st.sb("wq", [P, P]), st.sb("wkv", [P, 2 * P]), st.sb("wm", [P, P])
    w1x, w1m, w2 = st.sb("w1x", [P, 2, P]), st.sb("w1m", [P, 2, P]), st.sb("w2", [P, 2, P])
    gb = st.sb("gb", [P, 4])
    heads = st.sb("heads", [P, GB, D])
    xg, sq, std, qn, qe, qs = [st.sb(n, [P, GC]) for n in ("xg", "sq", "std", "qn", "qe", "qs")]
    kn, ke, ks = [st.sb(n, [P, TJ, 2, D]) for n in ("kn", "ke", "ks")]
    vo = st.sb("vo", [P, TJ, 2, 2 * D])
    num_w, den_w = st.sb("num_w", [P, GB, P]), st.sb("den_w", [P, GB, P])
    den, msg, merged, m1, relu, mlp, m2, hs = [st.sb(n, [P, 2, GC] if n == "relu" else [P, GC]) for n in
                                               ("den", "msg", "merged", "m1", "relu", "mlp", "m2", "hs")]
    q_ps, cp = st.ps("q_ps", [P, GC]), st.ps("cp", [P, GC])
    wide_ps = st.ps("wide_ps", [P, 4 * GC])
    kv_ps = wide_ps[:, 0:2 * GC].rearrange("p (a j w h d) -> p a j w h d", a=2, j=TJ // 2, w=2, h=2)
    sum_ps = wide_ps[:, :].rearrange("p (b j h d) -> p b j h d", b=2, j=TJ, h=2)
    num_ps, den_ps = st.ps("num_ps", [P, GC]), st.ps("den_ps", [P, GC])
    weights_in, ones_set, zero1, zero2, grouped, q_made, kv_made, q_low, q_exp, q_kept = st.sems(
        "weights_in ones_set zero1 zero2 grouped q_made kv_made q_low q_exp q_kept")
    k_low, k_exp, k_kept, v_kept, summed, num_kept, den_kept, num_made, den_made = st.sems(
        "k_low k_exp k_kept v_kept summed num_kept den_kept num_made den_made")
    guarded, inverted, scaled, messaged, merged_made, merged_kept, tuned1, mlp1, relued, mlp2, mlp_kept, tuned2, added, added2 = st.sems(
        "guarded inverted scaled messaged merged_made merged_kept tuned1 mlp1 relued mlp2 mlp_kept tuned2 added added2")
    n_1 = Norm(st, "n1", con, cp[:, :], q_ps[:, :], sq[:, :], std[:, :])
    n_2 = Norm(st, "n2", con, cp[:, :], q_ps[:, :], sq[:, :], std[:, :])
    n_o = Norm(st, "no", con, cp[:, :], q_ps[:, :], sq[:, :], std[:, :])
    loads = [(wq[:, :], "wq"), (wkv[:, :], "wkv"), (wm[:, :], "wm"), (w1x[:, :, :], "w1x"), (w1m[:, :, :], "w1m"),
             (w2[:, :, :], "w2"), (gb[:, :], "gb"), (heads[:, :, :], "heads")]
    block = st.ctx.enter_context(nc.Block())

    @block.sync
    def _(sp):
        for dst, src in loads:
            sp.dma_start(dst, a[f"att1_{src}"]).then_inc(weights_in, 16)

    @block.gpsimd
    def _(pool):
        pool.memset(vo[:, :, :, D:2 * D], 1.0).then_inc(ones_set, 1)
        pool.memset(num_w[:, :, :], 0.0).then_inc(zero1, 1)
        pool.memset(den_w[:, :, :], 0.0).then_inc(zero2, 1)

    @block.tensor
    def _(pe):
        pe.wait_ge(weights_in, 16 * len(loads))
        pe.wait_ge(ones_set, 1)
        with pe.Fori(0, G) as g:
            pe.wait_ge(grouped, g + 1)
            pe.matmul(q_ps[:, :], wq[:, :], xg[:, :], start=True, stop=True).then_inc(q_made, 1)
            for j in range(TJ):
                mm = pe.matmul(kv_ps[:, j // 2, j % 2, :, :, :].rearrange("p w h d -> p (w h d)"), xg[:, j * P:(j + 1) * P],
                               wkv[:, :], start=True, stop=True)
            mm.then_inc(kv_made, 1)
            pe.wait_ge(k_kept, g + 1)
            pe.wait_ge(v_kept, g + 1)
            for j in range(TJ):
                for b in range(2):
                    r = slice(b * D, (b + 1) * D)
                    mm = pe.matmul(sum_ps[:, b, j, :, :].rearrange("p h d -> p (h d)"), ks[r, j, :, :].rearrange("p h d -> p (h d)"),
                                   vo[r, j, :, :].rearrange("p h d -> p (h d)"), start=True, stop=True)
            mm.then_inc(summed, 1)
            pe.wait_ge(q_kept, g + 1)
            pe.wait_ge(num_kept, 2 * g + 2)
            for b in range(GB):
                mm = pe.matmul(num_ps[:, b * D:(b + 1) * D], num_w[:, b, :], qs[:, b * D:(b + 1) * D], start=True, stop=True)
            mm.then_inc(num_made, 1)
            pe.wait_ge(den_kept, 2 * g + 2)
            for b in range(GB):
                mm = pe.matmul(den_ps[:, b * D:(b + 1) * D], den_w[:, b, :], qs[:, b * D:(b + 1) * D], start=True, stop=True)
            mm.then_inc(den_made, 1)
            pe.wait_ge(messaged, g + 1)
            pe.matmul(q_ps[:, :], wm[:, :], msg[:, :], start=True, stop=True).then_inc(merged_made, 1)
            n_1.tensor_centre(pe, merged[:, :], merged_kept, g)
            n_1.tensor_average(pe, g)
            pe.wait_ge(tuned1, g + 1)
            for h in range(2):
                out = (num_ps, den_ps)[h][:, :]
                pe.matmul(out, w1x[:, h, :], xg[:, :], start=True, stop=False)
                mm = pe.matmul(out, w1m[:, h, :], m1[:, :], start=False, stop=True)
            mm.then_inc(mlp1, 1)
            pe.wait_ge(relued, 2 * g + 2)
            pe.matmul(q_ps[:, :], w2[:, 0, :], relu[:, 0, :], start=True, stop=False)
            pe.matmul(q_ps[:, :], w2[:, 1, :], relu[:, 1, :], start=False, stop=True).then_inc(mlp2, 1)
            n_2.tensor_centre(pe, mlp[:, :], mlp_kept, g)
            n_2.tensor_average(pe, g)
            n_o.tensor_centre(pe, hs[:, :], added2, g)
            n_o.tensor_average(pe, g)

    @block.scalar
    def _(act):
        with act.Fori(0, G) as g:
            act.wait_ge(k_low, g + 1)
            act.activation(ke[:, :, :, :], kn[:, :, :, :], ACT.Exp).then_inc(k_exp, 1)
            act.wait_ge(q_low, g + 1)
            act.activation(qe[:, :], qn[:, :], ACT.Exp).then_inc(q_exp, 1)
            act.wait_ge(k_kept, g + 1)
            for half in range(2):
                ins = act.activation(vo[:, 2 * half:2 * half + 2, :, 0:D], kv_ps[:, half, :, 1, :, :], ACT.Copy, scale=1.0 / T)
            ins.then_inc(v_kept, 1)
            act.wait_ge(merged_made, g + 1)
            act.activation(merged[:, :], q_ps[:, :], ACT.Copy).then_inc(merged_kept, 1)
            n_1.scalar(act, g)
            act.wait_ge(mlp1, g + 1)
            for h in range(2):
                act.activation(relu[:, h, :], (num_ps, den_ps)[h][:, :], ACT.Relu).then_inc(relued, 1)
            act.wait_ge(mlp2, g + 1)
            act.activation(mlp[:, :], q_ps[:, :], ACT.Copy).then_inc(mlp_kept, 1)
            n_2.scalar(act, g)
            n_o.scalar(act, g)

    @block.vector
    def _(v):
        v.wait_ge(weights_in, 16 * len(loads))
        v.wait_ge(zero1, 1)
        v.wait_ge(zero2, 1)
        with v.Fori(0, G) as g:
            v.tensor_copy(xg[:, :], group(X, g)).then_inc(grouped, 1)
            v.wait_ge(kv_made, g + 1)
            for half in range(2):
                ins = v.tensor_scalar(kn[:, 2 * half:2 * half + 2, :, :], kv_ps[:, half, :, 0, :, :], 0.0, None, ALU.min)
            ins.then_inc(k_low, 1)
            v.tensor_scalar(qn[:, :], q_ps[:, :], 0.0, None, ALU.min).then_inc(q_low, 1)
            v.wait_ge(k_exp, g + 1)
            for half in range(2):
                flat = lambda t: t[:, 2 * half:2 * half + 2, :, :].rearrange("p j h d -> p j (h d)")
                ins = v.scalar_tensor_tensor(flat(ks), kv_ps[:, half, :, 0, :, :].rearrange("p j h d -> p j (h d)"), 0.0,
                                             flat(ke), ALU.max, ALU.add)
            ins.then_inc(k_kept, 1)
            v.wait_ge(q_exp, g + 1)
            v.scalar_tensor_tensor(qs[:, :], q_ps[:, :], 0.0, qe[:, :], ALU.max, ALU.add).then_inc(q_kept, 1)
            v.wait_ge(summed, g + 1)
            for kept, w, o in ((num_kept, num_w, 0), (den_kept, den_w, D)):
                for h in range(2):
                    r = slice(h * D, (h + 1) * D)
                    for b in range(2):
                        ins = v.tensor_tensor(w[r, b::2, r], sum_ps[r, b, :, h, o:o + D], heads[r, 0:TJ, :], ALU.mult)
                    ins.then_inc(kept, 1)
            v.wait_ge(den_made, g + 1)
            v.tensor_scalar(den[:, :], den_ps[:, :], 1e-6, None, ALU.add).then_inc(guarded, 1)
            v.wait_ge(guarded, g + 1)
            v.reciprocal(den[:, :], den[:, :]).then_inc(inverted, 1)
            v.wait_ge(inverted, g + 1)
            v.scalar_tensor_tensor(msg[:, :], num_ps[:, :], float(T), den[:, :], ALU.mult, ALU.mult).then_inc(messaged, 1)
            n_1.vector(v, m1[:, :], g)
            v.wait_ge(n_1.normed, g + 1)
            v.tensor_scalar(m1[:, :], m1[:, :], gb[:, 0:1], gb[:, 1:2], ALU.mult, ALU.add).then_inc(tuned1, 1)
            n_2.vector(v, m2[:, :], g)
            v.wait_ge(n_2.normed, g + 1)
            v.tensor_scalar(m2[:, :], m2[:, :], gb[:, 2:3], gb[:, 3:4], ALU.mult, ALU.add).then_inc(tuned2, 1)
            v.wait_ge(tuned2, g + 1)
            v.tensor_tensor(m2[:, :], xg[:, :], m2[:, :], ALU.add).then_inc(added, 1)
            v.wait_ge(added, g + 1)
            v.tensor_tensor(hs[:, :], xg[:, :], m2[:, :], ALU.add).then_inc(added2, 1)
            n_o.vector(v, group(X, g), g)

    st.end()



LAYERS = 2
ROUTED = LAYERS * P + LAYERS


def fetch_experts(sp, routed, route, experts, routed_in):
    with sp.Fori(0, B) as b:
        e = sp.value_load(route[0:1, bass.ds(b, 1)], min_val=0, max_val=15)
        sp.dma_start(routed[:, bass.ds(b * ROUTED, ROUTED)], experts[:, bass.ds(e * ROUTED, ROUTED)]).then_inc(routed_in, 16)


def routed_mlp(nc, con, X, a):
    st = Stage(nc, "ffn1")
    NB = 2 * GB
    RING = 4
    wi, wo = st.sb("wi", [P, 2, P]), st.sb("wo", [P, 2, P])
    bi, bo, bs = st.sb("bi", [P, 1]), st.sb("bo", [P, 1]), st.sb("bs", [P, LAYERS])
    ws = st.sb("ws", [P, LAYERS, P])
    route = st.sb("route", [1, B], I32)
    routed = st.sb("routed", [P, B * ROUTED])
    own = [st.sb(f"own{k}", [P, P]) for k in range(RING)]
    xg, sq, std, hs = [st.sb(n, [P, GC]) for n in ("xg", "sq", "std", "hs")]
    hid = [st.sb(f"hid{k}", [P, 2, GC]) for k in range(LAYERS + 1)]
    pre = st.sb("pre", [P, 2, GC])
    hid_ps = [st.ps(f"hid_ps{h}", [P, GC]) for h in range(2)]
    out_ps, cp, vp = st.ps("out_ps", [P, GC]), st.ps("cp", [P, GC]), st.ps("vp", [P, GC])
    weights_in, route_in, routed_in, grouped, entered, copied = st.sems("weights_in route_in routed_in grouped entered copied")
    used, residual, biased, layered, left, added = st.sems("used residual biased layered left added")
    n_o = Norm(st, "no", con, cp[:, :], vp[:, :], sq[:, :], std[:, :])
    loads = [(wi[:, :, :], "wi"), (wo[:, :, :], "wo"), (bi[:, :], "bi"), (bo[:, :], "bo"), (bs[:, :], "bs"), (ws[:, :, :], "ws")]
    block = st.ctx.enter_context(nc.Block())

    @block.sync
    def _(sp):
        sp.dma_start(route[:, :], a["route"]).then_inc(route_in, 16)
        for dst, src in loads:
            sp.dma_start(dst, a[f"ffn1_{src}"]).then_inc(weights_in, 16)
        sp.wait_ge(route_in, 16)
        fetch_experts(sp, routed, route, a["ffn1_experts"], routed_in)

    @block.tensor
    def _(pe):
        pe.wait_ge(weights_in, 16 * len(loads))
        with pe.Fori(0, G) as g:
            pe.wait_ge(grouped, g + 1)
            for h in range(2):
                mm = pe.matmul(hid_ps[h][:, :], wi[:, h, :], xg[:, :], start=True, stop=True)
            mm.then_inc(entered, 1)
            for l in range(LAYERS):
                pe.wait_ge(layered, g * 2 * (LAYERS + 1) + 2 * l + 2)
                for h in range(2):
                    pe.matmul(hid_ps[h][:, :], ws[:, l, :], hid[l][:, h, :], start=True, stop=False)
                for n in range(NB):
                    h, b = n // GB, n % GB
                    m = l * NB + n
                    pe.wait_ge(copied, g * LAYERS * NB + m + 1)
                    cols = slice(b * T, (b + 1) * T)
                    pe.matmul(hid_ps[h][:, cols], own[m % RING][:, :], hid[l][:, h, cols], start=False,
                              stop=b == GB - 1).then_inc(used, 1)
            pe.wait_ge(layered, (g + 1) * 2 * (LAYERS + 1))
            for h in range(2):
                mm = pe.matmul(out_ps[:, :], wo[:, h, :], hid[LAYERS][:, h, :], start=h == 0, stop=h == 1)
            mm.then_inc(left, 1)
            n_o.tensor_centre(pe, hs[:, :], added, g)
            n_o.tensor_average(pe, g)

    @block.scalar
    def _(act):
        act.wait_ge(weights_in, 16 * len(loads))
        act.wait_ge(routed_in, 16 * B)
        with act.Fori(0, G) as g:
            def copy(m):
                l, h, b = m // NB, m % NB // GB, m % GB
                if m >= RING:
                    act.wait_ge(used, g * LAYERS * NB + m - RING + 1)
                src = routed[:, bass.ds(((h * G * GB + b) * ROUTED + l * P) + g * (GB * ROUTED), P)]
                act.activation(own[m % RING][:, :], src, ACT.Copy).then_inc(copied, 1)

            act.wait_ge(entered, g + 1)
            for h in range(2):
                act.activation(hid[0][:, h, :], hid_ps[h][:, :], ACT.Relu, bias=bi[:, 0:1]).then_inc(layered, 1)
            for l in range(LAYERS):
                for n in range(NB):
                    copy(l * NB + n)
                for h in range(2):
                    act.wait_ge(biased, g * 2 * LAYERS + 2 * l + h + 1)
                    act.activation(hid[l + 1][:, h, :], pre[:, h, :], ACT.Relu, bias=bs[:, l:l + 1]).then_inc(layered, 1)
            n_o.scalar(act, g)

    @block.vector
    def _(v):
        v.wait_ge(weights_in, 16 * len(loads))
        v.wait_ge(routed_in, 16 * B)
        with v.Fori(0, G) as g:
            v.tensor_copy(xg[:, :], group(X, g)).then_inc(grouped, 1)
            for l in range(LAYERS):
                for h in range(2):
                    k = g * 2 * LAYERS + 2 * l + h + 1
                    v.wait_ge(used, g * LAYERS * NB + (l * 2 + h + 1) * GB)
                    v.tensor_tensor(pre[:, h, :], hid_ps[h][:, :], hid[l][:, h, :], ALU.add).then_inc(residual, 1)
                    v.wait_ge(residual, k)
                    own_bias = routed[:, bass.ds((h * G * GB * ROUTED) + g * (GB * ROUTED), GB * ROUTED)].rearrange(
                        "p (b c) -> p b c", c=ROUTED)[:, :, LAYERS * P + l:LAYERS * P + l + 1].to_broadcast((P, GB, T))
                    p3 = pre[:, h, :].rearrange("p (b t) -> p b t", t=T)
                    v.tensor_tensor(p3, p3, own_bias, ALU.add).then_inc(biased, 1)
            v.wait_ge(left, g + 1)
            v.scalar_tensor_tensor(hs[:, :], out_ps[:, :], bo[:, 0:1], xg[:, :], ALU.add, ALU.add).then_inc(added, 1)
            n_o.vector(v, group(X, g), g)

    st.end()


def causal_convolution(v, out, x, taps, stepped, base=0):
    o3, x3 = (t[:, :].rearrange("p (b t) -> p b t", t=T) for t in (out, x))
    v.tensor_scalar(out[:, :], x[:, :], taps[:, 0:1], None, ALU.mult).then_inc(stepped, 1)
    for k in range(1, T):
        v.wait_ge(stepped, base + k)
        v.scalar_tensor_tensor(o3[:, :, k:T], x3[:, :, 0:T - k], taps[:, k:k + 1], o3[:, :, k:T],
                               ALU.mult, ALU.add).then_inc(stepped, 1)


def third_attention(nc, con, X, a):
    st = Stage(nc, "att2")
    taps, y = st.sb("taps", [P, T]), st.sb("y", [P, HALF])
    hs, sq, std = [st.sb(n, [P, GC]) for n in ("hs", "sq", "std")]
    cp, vp = st.ps("cp", [P, GC]), st.ps("vp", [P, GC])
    taps_in, stepped, added = st.sems("taps_in stepped added")
    n_o = Norm(st, "no", con, cp[:, :], vp[:, :], sq[:, :], std[:, :])
    block = st.ctx.enter_context(nc.Block())

    @block.sync
    def _(sp):
        sp.dma_start(taps[:, :], a["att2_c"]).then_inc(taps_in, 16)

    @block.tensor
    def _(pe):
        with pe.Fori(0, G) as g:
            n_o.tensor_centre(pe, hs[:, :], added, g)
            n_o.tensor_average(pe, g)

    @block.scalar
    def _(act):
        with act.Fori(0, G) as g:
            n_o.scalar(act, g)

    @block.vector
    def _(v):
        v.wait_ge(taps_in, 16)
        causal_convolution(v, y, X, taps, stepped)
        v.wait_ge(stepped, T)
        with v.Fori(0, G) as g:
            v.tensor_tensor(hs[:, :], group(X, g), group(y, g), ALU.add).then_inc(added, 1)
            n_o.vector(v, group(X, g), g)

    st.end()


def fourth_attention(nc, con, X, a):
    st = Stage(nc, "att3")
    DT = 1.0 / T
    wb, wc, wd = st.sb("wb", [P, P]), st.sb("wc", [P, P]), st.sb("wd", [P, P])
    par = st.sb("par", [P, 4])
    rx, rz = st.sb("rx", [P, T]), st.sb("rz", [P, T])
    tx, tz = st.sb("tx", [P, T // 2]), st.sb("tz", [P, T // 2])
    p_, q_, aq, t1, t2 = [st.sb(n, [P, 1]) for n in ("p_", "q_", "aq", "t1", "t2")]
    u, y = st.sb("u", [P, HALF]), st.sb("y", [P, HALF])
    gx, xg, xs, sg, hs, sq, std = [st.sb(n, [P, GC]) for n in ("gx", "xg", "xs", "sg", "hs", "sq", "std")]
    u_ps, o_ps, cp, vp = [st.ps(n, [P, GC]) for n in ("u_ps", "o_ps", "cp", "vp")]
    bcd = st.sb("bcd", [P, 1])
    weights_in, chained, u_made, u_kept, stepped, out_made, xg_kept, gelued, sigmoided = st.sems(
        "weights_in chained u_made u_kept stepped out_made xg_kept gelued sigmoided")
    gated, added, added2, conv_done = st.sems("gated added added2 conv_done")
    n_o = Norm(st, "no", con, cp[:, :], vp[:, :], sq[:, :], std[:, :])
    loads = [(wb[:, :], "wb"), (wc[:, :], "wc"), (wd[:, :], "wd"), (par[:, :], "par")]
    block = st.ctx.enter_context(nc.Block())

    @block.sync
    def _(sp):
        for dst, src in loads:
            sp.dma_start(dst, a[f"att3_{src}"]).then_inc(weights_in, 16)

    @block.tensor
    def _(pe):
        pe.wait_ge(weights_in, 16 * len(loads))
        for k in range(G):
            if k:
                pe.wait_ge(u_kept, k)
            pe.matmul(u_ps[:, :], wb[:, :], X[:, k * GC:(k + 1) * GC], start=True, stop=True).then_inc(u_made, 1)
        pe.wait_ge(conv_done, 1)
        with pe.Fori(0, G) as g:
            pe.matmul(o_ps[:, :], wc[:, :], group(y, g), start=True, stop=False)
            pe.matmul(o_ps[:, :], wd[:, :], group(X, g), start=False, stop=True).then_inc(out_made, 1)
            n_o.tensor_centre(pe, hs[:, :], added2, g)
            n_o.tensor_average(pe, g)

    @block.scalar
    def _(act):
        act.wait_ge(weights_in, 16 * len(loads))
        for k in range(G):
            act.wait_ge(u_made, k + 1)
            act.activation(u[:, k * GC:(k + 1) * GC], u_ps[:, :], ACT.Identity, bias=par[:, 1:2]).then_inc(u_kept, 1)
        act.wait_ge(conv_done, 1)
        with act.Fori(0, G) as g:
            act.wait_ge(out_made, g + 1)
            act.activation(gx[:, :], o_ps[:, :], ACT.Gelu, bias=bcd[:, 0:1]).then_inc(gelued, 1)
            act.wait_ge(gelued, g + 1)
            act.activation(sg[:, :], gx[:, :], ACT.Sigmoid).then_inc(sigmoided, 1)
            n_o.scalar(act, g)

    @block.vector
    def _(v):
        v.wait_ge(weights_in, 16 * len(loads))
        count = 0

        def link(ins):
            nonlocal count
            count += 1
            ins.then_inc(chained, 1)
            v.wait_ge(chained, count)

        acol = par[:, 0:1]
        link(v.tensor_tensor(bcd[:, :], par[:, 2:3], par[:, 3:4], ALU.add))
        link(v.tensor_scalar(t1[:, :], acol, DT * DT, 1.0, ALU.mult, ALU.add))
        link(v.reciprocal(p_[:, :], t1[:, :]))
        link(v.tensor_scalar(q_[:, :], p_[:, :], DT, None, ALU.mult))
        link(v.tensor_copy(rx[:, 0:1], q_[:, :]))
        link(v.tensor_scalar(rz[:, 0:1], q_[:, :], DT, None, ALU.mult))
        m = 1
        while m < T:
            link(v.tensor_tensor(aq[:, :], acol, q_[:, :], ALU.mult))
            link(v.tensor_scalar(tx[:, 0:m], rz[:, 0:m], aq[:, 0:1], None, ALU.mult))
            link(v.tensor_scalar(tz[:, 0:m], rz[:, 0:m], p_[:, 0:1], None, ALU.mult))
            link(v.scalar_tensor_tensor(rz[:, m:2 * m], rx[:, 0:m], q_[:, 0:1], tz[:, 0:m], ALU.mult, ALU.add))
            link(v.scalar_tensor_tensor(rx[:, m:2 * m], rx[:, 0:m], p_[:, 0:1], tx[:, 0:m], ALU.mult, ALU.subtract))
            link(v.tensor_tensor(t1[:, :], aq[:, :], q_[:, :], ALU.mult))
            link(v.tensor_scalar(t2[:, :], p_[:, :], q_[:, 0:1], 2.0, ALU.mult, ALU.mult))
            link(v.scalar_tensor_tensor(p_[:, :], p_[:, :], p_[:, 0:1], t1[:, :], ALU.mult, ALU.subtract))
            link(v.tensor_copy(q_[:, :], t2[:, :]))
            m *= 2
        v.wait_ge(u_kept, G)
        causal_convolution(v, y, u, rz, stepped)
        v.wait_ge(stepped, T)
        v.nop().then_inc(conv_done, 1)
        with v.Fori(0, G) as g:
            v.wait_ge(sigmoided, g + 1)
            v.tensor_tensor(xs[:, :], gx[:, :], sg[:, :], ALU.mult).then_inc(gated, 1)
            v.wait_ge(gated, g + 1)
            v.tensor_tensor(xs[:, :], xs[:, :], group(X, g), ALU.add).then_inc(added, 1)
            v.wait_ge(added, g + 1)
            v.tensor_tensor(hs[:, :], xs[:, :], group(X, g), ALU.add).then_inc(added2, 1)
            n_o.vector(v, group(X, g), g)

    st.end()


EDGES = 262144
EW = EDGES // P
CH = 8
CHUNKS = EW // CH
STEPS = 4


def order_edges(nc, con, X, a):
    st = Stage(nc, "edges")
    src, dst = st.sb("src", [P, EW], I32), st.sb("dst", [P, EW], I32)
    key, inside = st.sb("key", [P, EW]), st.sb("inside", [P, EW])
    top, spare = st.sb("top", [P, CH]), st.sb("spare", [P, CH])
    count, most = st.sb("count", [P, 1]), st.sb("most", [P, 1])
    src_in, dst_in, cleared, capped, keyed, marked, zeroed, counted, maxed, most_kept = st.sems(
        "src_in dst_in cleared capped keyed marked zeroed counted maxed most_kept")
    topped, taken, stored = st.sems("topped taken stored")
    block = st.ctx.enter_context(nc.Block())

    @block.sync
    def _(sp):
        sp.dma_start(src[:, :], a["edge_src"]).then_inc(src_in, 16)
        sp.dma_start(dst[:, :], a["edge_dst"]).then_inc(dst_in, 16)

    @block.gpsimd
    def _(pool):
        pool.wait_ge(counted, 1)
        pool.partition_all_reduce(most[:, :], count[:, :], P, bass.bass_isa.ReduceOp.max).then_inc(maxed, 1)

    @block.vector
    def _(v):
        v.memset(con["keys"], 0.0).then_inc(cleared, 1)
        v.wait_ge(src_in, 16)
        v.tensor_scalar(inside[:, :], src[:, :], float(TOK - 1), 1.0, ALU.min, ALU.add).then_inc(capped, 1)
        v.wait_ge(capped, 1)
        v.wait_ge(dst_in, 16)
        v.scalar_tensor_tensor(key[:, :], dst[:, :], float(TOK), inside[:, :], ALU.mult, ALU.add).then_inc(keyed, 1)
        v.wait_ge(keyed, 1)
        v.tensor_scalar(inside[:, :], dst[:, :], float(TOK), None, ALU.is_lt).then_inc(marked, 1)
        v.wait_ge(marked, 1)
        v.tensor_tensor(key[:, :], key[:, :], inside[:, :], ALU.mult).then_inc(zeroed, 1)
        v.tensor_reduce(count[:, :], inside[:, :], AX, ALU.add).then_inc(counted, 1)
        v.wait_ge(maxed, 1)
        v.tensor_copy(con["most"], most[:, :]).then_inc(most_kept, 1)
        v.wait_ge(zeroed, 1)
        v.wait_ge(cleared, 1)
        v.wait_ge(most_kept, 1)
        n = v.value_load(con["most"][0:1, 0:1], min_val=0, max_val=EW)
        with v.Fori(0, CHUNKS // STEPS) as k:
            with v.If(n > k * (CH * STEPS)):
                for j in range(STEPS):
                    v.max(top[:, :], key[:, :]).then_inc(topped, 1)
                    v.wait_ge(topped, k * STEPS + j + 1)
                    v.tensor_copy(spare[:, :], top[:, :])
                    v.match_replace(key[:, :], top[:, :], key[:, :], 0.0).then_inc(taken, 1)
                    v.tensor_copy(con["keys"][:, bass.ds(k * (CH * STEPS) + j * CH, CH)], top[:, :]).then_inc(stored, 1)
                    v.wait_ge(taken, k * STEPS + j + 1)
                    v.wait_ge(stored, k * STEPS + j + 1)
                    v.memset(spare[:, 0:1], 0.0)

    st.end()


HEADS, GE = 4, 4
GF = HEADS * GE
NF = GF + HEADS
HI = TOK // P
AHEAD = 2
RUN = 16


def graph_attention(nc, con, X, a):
    st = Stage(nc, "gat")
    TILES = HALF // P
    BF16 = mybir.dt.bfloat16
    rows_dram = nc.dram_tensor("gat_rows", (TOK, NF), F32, kind="Internal").ap()
    wg = st.sb("wg", [P, 2 * GF])
    att = st.sb("att", [P, 2, HI, GF])
    norm_par = st.sb("norm_par", [P, 3, HI, GF])
    iota = st.sb("iota", [P, P])
    rowt = st.sb("rowt", [P, HI, NF])
    prod = st.sb("prod", [P, 2, HI, GF])
    ad, shift, selfw = [st.sb(n, [P, HI, HEADS]) for n in ("ad", "shift", "selfw")]
    amax1, amax = st.sb("amax1", [P, HEADS]), st.sb("amax", [P, HEADS])
    rest = st.sb("rest", [P, 2, HI, HEADS])
    adp = st.sb("adp", [P, 3, HI * HEADS], BF16)
    words = [st.sb(f"words{k}", [P, EW + CH * AHEAD], I32) for k in range(2)]
    srci = st.sb("srci", [P, EW + CH * AHEAD], U32)
    low, high = st.sb("low", [P, EW + CH * AHEAD]), st.sb("high", [P, EW + CH * AHEAD])
    index = [st.sb(f"index{k}", [P, CH], U32) for k in range(2)]
    rows = [st.sb(f"rows{k}", [P, CH, NF]) for k in range(2)]
    oh_low = [st.sb(f"oh_low{k}", [P, CH, P]) for k in range(2)]
    oh_high = [st.sb(f"oh_high{k}", [P, CH, HI]) for k in range(2)]
    turned_b = st.sb("turned_b", [P, CH * P], BF16)
    picked = st.sb("picked", [P, CH, HI, HEADS])
    ade, edge, bound = [st.sb(n, [P, CH, HEADS]) for n in ("ade", "edge", "bound")]
    value = st.sb("value", [P, CH, NF])
    spread = st.sb("spread", [P, CH, HI, NF])
    zeros, spare = st.sb("zeros", [P, GC]), st.sb("spare", [P, 2])
    std_t = st.sb("std", [P, HI])
    std = std_t[:, :]
    feat_ps = st.ps("feat_ps", [P, TILES, 2, GF])
    turn_ps = st.ps("turn_ps", [P, CH * P])
    gat_ps = st.ps("gat_ps", [P, CH, HI * HEADS])
    sum_ps = st.ps("sum_ps", [P, 2, GC])
    HB = HI // 2
    weights_in, chained, featured, tables, maxed, self_ready, self_done, rows_out, zero_set, started = st.sems(
        "weights_in chained featured tables maxed self_ready self_done rows_out zero_set started")
    staged, onehot, turned, turned_kept, target_out, target_read = st.sems(
        "staged onehot turned turned_kept target_out target_read")
    scored, weighted, valued, spreaded, scattered, prepared, picked1, reduced, step1, step2, step3, step4, all_done = st.sems(
        "scored weighted valued spreaded scattered prepared picked1 reduced step1 step2 step3 step4 all_done")
    rooted, rooted_in, carried = st.sems("rooted rooted_in carried")
    gathered = [st.sem(f"gathered{k}") for k in range(2)]
    loads = [(wg[:, :], "wg"), (att[:, :, :, :], "att"), (norm_par[:, :, :, :], "norm"), (iota[:, :], "iota")]
    block = st.ctx.enter_context(nc.Block())

    def chunks(eng, body):
        n = eng.value_load(con["most"][0:1, 0:1], min_val=0, max_val=EW)
        with eng.Fori(0, CHUNKS // 2 // RUN) as o:
            with eng.If(n > o * (RUN * 2 * CH)):
                with eng.Fori(0, RUN) as i:
                    with eng.If(n > o * (RUN * 2 * CH) + i * (2 * CH)):
                        for k in range(2):
                            body(o * (RUN * 2) + i * 2 + k, k, o * RUN + i)
        return n

    @block.sync
    def _(sp):
        for dst, src in loads:
            sp.dma_start(dst, a[f"gat_{src}"]).then_inc(weights_in, 16)
        sp.wait_ge(tables, 1)
        sp.dma_start(rows_dram.rearrange("(h p) f -> p h f", p=P), rowt[:, :, :]).then_inc(rows_out, 16)
        sp.wait_ge(rows_out, 16)

    @block.gpsimd
    def _(pool):
        pool.memset(spare[:, :], 0.0).then_inc(carried, 1)
        pool.wait_ge(carried, 1)
        pool.wait_ge(maxed, 1)
        pool.partition_all_reduce(amax[:, :], amax1[:, :], P, bass.bass_isa.ReduceOp.max).then_inc(maxed, 1)
        pool.wait_ge(rows_out, 16)

        def gather(want, k):
            pool.wait_ge(staged, want)
            pool.wait_ge(carried, want)
            pool.tensor_tensor(spare[:, 1:2], spare[:, 0:1], spare[:, 0:1], ALU.add).then_inc(carried, 1)
            for t in range(CH):
                pool.indirect_dma_start(rows[k][:, t, :], None, rows_dram,
                                        bass.IndirectOffsetOnAxis(ap=index[k][:, t:t + 1], axis=0)).then_inc(gathered[k], 16)

        for c in range(AHEAD):
            gather(c + 1, c)
        chunks(pool, lambda c, k, i: gather(c + AHEAD + 1, k))

    @block.tensor
    def _(pe):
        pe.wait_ge(weights_in, 16 * len(loads))
        for n in range(TILES):
            mm = pe.matmul(feat_ps[:, n, :, :].rearrange("p h f -> p (h f)"), X[:, n * P:(n + 1) * P], wg[:, :], start=True, stop=True)
        mm.then_inc(featured, 1)
        pe.wait_ge(zero_set, 1)
        for w in range(2):
            mm = pe.matmul(sum_ps[:, w, :], zeros[:, 0:P], zeros[:, :], start=True, stop=False, skip_group_check=True)
        mm.then_inc(scattered, 1)

        def turn(want, k):
            pe.wait_ge(onehot, want)
            for t in range(CH):
                mm = pe.transpose(turn_ps[:, t * P:(t + 1) * P], oh_low[k][:, t, :], con["ident"])
            mm.then_inc(turned, 1)

        def targets(want, k):
            pe.wait_ge(turned_kept, want)
            for t in range(CH):
                for part in range(3):
                    mm = pe.matmul(gat_ps[:, t, :], turned_b[:, t * P:(t + 1) * P], adp[:, part, :], start=part == 0, stop=part == 2)
            mm.then_inc(target_out, 1)

        pe.wait_ge(prepared, 1)
        turn(1, 0)
        targets(1, 0)

        def chunk(c, k, i):
            turn(c + 2, 1 - k)
            for t in range(CH):
                pe.wait_ge(spreaded, c * CH + t + 1)
                for w in range(2):
                    mm = pe.matmul(sum_ps[:, w, 0:HB * NF], oh_low[k][:, t, :],
                                   spread[:, t, w * HB:(w + 1) * HB, :].rearrange("p h f -> p (h f)"),
                                   start=False, stop=False, skip_group_check=True)
                if t == 1:
                    pe.wait_ge(target_read, c + 1)
                    targets(c + 2, 1 - k)
            mm.then_inc(scattered, 1)

        chunks(pe, chunk)
        for w in range(2):
            mm = pe.matmul(sum_ps[:, w, :], zeros[:, 0:P], zeros[:, :], start=False, stop=True, skip_group_check=True)
        mm.then_inc(all_done, 1)

    @block.scalar
    def _(act):
        act.wait_ge(prepared, 1)

        def stage(c, k):
            act.activation(index[k][:, :], srci[:, bass.ds(c * CH, CH)], ACT.Copy).then_inc(staged, 1)

        for c in range(AHEAD):
            stage(c, c)
        act.wait_ge(self_ready, 1)
        act.activation(selfw[:, :, :], selfw[:, :, :], ACT.Exp).then_inc(self_done, 1)

        def turned_copy(want):
            act.wait_ge(turned, want)
            act.activation(turned_b[:, :], turn_ps[:, :], ACT.Copy).then_inc(turned_kept, 1)

        turned_copy(1)

        def chunk(c, k, i):
            act.wait_ge(target_out, c + 1)
            turned_copy(c + 2)
            act.wait_ge(scored, c + 1)
            act.activation(value[:, :, GF:NF], edge[:, :, :], ACT.Exp).then_inc(weighted, 1)
            act.wait_ge(valued, c + 1)
            stage(c + AHEAD, k)

        chunks(act, chunk)
        act.wait_ge(rooted_in, 1)
        act.activation(std, std,
                       ACT.Sqrt, bias=con["eps"]).then_inc(rooted, 1)

    @block.vector
    def _(v):
        count = 0

        def link(ins):
            nonlocal count
            count += 1
            ins.then_inc(chained, 1)
            v.wait_ge(chained, count)

        f2 = lambda t: t.rearrange("p h f -> p (h f)")
        v.memset(zeros[:, :], 0.0).then_inc(zero_set, 1)
        for w in words:
            link(v.memset(w[:, EW:EW + CH * AHEAD], -1))
        link(v.tensor_scalar(words[0][:, 0:EW], con["keys"], -1.0, None, ALU.add))
        link(v.tensor_scalar(words[1][:, :], words[0][:, :], TOK - 1, None, ALU.bitwise_and))
        link(v.tensor_copy(srci[:, :], words[1][:, :]))
        link(v.tensor_scalar(words[1][:, :], words[0][:, :], 12, P - 1, ALU.logical_shift_right, ALU.bitwise_and))
        link(v.tensor_copy(low[:, :], words[1][:, :]))
        link(v.tensor_scalar(words[1][:, :], words[0][:, :], 19, None, ALU.arith_shift_right))
        link(v.tensor_copy(high[:, :], words[1][:, :]))
        v.wait_ge(weights_in, 16 * len(loads))
        v.wait_ge(featured, 1)
        feats = rowt[:, :, HEADS:NF]
        for h in range(2):
            link(v.tensor_copy(feats[:, h * TILES:(h + 1) * TILES, :], feat_ps[:, :, h, :]))
        for w, dst in ((0, rowt[:, :, 0:HEADS]), (1, ad[:, :, :])):
            link(v.tensor_tensor(prod[:, w, :, :], feats, att[:, w, :, :], ALU.mult))
            link(v.tensor_reduce(dst, prod[:, w, :, :].rearrange("p n (h x) -> p n h x", x=GE), AX, ALU.add))
        v.nop().then_inc(tables, 1)
        v.tensor_reduce(amax1[:, :], rowt[:, :, 0:HEADS].rearrange("p n h -> p h n"), AX, ALU.max).then_inc(maxed, 1)
        link(v.tensor_copy(adp[:, 0, :], f2(ad[:, :, :])))
        link(v.tensor_tensor(f2(rest[:, 0, :, :]), f2(ad[:, :, :]), adp[:, 0, :], ALU.subtract))
        link(v.tensor_copy(adp[:, 1, :], f2(rest[:, 0, :, :])))
        link(v.tensor_tensor(f2(rest[:, 1, :, :]), f2(rest[:, 0, :, :]), adp[:, 1, :], ALU.subtract))
        link(v.tensor_copy(adp[:, 2, :], f2(rest[:, 1, :, :])))
        v.nop().then_inc(prepared, 1)

        def leaky(dst, src):
            return v.scalar_tensor_tensor(dst, src, 0.2, src, ALU.mult, ALU.max)

        v.wait_ge(maxed, 2)
        link(v.tensor_tensor(shift[:, :, :], ad[:, :, :], amax[:, None, :].to_broadcast((P, HI, HEADS)), ALU.add))
        link(leaky(shift[:, :, :], shift[:, :, :]))
        link(v.tensor_tensor(selfw[:, :, :], rowt[:, :, 0:HEADS], ad[:, :, :], ALU.add))
        link(leaky(selfw[:, :, :], selfw[:, :, :]))
        v.tensor_tensor(selfw[:, :, :], selfw[:, :, :], shift[:, :, :], ALU.subtract).then_inc(self_ready, 1)

        def one_hots(c, k):
            cols = bass.ds(c * CH, CH)
            v.tensor_tensor(oh_high[k][:, :, :], high[:, cols][:, :, None].to_broadcast((P, CH, HI)),
                            iota[:, None, 0:HI].to_broadcast((P, CH, HI)), ALU.is_equal)
            v.tensor_tensor(oh_low[k][:, :, :], low[:, cols][:, :, None].to_broadcast((P, CH, P)),
                            iota[:, None, :].to_broadcast((P, CH, P)), ALU.is_equal).then_inc(onehot, 1)

        one_hots(0, 0)

        def chunk(c, k, i):
            v.wait_ge(scattered, c + 1)
            one_hots(c + 1, 1 - k)
            v.wait_ge(target_out, c + 1)
            v.tensor_tensor(picked[:, :, :, :], gat_ps[:, :, :].rearrange("p c (h x) -> p c h x", x=HEADS),
                            oh_high[k][:, :, :, None].to_broadcast((P, CH, HI, HEADS)), ALU.mult).then_inc(target_read, 1)
            v.wait_ge(target_read, c + 1)
            v.tensor_reduce(ade[:, :, :], picked[:, :, :, :].rearrange("p c h x -> p c x h"), AX, ALU.add).then_inc(reduced, 1)
            v.wait_ge(gathered[k], (i + 1) * (16 * CH))
            v.wait_ge(reduced, c + 1)
            v.tensor_tensor(edge[:, :, :], rows[k][:, :, 0:HEADS], ade[:, :, :], ALU.add).then_inc(step1, 1)
            v.tensor_tensor(bound[:, :, :], ade[:, :, :], amax[:, None, :].to_broadcast((P, CH, HEADS)), ALU.add).then_inc(step2, 1)
            v.wait_ge(step1, c + 1)
            leaky(edge[:, :, :], edge[:, :, :]).then_inc(step3, 1)
            v.wait_ge(step2, c + 1)
            leaky(bound[:, :, :], bound[:, :, :]).then_inc(step4, 1)
            v.wait_ge(step3, c + 1)
            v.wait_ge(step4, c + 1)
            v.tensor_tensor(edge[:, :, :], edge[:, :, :], bound[:, :, :], ALU.subtract).then_inc(scored, 1)
            v.wait_ge(weighted, c + 1)
            v.tensor_tensor(value[:, :, 0:GF].rearrange("p c (h x) -> p c h x", x=GE),
                            rows[k][:, :, HEADS:NF].rearrange("p c (h x) -> p c h x", x=GE),
                            value[:, :, GF:NF][:, :, :, None].to_broadcast((P, CH, HEADS, GE)), ALU.mult).then_inc(valued, 1)
            v.wait_ge(valued, c + 1)
            v.wait_ge(scattered, c + 1)
            for t in range(CH):
                v.tensor_tensor(spread[:, t, :, :], oh_high[k][:, t, :, None].to_broadcast((P, HI, NF)),
                                value[:, t, None, :].to_broadcast((P, HI, NF)), ALU.mult).then_inc(spreaded, 1)

        n = chunks(v, chunk)
        v.wait_ge(all_done, 1)
        v.wait_ge(self_done, 1)
        for k in range(2):
            v.wait_ge(gathered[k], ((n + (2 * CH - 1)) // (2 * CH)) * (16 * CH) + 16 * CH)
        msg, den = prod[:, 0, :, :], shift[:, :, :]
        sums = lambda w: sum_ps[:, w, 0:HB * NF].rearrange("p (h f) -> p h f", f=NF)
        link(v.tensor_tensor(msg.rearrange("p n (h x) -> p n h x", x=GE), feats.rearrange("p n (h x) -> p n h x", x=GE),
                             selfw[:, :, :, None].to_broadcast((P, HI, HEADS, GE)), ALU.mult))
        for w in range(2):
            part = slice(w * HB, (w + 1) * HB)
            link(v.tensor_tensor(msg[:, part, :], msg[:, part, :], sums(w)[:, :, 0:GF], ALU.add))
            link(v.tensor_tensor(den[:, part, :], selfw[:, part, :], sums(w)[:, :, GF:NF], ALU.add))
        link(v.tensor_scalar(den, den, 1e-16, None, ALU.add))
        link(v.reciprocal(den, den))
        link(v.tensor_tensor(msg.rearrange("p n (h x) -> p n h x", x=GE), msg.rearrange("p n (h x) -> p n h x", x=GE),
                             den[:, :, :, None].to_broadcast((P, HI, HEADS, GE)), ALU.mult))
        link(v.tensor_tensor(msg, msg, norm_par[:, 0, :, :], ALU.add))
        mean, cen = ad[:, :, 0], prod[:, 1, :, :]
        link(v.tensor_reduce(mean, msg, AX, ALU.add))
        link(v.tensor_scalar(mean, mean, 1.0 / GF, None, ALU.mult))
        bc = lambda t: t[:, :, None].to_broadcast((P, HI, GF))
        link(v.tensor_tensor(cen, msg, bc(mean), ALU.subtract))
        link(v.tensor_tensor(msg, cen, cen, ALU.mult))
        link(v.tensor_reduce(std, msg, AX, ALU.add))
        v.tensor_scalar(std, std, 1.0 / GF, None, ALU.mult).then_inc(rooted_in, 1)
        v.wait_ge(rooted, 1)
        link(v.reciprocal(std, std))
        link(v.tensor_tensor(cen, cen, bc(std), ALU.mult))
        link(v.tensor_tensor(cen, cen, norm_par[:, 1, :, :], ALU.mult))
        link(v.tensor_tensor(cen, cen, norm_par[:, 2, :, :], ALU.add))
        link(v.tensor_reduce(ad[:, :, :], cen.rearrange("p n (h x) -> p n x h", x=GE), AX, ALU.add))
        for h in range(2):
            link(v.tensor_scalar(con["scores"].rearrange("p (j h x) -> p h j x", h=2, x=GE)[:, h], ad[:, h * TILES:(h + 1) * TILES, :],
                                 1.0 / HEADS, None, ALU.mult))

    st.end()


def fourth_experts(nc, con, X, a):
    experts(nc, con, X, a, "ffn3", 4, 1, ACT.Gelu, scored=con["scores"])



def build(nc, a, out):
    with ExitStack() as ctx:
        X = ctx.enter_context(nc.sbuf_tensor("X", [P, HALF], F32))
        consts = ctx.enter_context(nc.sbuf_tensor("consts", [P, 5 * P + 8], F32))
        con = {"consts": consts[:, :]}
        for n, name in enumerate(("ident", "centre", "average", "mean128", "ones")):
            con[name] = consts[:, n * P:(n + 1) * P]
        con["eps"] = consts[:, 5 * P:5 * P + 1]
        keys = ctx.enter_context(nc.sbuf_tensor("keys", [P, EW], F32))
        most = ctx.enter_context(nc.sbuf_tensor("most", [P, 1], I32))
        scores = ctx.enter_context(nc.sbuf_tensor("scores", [P, HI * GE], F32))
        con["scores"] = scores[:, :]
        con["keys"], con["most"] = keys[:, :], most[:, :]
        tokenizer(nc, con, X, a)
        stages = STAGE_LIST()
        for n, stage in enumerate(stages):
            if n < STAGES:
                stage(nc, con, X, a)
        finish(nc, con, X, out)


def STAGE_LIST():
    return [first_attention, first_experts, second_attention, routed_mlp,
            third_attention, third_experts, fourth_attention,
            order_edges, graph_attention, fourth_experts]


def constants(np):
    eye = np.eye(P, dtype=np.float32)
    half = np.kron(np.eye(2), np.ones((D, D))).astype(np.float32) / D
    t = np.arange(P)
    s, u = t[:, None], t[None, :]
    decay = np.where((s // T == u // T) & (s < u), 0.97 ** np.maximum(u - s - 1.0, 0), 0).astype(np.float32)
    tail = np.zeros((P, 8), np.float32)
    tail[:, 0] = EPS
    return {
        "consts": np.concatenate([eye, eye - half, half, np.full((P, P), 1 / P, np.float32), np.ones((P, P), np.float32), tail], 1),
        "decay": np.tile(decay, (1, TJ)),
        "later": np.tile((np.arange(2 * GC) % T != 0).astype(np.float32), (P, 1)),
    }


def kernel(**inputs):
    import numpy as np
    import concourse.bacc as bacc
    from concourse.bass_utils import run_bass_kernel_spmd

    i = {k: np.asarray(v) for k, v in inputs.items()}

    def rows(w):
        z = np.zeros((P, 2) + w.shape[1:], w.dtype)
        z[:D, 0], z[D:, 1] = w, w
        return z

    def cols(w):
        z = np.zeros((w.shape[0], 2, P), w.dtype)
        z[:, 0, :D], z[:, 1, D:] = w, w
        return z

    def both(w):
        n = w.shape[1]
        z = np.zeros((P, 2 * n), w.dtype)
        z[:D, :n], z[D:, n:] = w, w
        return z

    def twice(w):
        return np.concatenate([w, w], 0)

    arrays = constants(np)
    arrays["x"] = i["x"].reshape(TOK, D * 4)
    arrays["tok"] = np.concatenate([i["L0_tok_W"], i["L0_tok_b"][:, None]], 1)
    arrays["dx"] = rows(i["L0_attn_Dx"].T)
    arrays["dy"] = rows(i["L0_attn_Dy"].T)
    e = cols(i["L0_attn_E"].T).reshape(2, P, 2, P)
    arrays["et"] = e.transpose(1, 2, 0, 3)
    def moe(name, w1, b1, w2, b2, wr=None, biases=()):
        E, _, hidden = w1.shape
        hc = hidden // P
        arrays[f"{name}_w1"] = rows(w1.transpose(1, 0, 2))
        arrays[f"{name}_w2"] = cols(w2.reshape(E * hidden, D)).reshape(E, hc, P, 2, P).transpose(2, 0, 1, 3, 4)
        arrays[f"{name}_b1"] = b1.reshape(E, hc, P).transpose(2, 0, 1)
        z = np.zeros((2, E, P), np.float32)
        z[0, :, :D], z[1, :, D:] = b2, b2
        arrays[f"{name}_b2"] = z.reshape(2 * E, P)
        if wr is not None:
            arrays[f"{name}_wr"] = both(wr)
            biases = list(biases) + [np.zeros(E, np.float32)] * (2 - len(biases))
            arrays[f"{name}_br"] = np.broadcast_to(np.stack(biases)[None, :, None], (P, 2, 2 * TJ, E))

    moe("ffn0", i["L0_ffn_W1"], i["L0_ffn_b1"], i["L0_ffn_W2"], i["L0_ffn_b2"], i["L0_ffn_Wr"], [i["L0_ffn_br"]])
    arrays["ffn0_scale"], arrays["ffn0_shift"] = twice(i["L0_ffn_ln_g"].T), twice(i["L0_ffn_ln_b"].T)
    moe("ffn2", i["L2_ffn_W1"], i["L2_ffn_b1"], i["L2_ffn_W2"], i["L2_ffn_b2"], i["L2_ffn_Wg"], [i["L2_ffn_bg"], i["L2_ffn_bias"]])
    moe("ffn3", i["L3_ffn_W1"], i["L3_ffn_b1"], i["L3_ffn_W2"], i["L3_ffn_b2"])
    for E in (4, 8):
        z = np.zeros((2, E, E, P), np.float32)
        for e in range(E):
            z[0, e, e, :D], z[1, e, e, D:] = 1, 1
        arrays[f"sel{E}"] = z.reshape(2 * E, E, P)
        arrays[f"index{E}"] = np.broadcast_to(np.arange(E, dtype=np.float32), (P, 2 * TJ, E))

    arrays["att1_wq"], arrays["att1_wm"] = both(i["L1_attn_Wq"]), both(i["L1_attn_Wm"])
    arrays["att1_wkv"] = np.concatenate([both(i["L1_attn_Wk"]), both(i["L1_attn_Wv"])], 1)
    arrays["att1_w1x"], arrays["att1_w1m"] = rows(i["L1_attn_W1"][:D]), rows(i["L1_attn_W1"][D:])
    arrays["att1_w2"] = cols(i["L1_attn_W2"])
    arrays["att1_gb"] = twice(np.stack([i[f"L1_attn_{n}"] for n in ("g1", "b1", "g2", "b2")], 1))
    arrays["att1_heads"] = np.broadcast_to(np.tile(np.kron(np.eye(8), np.ones((8, 8))), (2, 1)).astype(np.float32)[:, None], (P, GB, D))
    arrays["ffn1_wi"], arrays["ffn1_wo"] = rows(i["L1_ffn_Wi"].T), cols(i["L1_ffn_Wo"].T)
    arrays["ffn1_bi"], arrays["ffn1_bo"] = i["L1_ffn_bi"][:, None], twice(i["L1_ffn_bo"][:, None])
    arrays["ffn1_bs"] = i["L1_ffn_bs"][:, 0].T
    arrays["ffn1_ws"] = i["L1_ffn_Ws"][:, 0].transpose(2, 0, 1)
    arrays["route"] = i["L1_ffn_route_id"][None]
    E = i["L1_ffn_Wr"].shape[1]
    arrays["ffn1_experts"] = np.concatenate(
        [i["L1_ffn_Wr"].transpose(3, 1, 0, 2).reshape(P, E, LAYERS * P), i["L1_ffn_br"].transpose(2, 1, 0)], 2).reshape(P, E * ROUTED)
    arrays["att2_c"] = twice(i["L2_attn_c"][0])
    for n in "BCD":
        arrays[f"att3_w{n.lower()}"] = both(i[f"L3_attn_W_{n}"].T)
    arrays["att3_par"] = twice(np.stack([i[f"L3_attn_{n}"] for n in ("a", "b_B", "b_C", "b_D")], 1))
    edges = i["L3_ffn_edge_index"].reshape(2, P, EW)
    arrays["edge_src"], arrays["edge_dst"] = edges[0], edges[1]
    arrays["gat_wg"] = both(i["L3_ffn_W_gat"])
    across = lambda *w: np.broadcast_to(np.stack([x.reshape(GF) for x in w])[None, :, None], (P, len(w), HI, GF))
    arrays["gat_att"] = across(i["L3_ffn_att_src"], i["L3_ffn_att_dst"])
    arrays["gat_norm"] = across(i["L3_ffn_b_gat"], i["L3_ffn_ln_gamma"], i["L3_ffn_ln_beta"])
    arrays["gat_iota"] = np.broadcast_to(np.arange(P, dtype=np.float32), (P, P))
    nc = bacc.Bacc("TRN2", target_bir_lowering=False, num_devices=1)
    arrays = {f"in_{k}": np.ascontiguousarray(v) for k, v in arrays.items()}
    a = {k[3:]: nc.dram_tensor(k, v.shape, mybir.dt.from_np(v.dtype), kind="ExternalInput").ap() for k, v in arrays.items()}
    out = nc.dram_tensor("out", (TOK, D), F32, kind="ExternalOutput").ap()
    build(nc, a, out)
    r = run_bass_kernel_spmd(nc, [arrays], core_ids=[0])
    return r.results[0]["out"].reshape(B, T, D)
```

```python
from contextlib import ExitStack

import concourse.bass as bass
from concourse import mybir
from concourse.alu_op_type import AluOpType as ALU

F32 = mybir.dt.float32
I32 = mybir.dt.int32
U32 = mybir.dt.uint32
ACT = mybir.ActivationFunctionType
AX = mybir.AxisListType.X

P = 128
B, T, D = 64, 64, 64
TOK = B * T
HALF = TOK // 2
GC = 512
G = HALF // GC
TJ = GC // P
GB = GC // T
NH = 256
EPS = 1e-5
LN_EXP = "natural_log_exp_and_others"
STAGES = 99


class Stage:

    def __init__(self, nc, name):
        self.nc, self.name, self.ctx, self.all = nc, name, ExitStack(), []

    def sem(self, what):
        s = self.nc.alloc_semaphore(f"{self.name}_{what}")
        self.all.append(s)
        return s

    def sems(self, names):
        return [self.sem(n) for n in names.split()]

    def sb(self, what, shape, dt=F32):
        return self.ctx.enter_context(self.nc.sbuf_tensor(f"{self.name}_{what}", shape, dt))

    def ps(self, what, shape):
        return self.ctx.enter_context(self.nc.psum_tensor(f"{self.name}_{what}", shape, F32))

    def end(self):
        self.ctx.close()
        self.nc.clear_and_free_semaphores(self.all)
        self.nc.all_engine_barrier()


class Norm:

    def __init__(self, st, name, con, centred_ps, var_ps, sq, std, switch=False):
        self.switch = switch
        self.con, self.cp, self.vp, self.sq, self.std = con, centred_ps, var_ps, sq, std
        self.centred, self.squared, self.averaged, self.rooted, self.inverted, self.normed = st.sems(
            " ".join(f"{name}_{x}" for x in "centred squared averaged rooted inverted normed".split()))

    def tensor_centre(self, pe, src, src_ready, g):
        pe.wait_ge(src_ready, g + 1)
        pe.matmul(self.cp, self.con["centre"], src, start=True, stop=True).then_inc(self.centred, 1)

    def tensor_average(self, pe, g):
        pe.wait_ge(self.squared, g + 1)
        pe.matmul(self.vp, self.con["average"], self.sq, start=True, stop=True).then_inc(self.averaged, 1)

    def scalar(self, act, g):
        self.scalar_square(act, g)
        self.scalar_root(act, g)

    def scalar_square(self, act, g):
        act.wait_ge(self.centred, g + 1)
        act.activation(self.sq, self.cp, ACT.Square).then_inc(self.squared, 1)

    def scalar_root(self, act, g):
        if self.switch:
            act.preload_act_table_set(LN_EXP)
        act.wait_ge(self.averaged, g + 1)
        act.activation(self.std, self.vp, ACT.Ln, bias=self.con["eps"]).then_inc(self.rooted, 1)
        act.wait_ge(self.rooted, g + 1)
        act.activation(self.std, self.std, ACT.Exp, scale=-0.5).then_inc(self.inverted, 1)

    def vector(self, v, out, g):
        v.wait_ge(self.inverted, g + 1)
        v.tensor_tensor(out, self.cp, self.std, ALU.mult).then_inc(self.normed, 1)


def group(t, g):
    return t[:, bass.ds(g * GC, GC)]


def tokenizer(nc, con, X, a):
    st = Stage(nc, "tok")
    F = 4
    wb = st.sb("wb", [P, F + 1])
    mean = st.sb("mean", [P, F + 1])
    xin = [st.sb(f"xin{k}", [P, TJ, 2, D * F]) for k in range(G)]
    tm = [st.sb(f"tm{k}", [P, GC]) for k in range(G)]
    mean_ps = st.ps("mean_ps", [P, F + 1])
    turn_ps = [st.ps(f"turn_ps{k}", [P, GC]) for k in range(G)]
    consts_in, w_in, meaned, mean_kept, summed, turned, kept = st.sems(
        "consts_in w_in meaned mean_kept summed turned kept")
    x_in = [st.sem(f"x_in{k}") for k in range(G)]
    edge_src, edge_dst = st.sb("edge_src", [P, EW], I32), st.sb("edge_dst", [P, EW], I32)
    inside = st.sb("inside", [P, EW])
    src_in, dst_in, cleared, capped, keyed, marked = st.sems("src_in dst_in cleared capped keyed marked")
    xr = a["x"].rearrange("(h k j p) c -> k p j h c", h=2, k=G, j=TJ, p=P)
    block = st.ctx.enter_context(nc.Block())

    @block.sync
    def _(sp):
        sp.dma_start(con["consts"], a["consts"]).then_inc(consts_in, 16)
        sp.dma_start(wb[:, :], a["tok"]).then_inc(w_in, 16)
        for k in range(G):
            for j in range(TJ):
                sp.dma_start(xin[k][:, j, :, :], xr[k][:, j, :, :]).then_inc(x_in[k], 16)
        sp.dma_start(edge_src[:, :], a["edge_src"]).then_inc(src_in, 16)
        sp.dma_start(edge_dst[:, :], a["edge_dst"]).then_inc(dst_in, 16)

    @block.tensor
    def _(pe):
        pe.wait_ge(consts_in, 16)
        pe.wait_ge(w_in, 16)
        pe.matmul(mean_ps[:, :], con["mean128"], wb[:, :], start=True, stop=True).then_inc(meaned, 1)
        for k in range(G):
            pe.wait_ge(summed, F * k + F)
            for j in range(TJ):
                mm = pe.transpose(turn_ps[k][:, j * P:(j + 1) * P], tm[k][:, j * P:(j + 1) * P], con["ident"])
            mm.then_inc(turned, 1)

    @block.vector
    def _(v):
        v.wait_ge(meaned, 1)
        v.tensor_copy(mean[:, :], mean_ps[:, :]).then_inc(mean_kept, 1)
        v.wait_ge(mean_kept, 1)
        for k in range(G):
            v.wait_ge(x_in[k], 16 * TJ)
            xf = xin[k][:, :, :, :].rearrange("p j h (d f) -> p (j h d) f", f=F)
            v.tensor_scalar(tm[k][:, :], xf[:, :, 0], mean[:, 0:1], mean[:, F:F + 1], ALU.mult,
                            ALU.add).then_inc(summed, 1)
            for f in range(1, F):
                v.wait_ge(summed, F * k + f)
                v.scalar_tensor_tensor(tm[k][:, :], xf[:, :, f], mean[:, f:f + 1], tm[k][:, :],
                                       ALU.mult, ALU.add).then_inc(summed, 1)
        key = con["left"][:, 0:EW]
        v.memset(con["keys"], 0.0)
        v.memset(con["padded"][:, GC + HALF:], 0.0)
        v.memset(con["scores"], 0.0)
        v.wait_ge(src_in, 16)
        v.tensor_scalar(inside[:, :], edge_src[:, :], float(TOK - 1), 1.0, ALU.min, ALU.add).then_inc(capped, 1)
        v.wait_ge(capped, 1)
        v.wait_ge(dst_in, 16)
        v.scalar_tensor_tensor(key, edge_dst[:, :], float(TOK), inside[:, :], ALU.mult, ALU.add).then_inc(keyed, 1)
        v.wait_ge(keyed, 1)
        v.tensor_scalar(inside[:, :], edge_dst[:, :], float(TOK), None, ALU.is_lt).then_inc(marked, 1)
        v.wait_ge(marked, 1)
        v.tensor_tensor(key, key, inside[:, :], ALU.mult)
        v.tensor_reduce(con["edge_count"], inside[:, :], AX, ALU.add)

    @block.scalar
    def _(act):
        for k in range(G):
            act.wait_ge(turned, k + 1)
            act.activation(X[:, k * GC:(k + 1) * GC], turn_ps[k][:, :], ACT.Copy).then_inc(kept, 1)

    st.end()


def first_attention(nc, con, X, a):
    st = Stage(nc, "att0")
    A = 0.97
    BIG = 1e12
    dx = st.sb("dx", [P, 2, NH])
    dy = st.sb("dy", [P, 2, NH])
    et = st.sb("et", [P, 2, 2, P])
    decay = st.sb("decay", [P, GC])
    later = st.sb("later", [P, 2 * GC])
    xg, nv, u = st.sb("xg", [P, GC]), st.sb("nv", [P, GC]), st.sb("u", [P, 4, GC])
    sq, std = st.sb("sq", [P, GC]), st.sb("std", [P, GC])
    run, q, sig, r, keep = [st.sb(n, [P, 2 * GC]) for n in ("run", "q", "sig", "r", "keep")]
    ur, xs = st.sb("ur", [P, 4, GC]), st.sb("xs", [P, 4, GC])
    gm, nvt = st.sb("gm", [P, 2, GC]), st.sb("nvt", [P, GC])
    an, asum, y, vs, hsum = st.sb("an", [P, GC]), st.sb("asum", [P, GC]), st.sb("y", [P, 4, GC]), st.sb("vs", [P, GC]), st.sb("hsum", [P, GC])
    big = st.ps("big", [P, 4, GC])
    sums = st.ps("sums", [P, 2, GC])
    cp, vp = st.ps("cp", [P, GC]), st.ps("vp", [P, GC])
    weights_in, grouped, u_made, u_kept, u_summed = st.sems("weights_in grouped u_made u_kept u_summed")
    ran, capped, q_raw, q_first, q_made, s_raw, s_first, sig_made = st.sems("ran capped q_raw q_first q_made s_raw s_first sig_made")
    raw, raw_first, guarded, inverted, kept, scaled, scanned = st.sems("raw raw_first guarded inverted kept scaled scanned")
    grams, masked, v_turned, v_kept, attended, a_kept, y_made, gated, v_made, vs_kept, added = st.sems(
        "grams masked v_turned v_kept attended a_kept y_made gated v_made vs_kept added")
    n_v = Norm(st, "nv", con, cp[:, :], vp[:, :], sq[:, :], std[:, :])
    n_a = Norm(st, "na", con, cp[:, :], vp[:, :], sq[:, :], std[:, :])
    n_s = Norm(st, "ns", con, cp[:, :], vp[:, :], sq[:, :], std[:, :])
    n_o = Norm(st, "no", con, cp[:, :], vp[:, :], sq[:, :], std[:, :])
    steps = lambda t: t[:, :].rearrange("p (b t) -> p b t", t=T)
    flat_sums = sums[:, :, :].rearrange("p h c -> p (h c)")
    block = st.ctx.enter_context(nc.Block())

    @block.sync
    def _(sp):
        for dst, src in ((dx[:, :, :], "dx"), (dy[:, :, :], "dy"), (et[:, :, :, :], "et"),
                         (decay[:, :], "decay"), (later[:, :], "later")):
            sp.dma_start(dst, a[src]).then_inc(weights_in, 16)

    @block.tensor
    def _(pe):
        pe.wait_ge(weights_in, 80)
        with pe.Fori(0, G) as g:
            n_v.tensor_centre(pe, xg[:, :], grouped, g)
            for h in range(2):
                for c in range(2):
                    mm = pe.matmul(big[:, 2 * h + c, :], dx[:, h, c * P:(c + 1) * P], xg[:, :], start=True, stop=True)
            mm.then_inc(u_made, 1)
            n_v.tensor_average(pe, g)
            pe.wait_ge(u_kept, g + 1)
            for h in range(2):
                for c in range(2):
                    mm = pe.matmul(sums[:, h, :], con["ones"], u[:, 2 * h + c, :], start=c == 0, stop=c == 1)
            mm.then_inc(u_summed, 1)
            pe.wait_ge(n_v.normed, g + 1)
            for j in range(TJ):
                mm = pe.transpose(big[:, 2, j * P:(j + 1) * P], nv[:, j * P:(j + 1) * P], con["ident"])
            mm.then_inc(v_turned, 1)
            pe.wait_ge(scanned, 4 * g + 4)
            for h in range(2):
                for j in range(TJ):
                    for c in range(2):
                        xt = xs[:, 2 * h + c, j * P:(j + 1) * P]
                        mm = pe.matmul(big[:, h, j * P:(j + 1) * P], xt, xt, start=c == 0, stop=c == 1)
            mm.then_inc(grams, 1)
            pe.wait_ge(masked, g + 1)
            pe.wait_ge(v_kept, g + 1)
            for h in range(2):
                for j in range(TJ):
                    mm = pe.matmul(big[h * D:(h + 1) * D, 3, j * P:(j + 1) * P], nvt[:, j * P + h * D:j * P + (h + 1) * D],
                                   gm[:, h, j * P:(j + 1) * P], start=True, stop=True)
            mm.then_inc(attended, 1)
            n_a.tensor_centre(pe, asum[:, :], a_kept, g)
            n_a.tensor_average(pe, g)
            pe.wait_ge(n_a.normed, g + 1)
            for h in range(2):
                for c in range(2):
                    mm = pe.matmul(big[:, 2 * h + c, :], dy[:, h, c * P:(c + 1) * P], an[:, :], start=True, stop=True)
            mm.then_inc(y_made, 1)
            pe.wait_ge(gated, g + 1)
            for n in range(4):
                mm = pe.matmul(sums[:, 0, :], et[:, n // 2, n % 2, :], y[:, n, :], start=n == 0, stop=n == 3)
            mm.then_inc(v_made, 1)
            n_s.tensor_centre(pe, vs[:, :], vs_kept, g)
            n_s.tensor_average(pe, g)
            n_o.tensor_centre(pe, hsum[:, :], added, g)
            n_o.tensor_average(pe, g)

    @block.scalar
    def _(act):
        act.preload_act_table_set(LN_EXP)
        with act.Fori(0, G) as g:
            act.wait_ge(u_made, g + 1)
            act.activation(u[:, :, :], big[:, :, :], ACT.Relu).then_inc(u_kept, 1)
            n_v.scalar(act, g)
            act.wait_ge(v_turned, g + 1)
            act.activation(nvt[:, :], big[:, 2, :], ACT.Copy).then_inc(v_kept, 1)
            act.wait_ge(attended, g + 1)
            act.activation(asum[:, :], big[:, 3, :], ACT.Copy).then_inc(a_kept, 1)
            n_a.scalar(act, g)
            act.wait_ge(v_made, g + 1)
            act.activation(vs[:, :], sums[:, 0, :], ACT.Copy).then_inc(vs_kept, 1)
            n_s.scalar(act, g)
            n_o.scalar(act, g)

    @block.vector
    def _(v):
        v.wait_ge(weights_in, 80)
        with v.Fori(0, G) as g:
            v.tensor_copy(xg[:, :], group(X, g)).then_inc(grouped, 1)
            n_v.vector(v, nv[:, :], g)
            v.wait_ge(u_summed, g + 1)
            v.tensor_tensor_scan(run[:, :], later[:, :], flat_sums, 0.0, ALU.mult, ALU.max).then_inc(ran, 1)
            v.wait_ge(ran, g + 1)
            v.tensor_scalar(run[:, :], run[:, :], BIG, 1.0, ALU.mult, ALU.min).then_inc(capped, 1)
            v.wait_ge(capped, g + 1)
            v.tensor_copy(steps(q)[:, :, 0], steps(run)[:, :, 0]).then_inc(q_first, 1)
            v.scalar_tensor_tensor(steps(q)[:, :, 1:T], steps(run)[:, :, 0:T - 1], A * BIG, steps(run)[:, :, 1:T],
                                   ALU.mult, ALU.add).then_inc(q_raw, 1)
            v.wait_ge(q_first, g + 1)
            v.wait_ge(q_raw, g + 1)
            v.tensor_scalar(q[:, :], q[:, :], 1.0, None, ALU.min).then_inc(q_made, 1)
            v.wait_ge(q_made, g + 1)
            v.tensor_copy(steps(sig)[:, :, 0], steps(run)[:, :, 0]).then_inc(s_first, 1)
            v.scalar_tensor_tensor(steps(sig)[:, :, 1:T], steps(q)[:, :, 0:T - 1], A * BIG, steps(run)[:, :, 1:T],
                                   ALU.mult, ALU.add).then_inc(s_raw, 1)
            v.wait_ge(s_first, g + 1)
            v.wait_ge(s_raw, g + 1)
            v.tensor_scalar(sig[:, :], sig[:, :], 1.0, None, ALU.min).then_inc(sig_made, 1)
            v.wait_ge(sig_made, g + 1)
            sb3 = flat_sums.rearrange("p (b t) -> p b t", t=T)
            v.tensor_copy(steps(r)[:, :, 0], sb3[:, :, 0]).then_inc(raw_first, 1)
            v.scalar_tensor_tensor(steps(r)[:, :, 1:T], steps(sig)[:, :, 0:T - 1], A, sb3[:, :, 1:T],
                                   ALU.mult, ALU.add).then_inc(raw, 1)
            v.wait_ge(raw_first, g + 1)
            v.wait_ge(raw, g + 1)
            v.tensor_scalar(r[:, :], r[:, :], 1.0 / BIG, None, ALU.max).then_inc(guarded, 1)
            v.wait_ge(guarded, g + 1)
            v.reciprocal(r[:, :], r[:, :]).then_inc(inverted, 1)
            v.wait_ge(inverted, g + 1)
            v.scalar_tensor_tensor(keep[:, :], r[:, :], A, later[:, :], ALU.mult, ALU.mult).then_inc(kept, 1)
            for n in range(4):
                rh = r[:, (n // 2) * GC:(n // 2 + 1) * GC]
                v.tensor_tensor(ur[:, n, :], u[:, n, :], rh, ALU.mult).then_inc(scaled, 1)
            v.wait_ge(kept, g + 1)
            for n in range(4):
                v.wait_ge(scaled, 4 * g + n + 1)
                v.tensor_tensor_scan(xs[:, n, :], keep[:, (n // 2) * GC:(n // 2 + 1) * GC], ur[:, n, :], 0.0,
                                     ALU.mult, ALU.add).then_inc(scanned, 1)
            v.wait_ge(grams, g + 1)
            for h in range(2):
                ins = v.tensor_tensor(gm[:, h, :], big[:, h, :], decay[:, :], ALU.mult)
            ins.then_inc(masked, 1)
            n_a.vector(v, an[:, :], g)
            v.wait_ge(y_made, g + 1)
            v.scalar_tensor_tensor(y[:, :, :].rearrange("p n c -> p (n c)"), big[:, :, :].rearrange("p n c -> p (n c)"), 0.0,
                                   xs[:, :, :].rearrange("p n c -> p (n c)"), ALU.max, ALU.mult).then_inc(gated, 1)
            n_s.vector(v, vs[:, :], g)
            v.wait_ge(n_s.normed, g + 1)
            v.tensor_tensor(hsum[:, :], xg[:, :], vs[:, :], ALU.add).then_inc(added, 1)
            n_o.vector(v, group(X, g), g)

    st.end()


def finish(nc, con, X, out):
    st = Stage(nc, "out")
    rows = [st.sb(f"rows{k}", [P, TJ, P]) for k in range(G)]
    turn_ps = [st.ps(f"turn_ps{k}", [P, GC]) for k in range(G)]
    turned, kept = st.sems("turned kept")
    stored = [st.sem(f"stored{k}") for k in range(G)]
    ov = out.rearrange("(h k j p) d -> k h p j d", h=2, k=G, j=TJ, p=P)
    block = st.ctx.enter_context(nc.Block())

    @block.tensor
    def _(pe):
        for k in range(G):
            for j in range(TJ):
                c = k * GC + j * P
                mm = pe.transpose(turn_ps[k][:, j * P:(j + 1) * P], X[:, c:c + P], con["ident"])
            mm.then_inc(turned, 1)

    @block.vector
    def _(v):
        for k in range(G):
            v.wait_ge(turned, k + 1)
            v.tensor_copy(rows[k][:, :, :].rearrange("p j c -> p (j c)"), turn_ps[k][:, :]).then_inc(kept, 1)

    @block.sync
    def _(sp):
        for k in range(G):
            sp.wait_ge(kept, k + 1)
            for h in range(2):
                sp.dma_start(ov[k][h], rows[k][:, :, h * D:(h + 1) * D]).then_inc(stored[k], 16)
        for k in range(G):
            sp.wait_ge(stored[k], 32)

    st.end()

def experts(nc, con, X, a, name, E, HC, act_fn, scored=None, prenorm=False, background=None, spare_work=None):
    st = Stage(nc, name)
    TH = TJ * 2
    N = E * 2 * HC
    XP = con["padded"]
    state = lambda g: XP[:, bass.ds((g + 1) * GC, GC)]
    if E == 8:
        at = dict(leave_centre=0, leave_average=1, leave_root=3, leave_scale=3 if HC == 2 else 4, enter=0, route=1, best=2,
                  exp=3, gate=4, centre=4, average=5, root=5, turn=5, turn_keep=5, scale=6, bias=6, start=6)
    else:
        at = dict(leave_centre=0, leave_average=1, leave_root=1, leave_scale=2, enter=0, route=None, best=0,
                  exp=1, gate=1, centre=None, average=None, root=None, turn=2, turn_keep=2, scale=None, bias=3, start=3)
    w1 = st.sb("w1", [P, 2, E, HC * P])
    w2 = st.sb("w2", [P, E, HC, 2, P])
    b1 = st.sb("b1", [P, E, HC])
    b2 = st.sb("b2", [2 * E, P])
    sel = st.sb("sel", [2 * E, E, P])
    index = st.sb("index", [P, TH, E])
    loads = [(w1[:, :, :, :], "w1"), (w2[:, :, :, :, :], "w2"), (b1[:, :, :], "b1"), (b2[:, :], "b2"),
             (sel[:, :, :], "sel"), (index[:, :, :], "index")]
    if scored is None:
        wr = st.sb("wr", [P, 2 * E])
        br = st.sb("br", [P, 2, TH, E])
        loads += [(wr[:, :], "wr"), (br[:, :, :, :], "br")]
    if prenorm:
        scale, shift = st.sb("scale", [P, E]), st.sb("shift", [P, E])
        loads += [(scale[:, :], "scale"), (shift[:, :], "shift")]
    sq, std, xn = [st.sb(n, [P, GC]) for n in ("sq", "std", "xn")]
    xg, acc, xe, hid, part = [[st.sb(f"{n}{k}", [P, GC]) for k in range(2)] for n in ("xg", "acc", "xe", "hid", "part")]
    spread = [st.sb(f"spread{k}", [P, GC]) for k in range(4)]
    gt = [st.sb(f"gt{k}", [2 * E, GC]) for k in range(2)]
    lo, eq, low, m1, m2, gate = [st.sb(n, [P, TH, E]) for n in ("lo", "eq", "low", "m1", "m2", "gate")]
    top1, top2, first, e2, den, wgt1, wgt2 = [st.sb(n, [P, TH]) for n in ("top1", "top2", "first", "e2", "den", "wgt1", "wgt2")]
    misc, spread_ps, cp, vp = [st.ps(n, [P, GC]) for n in ("misc", "spread_ps", "cp", "vp")]
    hid_ps, out_ps = [[st.ps(f"{n}{k}", [P, GC]) for k in range(2)] for n in ("hid_ps", "out_ps")]
    weights_in, grouped, scored_ps, biased1, biased2 = st.sems("weights_in grouped scored_ps biased1 biased2")
    best1, is1, cand1, first1, mark1, masked, best2, is2, cand2, first2, mark2, diff, exped = st.sems(
        "best1 is1 cand1 first1 mark1 masked best2 is2 cand2 first2 mark2 diff exped")
    summed, weight1, weight2, half_gate, gate2, gated, turned, turned_kept, bias_out, bias_kept = st.sems(
        "summed weight1 weight2 half_gate gate2 gated turned turned_kept bias_out bias_kept")
    hidden, activated, spread_made, spread_kept, out_made, weighed, accumulated, added, tuned = st.sems(
        "hidden activated spread_made spread_kept out_made weighed accumulated added tuned")
    gelu = act_fn == ACT.Gelu
    n_i = Norm(st, "ni", con, cp[:, :], vp[:, :], sq[:, :], std[:, :], gelu) if prenorm else None
    n_o = Norm(st, "no", con, cp[:, :], vp[:, :], sq[:, :], std[:, :], gelu)
    bc = lambda t: t[:, :, None].to_broadcast((P, TH, E))
    runs = spare_work(st) if spare_work else [(0, G // 2, None)]
    block = st.ctx.enter_context(nc.Block())

    @block.sync
    def _(sp):
        for dst, src in loads:
            sp.dma_start(dst, a[f"{name}_{src}" if src not in ("sel", "index") else f"{src}{E}"]).then_inc(weights_in, 16)
        if background is not None:
            background(sp)

    @block.tensor
    def _(pe):
        def route(g, k):
            if scored is None:
                pe.wait_ge(grouped, g + 1)
                pe.wait_ge(bias_kept, g)
                for j in range(TJ):
                    mm = pe.matmul(misc[:, j * 2 * E:(j + 1) * 2 * E], xg[k][:, j * P:(j + 1) * P], wr[:, :], start=True, stop=True)
                mm.then_inc(scored_ps, 1)

        def enter_centre(g, k):
            if prenorm:
                pe.wait_ge(n_o.normed, g)
                n_i.tensor_centre(pe, xg[k][:, :], grouped, g)

        def enter_average(g):
            if prenorm:
                n_i.tensor_average(pe, g)

        def turn(g):
            pe.wait_ge(gated, g + 1)
            pe.wait_ge(bias_kept, g)
            for j in range(TJ):
                mm = pe.transpose(misc[0:2 * E, j * P:(j + 1) * P], gate[:, 2 * j:2 * j + 2, :].rearrange("p h e -> p (h e)"), con["ident"])
            mm.then_inc(turned, 1)

        def bias(g, k):
            pe.wait_ge(turned_kept, g + 1)
            pe.matmul(misc[:, :], b2[:, :], gt[k][:, :], start=True, stop=True).then_inc(bias_out, 1)

        def leave_centre(g, k):
            if prenorm:
                pe.wait_ge(n_i.normed, g + 1)
            pe.wait_ge(n_o.normed, g)
            n_o.tensor_centre(pe, acc[1 - k][:, :], added, g)

        def hidden_of(g, n, k):
            e, h, c = n // (2 * HC), n // HC % 2, n % HC
            if prenorm:
                pe.wait_ge(tuned, g * E + e + 1)
            else:
                pe.wait_ge(grouped, g + 1)
            src = xe[e % 2] if prenorm else xg[k]
            pe.matmul(hid_ps[n % 2][:, :], w1[:, h, e, c * P:(c + 1) * P], src[:, :], start=True, stop=True).then_inc(hidden, 1)

        def output_of(g, n):
            e, h, c = n // (2 * HC), n // HC % 2, n % HC
            if n % (2 * HC) == 0:
                pe.wait_ge(weighed, g * E + e + 1)
            pe.wait_ge(activated, g * N + n + 1)
            mm = pe.matmul(out_ps[e % 2][:, :], w2[:, e, c, h, :], hid[n % 2][:, :],
                           start=n % (2 * HC) == 0, stop=n % (2 * HC) == 2 * HC - 1)
            if n % (2 * HC) == 2 * HC - 1:
                mm.then_inc(out_made, 1)

        def spread_of(g, e, k):
            if e == 0:
                pe.wait_ge(turned_kept, g + 1)
            pe.wait_ge(spread_kept, g * E + e)
            pe.matmul(spread_ps[:, :], sel[:, e, :], gt[k][:, :], start=True, stop=True).then_inc(spread_made, 1)

        pe.wait_ge(weights_in, 16 * len(loads))
        if scored is None:
            pe.wait_ge(grouped, 1)
            for j in range(TJ):
                mm = pe.matmul(misc[:, j * 2 * E:(j + 1) * 2 * E], xg[0][:, j * P:(j + 1) * P], wr[:, :], start=True, stop=True)
            mm.then_inc(scored_ps, 1)
        if prenorm:
            n_i.tensor_centre(pe, xg[0][:, :], grouped, 0)
            enter_average(0)
        hidden_of(0, 0, 0)
        hidden_of(0, 1, 0)
        pe.wait_ge(gated, 1)
        for j in range(TJ):
            mm = pe.transpose(misc[0:2 * E, j * P:(j + 1) * P], gate[:, 2 * j:2 * j + 2, :].rearrange("p h e -> p (h e)"), con["ident"])
        mm.then_inc(turned, 1)
        bias(0, 0)
        pe.matmul(spread_ps[:, :], sel[:, 0, :], gt[0][:, :], start=True, stop=True).then_inc(spread_made, 1)
        with pe.Fori(0, G // 2) as pair:
            for k in range(2):
                g = pair * 2 + k
                for n in range(N):
                    e = n // (2 * HC)
                    output_of(g, n)
                    hidden_of(g + (n + 2) // N, (n + 2) % N, (k + (n + 2) // N) % 2)
                    if n % (2 * HC) == 0:
                        spread_of(g + (e + 1) // E, (e + 1) % E, (k + (e + 1) // E) % 2)
                    if n % (2 * HC) == 1:
                        if at["leave_centre"] == e:
                            leave_centre(g, k)
                        if at["leave_average"] == e:
                            n_o.tensor_average(pe, g)
                        if at["route"] == e:
                            route(g + 1, 1 - k)
                        if at["centre"] == e:
                            enter_centre(g + 1, 1 - k)
                        if at["average"] == e:
                            enter_average(g + 1)
                        if at["turn"] == e:
                            turn(g + 1)
                        if at["bias"] == e:
                            bias(g + 1, 1 - k)
        pe.wait_ge(n_o.normed, G)
        n_o.tensor_centre(pe, acc[1][:, :], added, G)
        n_o.tensor_average(pe, G)

    @block.scalar
    def _(act):
        def exp_gate(g):
            act.wait_ge(diff, g + 1)
            act.activation(e2[:, :], top2[:, :], ACT.Exp).then_inc(exped, 1)

        def spread_copy(g, e):
            act.wait_ge(spread_made, g * E + e + 1)
            act.activation(spread[e % 4][:, :], spread_ps[:, :], ACT.Copy).then_inc(spread_kept, 1)

        act.preload_act_table_set(LN_EXP)
        act.wait_ge(weights_in, 16 * len(loads))
        if prenorm:
            n_i.scalar(act, 0)
        exp_gate(0)
        spread_copy(0, 0)
        with act.Fori(0, G // 2) as pair:
            for k in range(2):
                g = pair * 2 + k
                for n in range(N):
                    e = n // (2 * HC)
                    act.wait_ge(hidden, g * N + n + 1)
                    act.activation(hid[n % 2][:, :], hid_ps[n % 2][:, :], act_fn,
                                   bias=b1[:, e, n % HC:n % HC + 1]).then_inc(activated, 1)
                    if n % (2 * HC) == 1:
                        act.wait_ge(weighed, g * E + e)
                        spread_copy(g + (e + 1) // E, (e + 1) % E)
                    late = n - (3 if HC == 2 else 2)
                    if late % (2 * HC) == 0:
                        e = late // (2 * HC)
                        if at["leave_centre"] == e:
                            n_o.scalar_square(act, g)
                        if at["centre"] == e and prenorm:
                            n_i.scalar_square(act, g + 1)
                        if at["leave_root"] == e:
                            n_o.scalar_root(act, g)
                        if at["exp"] == e:
                            exp_gate(g + 1)
                        if at["root"] == e and prenorm:
                            n_i.scalar_root(act, g + 1)
        n_o.scalar(act, G)

    @block.vector
    def _(v):
        def enter(g, k):
            v.tensor_copy(xg[k][:, :], state(g)).then_inc(grouped, 1)

        def scale_entry(g):
            if prenorm:
                n_i.vector(v, xn[:, :], g)
                v.wait_ge(n_i.normed, g + 1)

        def tune(e):
            v.tensor_scalar(xe[e % 2][:, :], xn[:, :], scale[:, e:e + 1], shift[:, e:e + 1], ALU.mult, ALU.add).then_inc(tuned, 1)

        def best_two(g):
            if scored is None:
                v.wait_ge(scored_ps, g + 1)
                lg = misc[:, 0:TH * E].rearrange("p (t e) -> p t e", e=E)
                v.tensor_tensor(lo[:, :, :], lg, br[:, 0, :, :], ALU.add).then_inc(biased1, 1)
                v.wait_ge(biased1, g + 1)
                v.tensor_tensor(lo[:, :, :], lo[:, :, :], br[:, 1, :, :], ALU.add).then_inc(biased2, 1)
            else:
                v.tensor_copy(lo[:, :, :].rearrange("p t e -> p (t e)"), scored[:, bass.ds(g * TH * E, TH * E)]).then_inc(biased2, 1)
            v.wait_ge(biased2, g + 1)
            v.tensor_reduce(top1[:, :], lo[:, :, :], AX, ALU.max).then_inc(best1, 1)
            v.wait_ge(best1, g + 1)
            v.tensor_tensor(eq[:, :, :], lo[:, :, :], bc(top1), ALU.is_equal).then_inc(is1, 1)
            v.wait_ge(is1, g + 1)
            v.scalar_tensor_tensor(low[:, :, :], eq[:, :, :], -float(E), index[:, :, :], ALU.mult, ALU.add).then_inc(cand1, 1)
            v.wait_ge(cand1, g + 1)
            v.tensor_reduce(first[:, :], low[:, :, :], AX, ALU.min).then_inc(first1, 1)
            v.wait_ge(first1, g + 1)
            v.tensor_tensor(m1[:, :, :], low[:, :, :], bc(first), ALU.is_equal).then_inc(mark1, 1)
            v.wait_ge(mark1, g + 1)
            v.scalar_tensor_tensor(lo[:, :, :], m1[:, :, :], -3.0e38, lo[:, :, :], ALU.mult, ALU.add).then_inc(masked, 1)
            v.wait_ge(masked, g + 1)
            v.tensor_reduce(top2[:, :], lo[:, :, :], AX, ALU.max).then_inc(best2, 1)
            v.wait_ge(best2, g + 1)
            v.tensor_tensor(eq[:, :, :], lo[:, :, :], bc(top2), ALU.is_equal).then_inc(is2, 1)
            v.wait_ge(is2, g + 1)
            v.scalar_tensor_tensor(low[:, :, :], eq[:, :, :], -float(E), index[:, :, :], ALU.mult, ALU.add).then_inc(cand2, 1)
            v.tensor_tensor(top2[:, :], top2[:, :], top1[:, :], ALU.subtract).then_inc(diff, 1)
            v.wait_ge(cand2, g + 1)
            v.tensor_reduce(first[:, :], low[:, :, :], AX, ALU.min).then_inc(first2, 1)
            v.wait_ge(first2, g + 1)
            v.tensor_tensor(m2[:, :, :], low[:, :, :], bc(first), ALU.is_equal).then_inc(mark2, 1)

        def make_gates(g):
            v.wait_ge(exped, g + 1)
            v.tensor_scalar(den[:, :], e2[:, :], 1.0, None, ALU.add).then_inc(summed, 1)
            v.wait_ge(summed, g + 1)
            v.reciprocal(wgt1[:, :], den[:, :]).then_inc(weight1, 1)
            v.wait_ge(weight1, g + 1)
            v.tensor_tensor(wgt2[:, :], e2[:, :], wgt1[:, :], ALU.mult).then_inc(weight2, 1)
            v.tensor_tensor(gate[:, :, :], m1[:, :, :], bc(wgt1), ALU.mult).then_inc(half_gate, 1)
            v.wait_ge(weight2, g + 1)
            v.wait_ge(mark2, g + 1)
            v.tensor_tensor(m2[:, :, :], m2[:, :, :], bc(wgt2), ALU.mult).then_inc(gate2, 1)
            v.wait_ge(half_gate, g + 1)
            v.wait_ge(gate2, g + 1)
            v.tensor_tensor(gate[:, :, :], gate[:, :, :], m2[:, :, :], ALU.add).then_inc(gated, 1)

        def keep_turned(g, k):
            v.wait_ge(turned, g + 1)
            v.tensor_copy(gt[k][:, :], misc[0:2 * E, :]).then_inc(turned_kept, 1)

        def start_sum(g, k):
            v.wait_ge(bias_out, g + 1)
            v.tensor_tensor(acc[k][:, :], misc[:, :], xg[k][:, :], ALU.add).then_inc(bias_kept, 1)

        v.memset(acc[1][:, :], 0.0).then_inc(added, 1)
        for k in range(2):
            v.memset(part[k][:, :], 0.0).then_inc(weighed, 1)
        v.wait_ge(weights_in, 16 * len(loads))
        enter(0, 0)
        if prenorm:
            scale_entry(0)
            tune(0)
            tune(1)
        best_two(0)
        make_gates(0)
        keep_turned(0, 0)
        start_sum(0, 0)
        for first_pair, end_pair, work in runs:
            with v.Fori(first_pair, end_pair) as pair:
                for k in range(2):
                    g = pair * 2 + k
                    for e in range(E):
                        if e == 0:
                            v.wait_ge(bias_kept, g + 1)
                        v.wait_ge(out_made, g * E + e + 1)
                        v.wait_ge(spread_kept, g * E + e + 1)
                        v.tensor_tensor(part[e % 2][:, :], out_ps[e % 2][:, :], spread[e % 4][:, :], ALU.mult).then_inc(weighed, 1)
                        if at["enter"] == e:
                            enter(g + 1, 1 - k)
                        if at["leave_scale"] == e:
                            n_o.vector(v, state(g - 1), g)
                        if at["scale"] == e and prenorm:
                            v.wait_ge(tuned, g * E + E)
                            scale_entry(g + 1)
                        if prenorm:
                            tune((e + 2) % E)
                        v.wait_ge(weighed, g * E + e + 3)
                        if e:
                            v.wait_ge(accumulated, g * (E - 1) + e)
                        ins = v.tensor_tensor(acc[k][:, :], acc[k][:, :], part[e % 2][:, :], ALU.add)
                        ins.then_inc(accumulated if e < E - 1 else added, 1)
                        if at["best"] == e:
                            best_two(g + 1)
                        if at["gate"] == e:
                            make_gates(g + 1)
                        if at["turn_keep"] == e:
                            keep_turned(g + 1, 1 - k)
                        if at["start"] == e:
                            start_sum(g + 1, 1 - k)
                        if work is not None:
                            work(v, g, e)
        n_o.vector(v, state(G - 1), G)

    st.end()


def first_experts(nc, con, X, a):
    def background(sp):
        sp.dma_start(con["route"], a["route"]).then_inc(con["route_in"], 16)
        sp.wait_ge(con["route_in"], 16)
        fetch_experts(sp, con["routed"], con["route"], a["ffn1_experts"], con["routed_in"])

    experts(nc, con, X, a, "ffn0", 8, 2, ACT.Gelu, prenorm=True, background=background,
            spare_work=lambda st: [(0, 1, sift_edges(con)(st)), (1, G // 2, gather_edges(con, EARLY, G // 2, 0)(st))])


def third_experts(nc, con, X, a):
    experts(nc, con, X, a, "ffn2", 8, 1, ACT.Relu,
            spare_work=lambda st: [(0, G // 2, gather_edges(con, LATE, 0, G // 2 * sum(EARLY))(st))])


def second_attention(nc, con, X, a):
    st = Stage(nc, "att1")
    wq, wkv, wm = st.sb("wq", [P, P]), st.sb("wkv", [P, 2 * P]), st.sb("wm", [P, P])
    w1x, w1m, w2 = st.sb("w1x", [P, 2, P]), st.sb("w1m", [P, 2, P]), st.sb("w2", [P, 2, P])
    gb = st.sb("gb", [P, 4])
    heads = st.sb("heads", [P, GB, D])
    xg, sq, std, qn, qe, qs = [st.sb(n, [P, GC]) for n in ("xg", "sq", "std", "qn", "qe", "qs")]
    kn, ke, ks = [st.sb(n, [P, TJ, 2, D]) for n in ("kn", "ke", "ks")]
    vo = st.sb("vo", [P, TJ, 2, 2 * D])
    num_w, den_w = st.sb("num_w", [P, GB, P]), st.sb("den_w", [P, GB, P])
    den, msg, merged, m1, relu, mlp, m2, hs = [st.sb(n, [P, 2, GC] if n == "relu" else [P, GC]) for n in
                                               ("den", "msg", "merged", "m1", "relu", "mlp", "m2", "hs")]
    q_ps, cp = st.ps("q_ps", [P, GC]), st.ps("cp", [P, GC])
    wide_ps = st.ps("wide_ps", [P, 4 * GC])
    kv_ps = wide_ps[:, 0:2 * GC].rearrange("p (a j w h d) -> p a j w h d", a=2, j=TJ // 2, w=2, h=2)
    sum_ps = wide_ps[:, :].rearrange("p (b j h d) -> p b j h d", b=2, j=TJ, h=2)
    num_ps, den_ps = st.ps("num_ps", [P, GC]), st.ps("den_ps", [P, GC])
    weights_in, ones_set, zero1, zero2, grouped, q_made, kv_made, q_low, q_exp, q_kept = st.sems(
        "weights_in ones_set zero1 zero2 grouped q_made kv_made q_low q_exp q_kept")
    k_low, k_exp, k_kept, v_kept, summed, num_kept, den_kept, num_made, den_made = st.sems(
        "k_low k_exp k_kept v_kept summed num_kept den_kept num_made den_made")
    guarded, inverted, scaled, messaged, merged_made, merged_kept, tuned1, mlp1, relued, mlp2, mlp_kept, tuned2, added, added2 = st.sems(
        "guarded inverted scaled messaged merged_made merged_kept tuned1 mlp1 relued mlp2 mlp_kept tuned2 added added2")
    n_1 = Norm(st, "n1", con, cp[:, :], q_ps[:, :], sq[:, :], std[:, :])
    n_2 = Norm(st, "n2", con, cp[:, :], q_ps[:, :], sq[:, :], std[:, :])
    n_o = Norm(st, "no", con, cp[:, :], q_ps[:, :], sq[:, :], std[:, :])
    loads = [(wq[:, :], "wq"), (wkv[:, :], "wkv"), (wm[:, :], "wm"), (w1x[:, :, :], "w1x"), (w1m[:, :, :], "w1m"),
             (w2[:, :, :], "w2"), (gb[:, :], "gb"), (heads[:, :, :], "heads")]
    block = st.ctx.enter_context(nc.Block())

    @block.sync
    def _(sp):
        for dst, src in loads:
            sp.dma_start(dst, a[f"att1_{src}"]).then_inc(weights_in, 16)

    @block.gpsimd
    def _(pool):
        pool.memset(vo[:, :, :, D:2 * D], 1.0).then_inc(ones_set, 1)
        pool.memset(num_w[:, :, :], 0.0).then_inc(zero1, 1)
        pool.memset(den_w[:, :, :], 0.0).then_inc(zero2, 1)

    @block.tensor
    def _(pe):
        pe.wait_ge(weights_in, 16 * len(loads))
        pe.wait_ge(ones_set, 1)
        with pe.Fori(0, G) as g:
            pe.wait_ge(grouped, g + 1)
            pe.matmul(q_ps[:, :], wq[:, :], xg[:, :], start=True, stop=True).then_inc(q_made, 1)
            for j in range(TJ):
                mm = pe.matmul(kv_ps[:, j // 2, j % 2, :, :, :].rearrange("p w h d -> p (w h d)"), xg[:, j * P:(j + 1) * P],
                               wkv[:, :], start=True, stop=True)
            mm.then_inc(kv_made, 1)
            pe.wait_ge(k_kept, g + 1)
            pe.wait_ge(v_kept, g + 1)
            for j in range(TJ):
                for b in range(2):
                    r = slice(b * D, (b + 1) * D)
                    mm = pe.matmul(sum_ps[:, b, j, :, :].rearrange("p h d -> p (h d)"), ks[r, j, :, :].rearrange("p h d -> p (h d)"),
                                   vo[r, j, :, :].rearrange("p h d -> p (h d)"), start=True, stop=True)
            mm.then_inc(summed, 1)
            pe.wait_ge(q_kept, g + 1)
            pe.wait_ge(num_kept, 2 * g + 2)
            for b in range(GB):
                mm = pe.matmul(num_ps[:, b * D:(b + 1) * D], num_w[:, b, :], qs[:, b * D:(b + 1) * D], start=True, stop=True)
            mm.then_inc(num_made, 1)
            pe.wait_ge(den_kept, 2 * g + 2)
            for b in range(GB):
                mm = pe.matmul(den_ps[:, b * D:(b + 1) * D], den_w[:, b, :], qs[:, b * D:(b + 1) * D], start=True, stop=True)
            mm.then_inc(den_made, 1)
            pe.wait_ge(messaged, g + 1)
            pe.matmul(q_ps[:, :], wm[:, :], msg[:, :], start=True, stop=True).then_inc(merged_made, 1)
            n_1.tensor_centre(pe, merged[:, :], merged_kept, g)
            n_1.tensor_average(pe, g)
            pe.wait_ge(tuned1, g + 1)
            for h in range(2):
                out = (num_ps, den_ps)[h][:, :]
                pe.matmul(out, w1x[:, h, :], xg[:, :], start=True, stop=False)
                mm = pe.matmul(out, w1m[:, h, :], m1[:, :], start=False, stop=True)
            mm.then_inc(mlp1, 1)
            pe.wait_ge(relued, 2 * g + 2)
            pe.matmul(q_ps[:, :], w2[:, 0, :], relu[:, 0, :], start=True, stop=False)
            pe.matmul(q_ps[:, :], w2[:, 1, :], relu[:, 1, :], start=False, stop=True).then_inc(mlp2, 1)
            n_2.tensor_centre(pe, mlp[:, :], mlp_kept, g)
            n_2.tensor_average(pe, g)
            n_o.tensor_centre(pe, hs[:, :], added2, g)
            n_o.tensor_average(pe, g)

    @block.scalar
    def _(act):
        act.preload_act_table_set(LN_EXP)
        with act.Fori(0, G) as g:
            act.wait_ge(k_low, g + 1)
            act.activation(ke[:, :, :, :], kn[:, :, :, :], ACT.Exp).then_inc(k_exp, 1)
            act.wait_ge(q_low, g + 1)
            act.activation(qe[:, :], qn[:, :], ACT.Exp).then_inc(q_exp, 1)
            act.wait_ge(k_kept, g + 1)
            for half in range(2):
                ins = act.activation(vo[:, 2 * half:2 * half + 2, :, 0:D], kv_ps[:, half, :, 1, :, :], ACT.Copy, scale=1.0 / T)
            ins.then_inc(v_kept, 1)
            act.wait_ge(merged_made, g + 1)
            act.activation(merged[:, :], q_ps[:, :], ACT.Copy).then_inc(merged_kept, 1)
            n_1.scalar(act, g)
            act.wait_ge(mlp1, g + 1)
            for h in range(2):
                act.activation(relu[:, h, :], (num_ps, den_ps)[h][:, :], ACT.Relu).then_inc(relued, 1)
            act.wait_ge(mlp2, g + 1)
            act.activation(mlp[:, :], q_ps[:, :], ACT.Copy).then_inc(mlp_kept, 1)
            n_2.scalar(act, g)
            n_o.scalar(act, g)

    @block.vector
    def _(v):
        v.wait_ge(weights_in, 16 * len(loads))
        v.wait_ge(zero1, 1)
        v.wait_ge(zero2, 1)
        with v.Fori(0, G) as g:
            v.tensor_copy(xg[:, :], group(X, g)).then_inc(grouped, 1)
            v.wait_ge(kv_made, g + 1)
            for half in range(2):
                ins = v.tensor_scalar(kn[:, 2 * half:2 * half + 2, :, :], kv_ps[:, half, :, 0, :, :], 0.0, None, ALU.min)
            ins.then_inc(k_low, 1)
            v.tensor_scalar(qn[:, :], q_ps[:, :], 0.0, None, ALU.min).then_inc(q_low, 1)
            v.wait_ge(k_exp, g + 1)
            for half in range(2):
                flat = lambda t: t[:, 2 * half:2 * half + 2, :, :].rearrange("p j h d -> p j (h d)")
                ins = v.scalar_tensor_tensor(flat(ks), kv_ps[:, half, :, 0, :, :].rearrange("p j h d -> p j (h d)"), 0.0,
                                             flat(ke), ALU.max, ALU.add)
            ins.then_inc(k_kept, 1)
            v.wait_ge(q_exp, g + 1)
            v.scalar_tensor_tensor(qs[:, :], q_ps[:, :], 0.0, qe[:, :], ALU.max, ALU.add).then_inc(q_kept, 1)
            v.wait_ge(summed, g + 1)
            for kept, w, o in ((num_kept, num_w, 0), (den_kept, den_w, D)):
                for h in range(2):
                    r = slice(h * D, (h + 1) * D)
                    for b in range(2):
                        ins = v.tensor_tensor(w[r, b::2, r], sum_ps[r, b, :, h, o:o + D], heads[r, 0:TJ, :], ALU.mult)
                    ins.then_inc(kept, 1)
            v.wait_ge(den_made, g + 1)
            v.tensor_scalar(den[:, :], den_ps[:, :], 1e-6, None, ALU.add).then_inc(guarded, 1)
            v.wait_ge(guarded, g + 1)
            v.reciprocal(den[:, :], den[:, :]).then_inc(inverted, 1)
            v.wait_ge(inverted, g + 1)
            v.scalar_tensor_tensor(msg[:, :], num_ps[:, :], float(T), den[:, :], ALU.mult, ALU.mult).then_inc(messaged, 1)
            n_1.vector(v, m1[:, :], g)
            v.wait_ge(n_1.normed, g + 1)
            v.tensor_scalar(m1[:, :], m1[:, :], gb[:, 0:1], gb[:, 1:2], ALU.mult, ALU.add).then_inc(tuned1, 1)
            n_2.vector(v, m2[:, :], g)
            v.wait_ge(n_2.normed, g + 1)
            v.tensor_scalar(m2[:, :], m2[:, :], gb[:, 2:3], gb[:, 3:4], ALU.mult, ALU.add).then_inc(tuned2, 1)
            v.wait_ge(tuned2, g + 1)
            v.tensor_tensor(m2[:, :], xg[:, :], m2[:, :], ALU.add).then_inc(added, 1)
            v.wait_ge(added, g + 1)
            v.tensor_tensor(hs[:, :], xg[:, :], m2[:, :], ALU.add).then_inc(added2, 1)
            n_o.vector(v, group(X, g), g)

    st.end()



LAYERS = 2
ROUTED = LAYERS * P + LAYERS


def fetch_experts(sp, routed, route, experts, routed_in):
    with sp.Fori(0, B) as b:
        e = sp.value_load(route[0:1, bass.ds(b, 1)], min_val=0, max_val=15)
        sp.dma_start(routed[:, bass.ds(b * ROUTED, ROUTED)], experts[:, bass.ds(e * ROUTED, ROUTED)]).then_inc(routed_in, 16)


def routed_mlp(nc, con, X, a):
    st = Stage(nc, "ffn1")
    NB = 2 * GB
    RING = 4
    wi, wo = st.sb("wi", [P, 2, P]), st.sb("wo", [P, 2, P])
    bi, bo, bs = st.sb("bi", [P, 1]), st.sb("bo", [P, 1]), st.sb("bs", [P, LAYERS])
    ws = st.sb("ws", [P, LAYERS, P])
    routed, routed_in = con["routed"], con["routed_in"]
    own = [st.sb(f"own{k}", [P, P]) for k in range(RING)]
    xg, sq, std, hs = [st.sb(n, [P, GC]) for n in ("xg", "sq", "std", "hs")]
    hid = [st.sb(f"hid{k}", [P, 2, GC]) for k in range(LAYERS + 1)]
    pre = st.sb("pre", [P, 2, GC])
    hid_ps = [st.ps(f"hid_ps{h}", [P, GC]) for h in range(2)]
    out_ps, cp, vp = st.ps("out_ps", [P, GC]), st.ps("cp", [P, GC]), st.ps("vp", [P, GC])
    weights_in, grouped, entered, copied = st.sems("weights_in grouped entered copied")
    used, residual, biased, layered, left, added = st.sems("used residual biased layered left added")
    n_o = Norm(st, "no", con, cp[:, :], vp[:, :], sq[:, :], std[:, :])
    loads = [(wi[:, :, :], "wi"), (wo[:, :, :], "wo"), (bi[:, :], "bi"), (bo[:, :], "bo"), (bs[:, :], "bs"), (ws[:, :, :], "ws")]
    block = st.ctx.enter_context(nc.Block())

    @block.sync
    def _(sp):
        for dst, src in loads:
            sp.dma_start(dst, a[f"ffn1_{src}"]).then_inc(weights_in, 16)

    @block.tensor
    def _(pe):
        pe.wait_ge(weights_in, 16 * len(loads))
        with pe.Fori(0, G) as g:
            pe.wait_ge(grouped, g + 1)
            for h in range(2):
                mm = pe.matmul(hid_ps[h][:, :], wi[:, h, :], xg[:, :], start=True, stop=True)
            mm.then_inc(entered, 1)
            for l in range(LAYERS):
                pe.wait_ge(layered, g * 2 * (LAYERS + 1) + 2 * l + 2)
                for h in range(2):
                    pe.matmul(hid_ps[h][:, :], ws[:, l, :], hid[l][:, h, :], start=True, stop=False)
                for n in range(NB):
                    h, b = n // GB, n % GB
                    m = l * NB + n
                    pe.wait_ge(copied, g * LAYERS * NB + m + 1)
                    cols = slice(b * T, (b + 1) * T)
                    pe.matmul(hid_ps[h][:, cols], own[m % RING][:, :], hid[l][:, h, cols], start=False,
                              stop=b == GB - 1).then_inc(used, 1)
            pe.wait_ge(layered, (g + 1) * 2 * (LAYERS + 1))
            for h in range(2):
                mm = pe.matmul(out_ps[:, :], wo[:, h, :], hid[LAYERS][:, h, :], start=h == 0, stop=h == 1)
            mm.then_inc(left, 1)
            n_o.tensor_centre(pe, hs[:, :], added, g)
            n_o.tensor_average(pe, g)

    @block.scalar
    def _(act):
        act.wait_ge(weights_in, 16 * len(loads))
        act.wait_ge(routed_in, 16 * B)
        act.preload_act_table_set(LN_EXP)
        with act.Fori(0, G) as g:
            def copy(m):
                l, h, b = m // NB, m % NB // GB, m % GB
                if m >= RING:
                    act.wait_ge(used, g * LAYERS * NB + m - RING + 1)
                src = routed[:, bass.ds(((h * G * GB + b) * ROUTED + l * P) + g * (GB * ROUTED), P)]
                act.activation(own[m % RING][:, :], src, ACT.Copy).then_inc(copied, 1)

            act.wait_ge(entered, g + 1)
            for h in range(2):
                act.activation(hid[0][:, h, :], hid_ps[h][:, :], ACT.Relu, bias=bi[:, 0:1]).then_inc(layered, 1)
            for l in range(LAYERS):
                for n in range(NB):
                    copy(l * NB + n)
                for h in range(2):
                    act.wait_ge(biased, g * 2 * LAYERS + 2 * l + h + 1)
                    act.activation(hid[l + 1][:, h, :], pre[:, h, :], ACT.Relu, bias=bs[:, l:l + 1]).then_inc(layered, 1)
            n_o.scalar(act, g)

    @block.vector
    def _(v):
        v.wait_ge(weights_in, 16 * len(loads))
        v.wait_ge(routed_in, 16 * B)
        with v.Fori(0, G) as g:
            v.tensor_copy(xg[:, :], group(X, g)).then_inc(grouped, 1)
            for l in range(LAYERS):
                for h in range(2):
                    k = g * 2 * LAYERS + 2 * l + h + 1
                    v.wait_ge(used, g * LAYERS * NB + (l * 2 + h + 1) * GB)
                    v.tensor_tensor(pre[:, h, :], hid_ps[h][:, :], hid[l][:, h, :], ALU.add).then_inc(residual, 1)
                    v.wait_ge(residual, k)
                    own_bias = routed[:, bass.ds((h * G * GB * ROUTED) + g * (GB * ROUTED), GB * ROUTED)].rearrange(
                        "p (b c) -> p b c", c=ROUTED)[:, :, LAYERS * P + l:LAYERS * P + l + 1].to_broadcast((P, GB, T))
                    p3 = pre[:, h, :].rearrange("p (b t) -> p b t", t=T)
                    v.tensor_tensor(p3, p3, own_bias, ALU.add).then_inc(biased, 1)
            v.wait_ge(left, g + 1)
            v.scalar_tensor_tensor(hs[:, :], out_ps[:, :], bo[:, 0:1], xg[:, :], ALU.add, ALU.add).then_inc(added, 1)
            n_o.vector(v, group(X, g), g)

    st.end()


def causal_convolution(v, out, x, taps, stepped, base=0):
    o3, x3 = (t[:, :].rearrange("p (b t) -> p b t", t=T) for t in (out, x))
    v.tensor_scalar(out[:, :], x[:, :], taps[:, 0:1], None, ALU.mult).then_inc(stepped, 1)
    for k in range(1, T):
        v.wait_ge(stepped, base + k)
        v.scalar_tensor_tensor(o3[:, :, k:T], x3[:, :, 0:T - k], taps[:, k:k + 1], o3[:, :, k:T],
                               ALU.mult, ALU.add).then_inc(stepped, 1)


def third_attention(nc, con, X, a):
    st = Stage(nc, "att2")
    taps, y = st.sb("taps", [P, T]), st.sb("y", [P, HALF])
    hs, sq, std = [st.sb(n, [P, GC]) for n in ("hs", "sq", "std")]
    cp, vp = st.ps("cp", [P, GC]), st.ps("vp", [P, GC])
    taps_in, stepped, added = st.sems("taps_in stepped added")
    n_o = Norm(st, "no", con, cp[:, :], vp[:, :], sq[:, :], std[:, :])
    block = st.ctx.enter_context(nc.Block())

    @block.sync
    def _(sp):
        sp.dma_start(taps[:, :], a["att2_c"]).then_inc(taps_in, 16)

    @block.tensor
    def _(pe):
        with pe.Fori(0, G) as g:
            n_o.tensor_centre(pe, hs[:, :], added, g)
            n_o.tensor_average(pe, g)

    @block.scalar
    def _(act):
        act.preload_act_table_set(LN_EXP)
        with act.Fori(0, G) as g:
            n_o.scalar(act, g)

    @block.vector
    def _(v):
        v.wait_ge(taps_in, 16)
        causal_convolution(v, y, X, taps, stepped)
        v.wait_ge(stepped, T)
        with v.Fori(0, G) as g:
            v.tensor_tensor(hs[:, :], group(X, g), group(y, g), ALU.add).then_inc(added, 1)
            n_o.vector(v, group(X, g), g)

    st.end()


def fourth_attention(nc, con, X, a):
    st = Stage(nc, "att3")
    DT = 1.0 / T
    wb, wc, wd = st.sb("wb", [P, P]), st.sb("wc", [P, P]), st.sb("wd", [P, P])
    par = st.sb("par", [P, 4])
    rx, rz = st.sb("rx", [P, T]), st.sb("rz", [P, T])
    tx, tz = st.sb("tx", [P, T // 2]), st.sb("tz", [P, T // 2])
    p_, q_, aq, t1, t2 = [st.sb(n, [P, 1]) for n in ("p_", "q_", "aq", "t1", "t2")]
    u, y = st.sb("u", [P, HALF]), st.sb("y", [P, HALF])
    gx, xg, xs, sg, hs, sq, std = [st.sb(n, [P, GC]) for n in ("gx", "xg", "xs", "sg", "hs", "sq", "std")]
    u_ps, o_ps, cp, vp = [st.ps(n, [P, GC]) for n in ("u_ps", "o_ps", "cp", "vp")]
    bcd = st.sb("bcd", [P, 1])
    weights_in, chained, u_made, u_kept, stepped, out_made, xg_kept, gelued, sigmoided = st.sems(
        "weights_in chained u_made u_kept stepped out_made xg_kept gelued sigmoided")
    gated, added, added2, conv_done = st.sems("gated added added2 conv_done")
    n_o = Norm(st, "no", con, cp[:, :], vp[:, :], sq[:, :], std[:, :], True)
    loads = [(wb[:, :], "wb"), (wc[:, :], "wc"), (wd[:, :], "wd"), (par[:, :], "par")]
    block = st.ctx.enter_context(nc.Block())

    @block.sync
    def _(sp):
        for dst, src in loads:
            sp.dma_start(dst, a[f"att3_{src}"]).then_inc(weights_in, 16)

    @block.tensor
    def _(pe):
        pe.wait_ge(weights_in, 16 * len(loads))
        for k in range(G):
            if k:
                pe.wait_ge(u_kept, k)
            pe.matmul(u_ps[:, :], wb[:, :], X[:, k * GC:(k + 1) * GC], start=True, stop=True).then_inc(u_made, 1)
        pe.wait_ge(conv_done, 1)
        with pe.Fori(0, G) as g:
            pe.matmul(o_ps[:, :], wc[:, :], group(y, g), start=True, stop=False)
            pe.matmul(o_ps[:, :], wd[:, :], group(X, g), start=False, stop=True).then_inc(out_made, 1)
            n_o.tensor_centre(pe, hs[:, :], added2, g)
            n_o.tensor_average(pe, g)

    @block.scalar
    def _(act):
        act.wait_ge(weights_in, 16 * len(loads))
        for k in range(G):
            act.wait_ge(u_made, k + 1)
            act.activation(u[:, k * GC:(k + 1) * GC], u_ps[:, :], ACT.Identity, bias=par[:, 1:2]).then_inc(u_kept, 1)
        act.wait_ge(conv_done, 1)
        with act.Fori(0, G) as g:
            act.wait_ge(out_made, g + 1)
            act.activation(gx[:, :], o_ps[:, :], ACT.Gelu, bias=bcd[:, 0:1]).then_inc(gelued, 1)
            act.wait_ge(gelued, g + 1)
            act.activation(sg[:, :], gx[:, :], ACT.Sigmoid).then_inc(sigmoided, 1)
            n_o.scalar(act, g)

    @block.vector
    def _(v):
        v.wait_ge(weights_in, 16 * len(loads))
        count = 0

        def link(ins):
            nonlocal count
            count += 1
            ins.then_inc(chained, 1)
            v.wait_ge(chained, count)

        acol = par[:, 0:1]
        link(v.tensor_tensor(bcd[:, :], par[:, 2:3], par[:, 3:4], ALU.add))
        link(v.tensor_scalar(t1[:, :], acol, DT * DT, 1.0, ALU.mult, ALU.add))
        link(v.reciprocal(p_[:, :], t1[:, :]))
        link(v.tensor_scalar(q_[:, :], p_[:, :], DT, None, ALU.mult))
        link(v.tensor_copy(rx[:, 0:1], q_[:, :]))
        link(v.tensor_scalar(rz[:, 0:1], q_[:, :], DT, None, ALU.mult))
        m = 1
        while m < T:
            link(v.tensor_tensor(aq[:, :], acol, q_[:, :], ALU.mult))
            link(v.tensor_scalar(tx[:, 0:m], rz[:, 0:m], aq[:, 0:1], None, ALU.mult))
            link(v.tensor_scalar(tz[:, 0:m], rz[:, 0:m], p_[:, 0:1], None, ALU.mult))
            link(v.scalar_tensor_tensor(rz[:, m:2 * m], rx[:, 0:m], q_[:, 0:1], tz[:, 0:m], ALU.mult, ALU.add))
            link(v.scalar_tensor_tensor(rx[:, m:2 * m], rx[:, 0:m], p_[:, 0:1], tx[:, 0:m], ALU.mult, ALU.subtract))
            link(v.tensor_tensor(t1[:, :], aq[:, :], q_[:, :], ALU.mult))
            link(v.tensor_scalar(t2[:, :], p_[:, :], q_[:, 0:1], 2.0, ALU.mult, ALU.mult))
            link(v.scalar_tensor_tensor(p_[:, :], p_[:, :], p_[:, 0:1], t1[:, :], ALU.mult, ALU.subtract))
            link(v.tensor_copy(q_[:, :], t2[:, :]))
            m *= 2
        v.wait_ge(u_kept, G)
        causal_convolution(v, y, u, rz, stepped)
        v.wait_ge(stepped, T)
        v.nop().then_inc(conv_done, 1)
        with v.Fori(0, G) as g:
            v.wait_ge(sigmoided, g + 1)
            v.tensor_tensor(xs[:, :], gx[:, :], sg[:, :], ALU.mult).then_inc(gated, 1)
            v.wait_ge(gated, g + 1)
            v.tensor_tensor(xs[:, :], xs[:, :], group(X, g), ALU.add).then_inc(added, 1)
            v.wait_ge(added, g + 1)
            v.tensor_tensor(hs[:, :], xs[:, :], group(X, g), ALU.add).then_inc(added2, 1)
            n_o.vector(v, group(X, g), g)

    st.end()


EDGES = 262144
EW = EDGES // P
CH = 8
CHUNKS = EW // CH
STEPS = 4
EIGHTH = EW // 8
SIFT_ROUNDS = 3
SIFTED = 8 * 2 * SIFT_ROUNDS * 2 * CH
EARLY = (3, 2) * 4
LATE = (1,) * 8
FIXED_ROUNDS = G // 2 * sum(EARLY) + G * sum(LATE)


def sift_edges(con):
    PAIR = 2 * CH

    def work_of(st):
        top, carrier = st.sb("sift_top", [P, PAIR]), st.sb("sift_carrier", [P, PAIR])
        topped, taken, stored = st.sems("sift_topped sift_taken sift_stored")

        def work(v, g, e):
            for j in range(SIFT_ROUNDS):
                want = g * (8 * SIFT_ROUNDS) + e * SIFT_ROUNDS + j + 1
                parts = [con["left"][:, q * EIGHTH:(q + 1) * EIGHTH] for q in (e, (e + 4) % 8)]
                for w, part in enumerate(parts):
                    ins = v.max(top[:, w * CH:(w + 1) * CH], part)
                ins.then_inc(topped, 1)
                v.wait_ge(topped, want)
                v.tensor_copy(carrier[:, :], top[:, :])
                for w, part in enumerate(parts):
                    ins = v.match_replace(part, top[:, w * CH:(w + 1) * CH], part, 0.0)
                ins.then_inc(taken, 1)
                v.tensor_copy(con["left"][:, bass.ds(g * (8 * SIFT_ROUNDS * PAIR) + (EW + (e * SIFT_ROUNDS + j) * PAIR), PAIR)],
                              top[:, :]).then_inc(stored, 1)
                v.wait_ge(taken, want)
                v.wait_ge(stored, want)
                v.memset(carrier[:, 0:1], 0.0)

        return work

    return work_of


def gather_edges(con, rounds, first_group, done):
    def work_of(st):
        top, carrier = st.sb("take_top", [P, CH]), st.sb("take_carrier", [P, CH])
        topped, taken, stored = st.sems("take_topped take_taken take_stored")
        sifted = con["left"][:, EW:EW + SIFTED]

        def work(v, g, e):
            for j in range(rounds[e]):
                n = g * sum(rounds) + (sum(rounds[:e]) + j - first_group * sum(rounds))
                v.max(top[:, :], sifted).then_inc(topped, 1)
                v.wait_ge(topped, n + 1)
                v.tensor_copy(carrier[:, :], top[:, :])
                v.match_replace(sifted, top[:, :], sifted, 0.0).then_inc(taken, 1)
                v.tensor_copy(con["keys"][:, bass.ds(n * CH + done * CH, CH)], top[:, :]).then_inc(stored, 1)
                v.wait_ge(taken, n + 1)
                v.wait_ge(stored, n + 1)
                v.memset(carrier[:, 0:1], 0.0)

        return work

    return work_of


def order_edges(nc, con, X, a):
    st = Stage(nc, "edges")
    FRONT = FIXED_ROUNDS * CH
    inside = st.sb("inside", [P, EW + SIFTED])
    top, spare = st.sb("top", [P, CH]), st.sb("spare", [P, CH])
    most, most_i, number = st.sb("most", [P, 2]), st.sb("most_i", [P, 2], I32), st.sb("number", [P, 2])
    chained, counted, maxed = st.sems("chained counted maxed")
    topped, taken, stored = st.sems("topped taken stored")
    left = con["left"]
    block = st.ctx.enter_context(nc.Block())

    @block.gpsimd
    def _(pool):
        pool.wait_ge(counted, 1)
        pool.partition_all_reduce(most[:, :], number[:, :], P, bass.bass_isa.ReduceOp.max).then_inc(maxed, 1)

    @block.vector
    def _(v):
        count = 0

        def link(ins):
            nonlocal count
            count += 1
            ins.then_inc(chained, 1)
            v.wait_ge(chained, count)

        link(v.tensor_scalar(inside[:, :], left, 0.0, None, ALU.is_gt))
        link(v.tensor_reduce(number[:, 1:2], inside[:, :], AX, ALU.add))
        link(v.tensor_scalar(number[:, 0:1], number[:, 1:2], 1.0, float(FRONT), ALU.min, ALU.mult))
        link(v.tensor_tensor(number[:, 0:1], number[:, 0:1], number[:, 1:2], ALU.add))
        link(v.tensor_tensor(spare[:, 0:1], con["edge_count"], number[:, 1:2], ALU.subtract))
        v.tensor_tensor(number[:, 0:1], number[:, 0:1], spare[:, 0:1], ALU.max).then_inc(counted, 1)
        v.wait_ge(maxed, 1)
        link(v.tensor_copy(most_i[:, :], most[:, :]))
        link(v.tensor_copy(con["most"], most_i[:, 0:1]))
        n = v.value_load(most_i[0:1, 1:2], min_val=0, max_val=EW)
        with v.If(n > 0):
            with v.Fori(0, (CHUNKS - FIXED_ROUNDS) // STEPS) as k:
                with v.If(n > k * (CH * STEPS)):
                    for j in range(STEPS):
                        v.max(top[:, :], left).then_inc(topped, 1)
                        v.wait_ge(topped, k * STEPS + j + 1)
                        v.tensor_copy(spare[:, :], top[:, :])
                        v.match_replace(left, top[:, :], left, 0.0).then_inc(taken, 1)
                        v.tensor_copy(con["keys"][:, bass.ds(k * (CH * STEPS) + (j * CH + FRONT), CH)], top[:, :]).then_inc(stored, 1)
                        v.wait_ge(taken, k * STEPS + j + 1)
                        v.wait_ge(stored, k * STEPS + j + 1)
                        v.memset(spare[:, 0:1], 0.0)

    st.end()


HEADS, GE = 4, 4
GF = HEADS * GE
NF = GF + HEADS
HI = TOK // P
AHEAD = 4
RUN = 8


def graph_attention(nc, con, X, a):
    st = Stage(nc, "gat")
    TILES = HALF // P
    BF16 = mybir.dt.bfloat16
    rows_dram = nc.dram_tensor("gat_rows", (TOK, NF), F32, kind="Internal").ap()
    wg = st.sb("wg", [P, 2 * GF])
    att = st.sb("att", [P, 2, HI, GF])
    norm_par = st.sb("norm_par", [P, 3, HI, GF])
    iota = st.sb("iota", [P, P])
    rowt = st.sb("rowt", [P, HI, NF])
    prod = st.sb("prod", [P, 2, HI, GF])
    ad, shift, selfw = [st.sb(n, [P, HI, HEADS]) for n in ("ad", "shift", "selfw")]
    amax1, amax = st.sb("amax1", [P, HEADS]), st.sb("amax", [P, HEADS])
    rest = st.sb("rest", [P, 2, HI, HEADS])
    adp = st.sb("adp", [P, 3, HI * HEADS], BF16)
    words = [st.sb(f"words{k}", [P, EW + CH * AHEAD], I32) for k in range(2)]
    srci = st.sb("srci", [P, EW + CH * AHEAD], U32)
    low, high = st.sb("low", [P, EW + CH * AHEAD]), st.sb("high", [P, EW + CH * AHEAD])
    index = [st.sb(f"index{k}", [P, CH], U32) for k in range(AHEAD)]
    rows = [st.sb(f"rows{k}", [P, CH, NF]) for k in range(AHEAD)]
    oh_low = [st.sb(f"oh_low{k}", [P, CH, P]) for k in range(AHEAD)]
    oh_high = [st.sb(f"oh_high{k}", [P, CH, HI]) for k in range(AHEAD)]
    turned_b = st.sb("turned_b", [P, CH * P], BF16)
    picked = st.sb("picked", [P, CH, HI, HEADS])
    ade, edge, bound = [st.sb(n, [P, CH, HEADS]) for n in ("ade", "edge", "bound")]
    value = [st.sb(f"value{k}", [P, CH, NF]) for k in range(AHEAD)]
    spread = [st.sb(f"spread{k}", [P, CH, HI, NF]) for k in range(2)]
    zeros, spare = st.sb("zeros", [P, GC]), st.sb("spare", [P, 2])
    std_t = st.sb("std", [P, HI])
    std = std_t[:, :]
    feat_ps = st.ps("feat_ps", [P, TILES, 2, GF])
    turn_ps = st.ps("turn_ps", [P, CH * P])
    gat_ps = st.ps("gat_ps", [P, CH, HI * HEADS])
    sum_ps = st.ps("sum_ps", [P, 2, GC])
    HB = HI // 2
    weights_in, chained, featured, tables, maxed, self_ready, self_done, rows_out, zero_set, started = st.sems(
        "weights_in chained featured tables maxed self_ready self_done rows_out zero_set started")
    staged, onehot, turned, turned_kept, target_out, target_read = st.sems(
        "staged onehot turned turned_kept target_out target_read")
    scored, weighted, valued, spreaded, scattered, prepared, picked1, reduced, step1, step2, step3, step4, all_done = st.sems(
        "scored weighted valued spreaded scattered prepared picked1 reduced step1 step2 step3 step4 all_done")
    rooted, rooted_in, carried = st.sems("rooted rooted_in carried")
    gathered = [st.sem(f"gathered{k}") for k in range(AHEAD)]
    loads = [(wg[:, :], "wg"), (att[:, :, :, :], "att"), (norm_par[:, :, :, :], "norm"), (iota[:, :], "iota")]
    block = st.ctx.enter_context(nc.Block())

    def chunks(eng, body):
        n = eng.value_load(con["most"][0:1, 0:1], min_val=0, max_val=EW)
        with eng.Fori(0, CHUNKS // AHEAD // RUN) as o:
            with eng.If(n > o * (RUN * AHEAD * CH)):
                with eng.Fori(0, RUN) as i:
                    with eng.If(n > o * (RUN * AHEAD * CH) + i * (AHEAD * CH)):
                        for k in range(AHEAD):
                            body(o * (RUN * AHEAD) + i * AHEAD + k, k, o * RUN + i)
        return n

    @block.sync
    def _(sp):
        for dst, src in loads:
            sp.dma_start(dst, a[f"gat_{src}"]).then_inc(weights_in, 16)
        sp.wait_ge(tables, 1)
        sp.dma_start(rows_dram.rearrange("(h p) f -> p h f", p=P), rowt[:, :, :]).then_inc(rows_out, 16)
        sp.wait_ge(rows_out, 16)

    @block.gpsimd
    def _(pool):
        pool.memset(spare[:, :], 0.0).then_inc(carried, 1)
        pool.wait_ge(carried, 1)
        pool.wait_ge(maxed, 1)
        pool.partition_all_reduce(amax[:, :], amax1[:, :], P, bass.bass_isa.ReduceOp.max).then_inc(maxed, 1)
        pool.wait_ge(rows_out, 16)

        def gather(want, k):
            pool.wait_ge(staged, want)
            pool.wait_ge(carried, want)
            pool.tensor_tensor(spare[:, 1:2], spare[:, 0:1], spare[:, 0:1], ALU.add).then_inc(carried, 1)
            for t in range(CH):
                pool.indirect_dma_start(rows[k][:, t, :], None, rows_dram,
                                        bass.IndirectOffsetOnAxis(ap=index[k][:, t:t + 1], axis=0)).then_inc(gathered[k], 16)

        for c in range(AHEAD):
            gather(c + 1, c)
        chunks(pool, lambda c, k, i: gather(c + AHEAD + 1, k))

    @block.tensor
    def _(pe):
        pe.wait_ge(weights_in, 16 * len(loads))
        for n in range(TILES):
            mm = pe.matmul(feat_ps[:, n, :, :].rearrange("p h f -> p (h f)"), X[:, n * P:(n + 1) * P], wg[:, :], start=True, stop=True)
        mm.then_inc(featured, 1)
        pe.wait_ge(zero_set, 1)
        for w in range(2):
            pe.matmul(sum_ps[:, w, :], zeros[:, 0:P], zeros[:, :], start=True, stop=False,
                      skip_group_check=True).then_inc(scattered, 1)

        def turn(want, k):
            pe.wait_ge(onehot, want)
            for t in range(CH):
                mm = pe.transpose(turn_ps[:, t * P:(t + 1) * P], oh_low[k][:, t, :], con["ident"])
            mm.then_inc(turned, 1)

        def targets(want, k):
            pe.wait_ge(turned_kept, want)
            for t in range(CH):
                for part in range(3):
                    mm = pe.matmul(gat_ps[:, t, :], turned_b[:, t * P:(t + 1) * P], adp[:, part, :], start=part == 0, stop=part == 2)
            mm.then_inc(target_out, 1)

        pe.wait_ge(prepared, 1)
        turn(1, 0)
        targets(1, 0)

        def chunk(c, k, i):
            turn(c + 2, (k + 1) % AHEAD)
            for t in range(CH):
                pe.wait_ge(spreaded, c * CH + t + 1)
                for w in range(2):
                    mm = pe.matmul(sum_ps[:, w, 0:HB * NF], oh_low[k][:, t, :],
                                   spread[k % 2][:, t, w * HB:(w + 1) * HB, :].rearrange("p h f -> p (h f)"),
                                   start=False, stop=False, skip_group_check=True)
                if t == 1:
                    pe.wait_ge(target_read, c + 1)
                    targets(c + 2, (k + 1) % AHEAD)
            mm.then_inc(scattered, 1)

        chunks(pe, chunk)
        for w in range(2):
            mm = pe.matmul(sum_ps[:, w, :], zeros[:, 0:P], zeros[:, :], start=False, stop=True, skip_group_check=True)
        mm.then_inc(all_done, 1)

    @block.scalar
    def _(act):
        act.wait_ge(prepared, 1)

        def stage(c, k):
            act.activation(index[k][:, :], srci[:, bass.ds(c * CH, CH)], ACT.Copy).then_inc(staged, 1)

        for c in range(AHEAD):
            stage(c, c)
        act.wait_ge(self_ready, 1)
        act.activation(selfw[:, :, :], selfw[:, :, :], ACT.Exp).then_inc(self_done, 1)

        def turned_copy(want):
            act.wait_ge(turned, want)
            act.activation(turned_b[:, :], turn_ps[:, :], ACT.Copy).then_inc(turned_kept, 1)

        turned_copy(1)

        def chunk(c, k, i):
            act.wait_ge(scored, c + 1)
            act.activation(value[k][:, :, GF:NF], edge[:, :, :], ACT.Exp).then_inc(weighted, 1)
            act.wait_ge(target_out, c + 1)
            turned_copy(c + 2)
            act.wait_ge(valued, c + 1)
            stage(c + AHEAD, k)

        chunks(act, chunk)
        act.wait_ge(rooted_in, 1)
        act.activation(std, std,
                       ACT.Sqrt, bias=con["eps"]).then_inc(rooted, 1)

    @block.vector
    def _(v):
        count = 0

        def link(ins):
            nonlocal count
            count += 1
            ins.then_inc(chained, 1)
            v.wait_ge(chained, count)

        f2 = lambda t: t.rearrange("p h f -> p (h f)")
        v.memset(zeros[:, :], 0.0).then_inc(zero_set, 1)
        for w in words:
            link(v.memset(w[:, EW:EW + CH * AHEAD], -1))
        link(v.tensor_scalar(words[0][:, 0:EW], con["keys"], -1.0, None, ALU.add))
        link(v.tensor_scalar(words[1][:, :], words[0][:, :], TOK - 1, None, ALU.bitwise_and))
        link(v.tensor_copy(srci[:, :], words[1][:, :]))
        link(v.tensor_scalar(words[1][:, :], words[0][:, :], 12, P - 1, ALU.logical_shift_right, ALU.bitwise_and))
        link(v.tensor_copy(low[:, :], words[1][:, :]))
        link(v.tensor_scalar(words[1][:, :], words[0][:, :], 19, None, ALU.arith_shift_right))
        link(v.tensor_copy(high[:, :], words[1][:, :]))
        v.wait_ge(weights_in, 16 * len(loads))
        v.wait_ge(featured, 1)
        feats = rowt[:, :, HEADS:NF]
        for h in range(2):
            link(v.tensor_copy(feats[:, h * TILES:(h + 1) * TILES, :], feat_ps[:, :, h, :]))
        for w, dst in ((0, rowt[:, :, 0:HEADS]), (1, ad[:, :, :])):
            link(v.tensor_tensor(prod[:, w, :, :], feats, att[:, w, :, :], ALU.mult))
            link(v.tensor_reduce(dst, prod[:, w, :, :].rearrange("p n (h x) -> p n h x", x=GE), AX, ALU.add))
        v.nop().then_inc(tables, 1)
        v.tensor_reduce(amax1[:, :], rowt[:, :, 0:HEADS].rearrange("p n h -> p h n"), AX, ALU.max).then_inc(maxed, 1)
        link(v.tensor_copy(adp[:, 0, :], f2(ad[:, :, :])))
        link(v.tensor_tensor(f2(rest[:, 0, :, :]), f2(ad[:, :, :]), adp[:, 0, :], ALU.subtract))
        link(v.tensor_copy(adp[:, 1, :], f2(rest[:, 0, :, :])))
        link(v.tensor_tensor(f2(rest[:, 1, :, :]), f2(rest[:, 0, :, :]), adp[:, 1, :], ALU.subtract))
        link(v.tensor_copy(adp[:, 2, :], f2(rest[:, 1, :, :])))
        v.nop().then_inc(prepared, 1)

        def leaky(dst, src):
            return v.scalar_tensor_tensor(dst, src, 0.2, src, ALU.mult, ALU.max)

        v.wait_ge(maxed, 2)
        link(v.tensor_tensor(shift[:, :, :], ad[:, :, :], amax[:, None, :].to_broadcast((P, HI, HEADS)), ALU.add))
        link(leaky(shift[:, :, :], shift[:, :, :]))
        link(v.tensor_tensor(selfw[:, :, :], rowt[:, :, 0:HEADS], ad[:, :, :], ALU.add))
        link(leaky(selfw[:, :, :], selfw[:, :, :]))
        v.tensor_tensor(selfw[:, :, :], selfw[:, :, :], shift[:, :, :], ALU.subtract).then_inc(self_ready, 1)

        def high_hot(c, k):
            return v.tensor_tensor(oh_high[k][:, :, :], high[:, bass.ds(c * CH, CH)][:, :, None].to_broadcast((P, CH, HI)),
                                   iota[:, None, 0:HI].to_broadcast((P, CH, HI)), ALU.is_equal)

        def low_hot(c, k):
            v.tensor_tensor(oh_low[k][:, :, :], low[:, bass.ds(c * CH, CH)][:, :, None].to_broadcast((P, CH, P)),
                            iota[:, None, :].to_broadcast((P, CH, P)), ALU.is_equal).then_inc(onehot, 1)

        high_hot(0, 0)
        low_hot(0, 0)

        def chunk(c, k, i):
            v.wait_ge(target_out, c + 1)
            v.tensor_tensor(picked[:, :, :, :], gat_ps[:, :, :].rearrange("p c (h x) -> p c h x", x=HEADS),
                            oh_high[k][:, :, :, None].to_broadcast((P, CH, HI, HEADS)), ALU.mult).then_inc(target_read, 1)
            high_hot(c + 1, (k + 1) % AHEAD)
            v.wait_ge(target_read, c + 1)
            v.tensor_reduce(ade[:, :, :], picked[:, :, :, :].rearrange("p c h x -> p c x h"), AX, ALU.add).then_inc(reduced, 1)
            v.wait_ge(gathered[k], (i + 1) * (16 * CH))
            v.wait_ge(reduced, c + 1)
            v.tensor_tensor(edge[:, :, :], rows[k][:, :, 0:HEADS], ade[:, :, :], ALU.add).then_inc(step1, 1)
            v.tensor_tensor(bound[:, :, :], ade[:, :, :], amax[:, None, :].to_broadcast((P, CH, HEADS)), ALU.add).then_inc(step2, 1)
            v.wait_ge(step1, c + 1)
            leaky(edge[:, :, :], edge[:, :, :]).then_inc(step3, 1)
            v.wait_ge(step2, c + 1)
            leaky(bound[:, :, :], bound[:, :, :]).then_inc(step4, 1)
            v.wait_ge(step3, c + 1)
            v.wait_ge(step4, c + 1)
            v.tensor_tensor(edge[:, :, :], edge[:, :, :], bound[:, :, :], ALU.subtract).then_inc(scored, 1)
            low_hot(c + 1, (k + 1) % AHEAD)
            v.wait_ge(weighted, c + 1)
            v.tensor_tensor(value[k][:, :, 0:GF].rearrange("p c (h x) -> p c h x", x=GE),
                            rows[k][:, :, HEADS:NF].rearrange("p c (h x) -> p c h x", x=GE),
                            value[k][:, :, GF:NF][:, :, :, None].to_broadcast((P, CH, HEADS, GE)), ALU.mult).then_inc(valued, 1)
            v.wait_ge(valued, c + 1)
            v.wait_ge(scattered, c + 1)
            for t in range(CH):
                v.tensor_tensor(spread[k % 2][:, t, :, :], oh_high[k][:, t, :, None].to_broadcast((P, HI, NF)),
                                value[k][:, t, None, :].to_broadcast((P, HI, NF)), ALU.mult).then_inc(spreaded, 1)

        n = chunks(v, chunk)
        v.wait_ge(all_done, 1)
        v.wait_ge(self_done, 1)
        for k in range(AHEAD):
            v.wait_ge(gathered[k], ((n + (AHEAD * CH - 1)) // (AHEAD * CH)) * (16 * CH) + 16 * CH)
        msg, den = prod[:, 0, :, :], shift[:, :, :]
        sums = lambda w: sum_ps[:, w, 0:HB * NF].rearrange("p (h f) -> p h f", f=NF)
        link(v.tensor_tensor(msg.rearrange("p n (h x) -> p n h x", x=GE), feats.rearrange("p n (h x) -> p n h x", x=GE),
                             selfw[:, :, :, None].to_broadcast((P, HI, HEADS, GE)), ALU.mult))
        for w in range(2):
            part = slice(w * HB, (w + 1) * HB)
            link(v.tensor_tensor(msg[:, part, :], msg[:, part, :], sums(w)[:, :, 0:GF], ALU.add))
            link(v.tensor_tensor(den[:, part, :], selfw[:, part, :], sums(w)[:, :, GF:NF], ALU.add))
        link(v.tensor_scalar(den, den, 1e-16, None, ALU.add))
        link(v.reciprocal(den, den))
        link(v.tensor_tensor(msg.rearrange("p n (h x) -> p n h x", x=GE), msg.rearrange("p n (h x) -> p n h x", x=GE),
                             den[:, :, :, None].to_broadcast((P, HI, HEADS, GE)), ALU.mult))
        link(v.tensor_tensor(msg, msg, norm_par[:, 0, :, :], ALU.add))
        mean, cen = ad[:, :, 0], prod[:, 1, :, :]
        link(v.tensor_reduce(mean, msg, AX, ALU.add))
        link(v.tensor_scalar(mean, mean, 1.0 / GF, None, ALU.mult))
        bc = lambda t: t[:, :, None].to_broadcast((P, HI, GF))
        link(v.tensor_tensor(cen, msg, bc(mean), ALU.subtract))
        link(v.tensor_tensor(msg, cen, cen, ALU.mult))
        link(v.tensor_reduce(std, msg, AX, ALU.add))
        v.tensor_scalar(std, std, 1.0 / GF, None, ALU.mult).then_inc(rooted_in, 1)
        v.wait_ge(rooted, 1)
        link(v.reciprocal(std, std))
        link(v.tensor_tensor(cen, cen, bc(std), ALU.mult))
        link(v.tensor_tensor(cen, cen, norm_par[:, 1, :, :], ALU.mult))
        link(v.tensor_tensor(cen, cen, norm_par[:, 2, :, :], ALU.add))
        link(v.tensor_reduce(ad[:, :, :], cen.rearrange("p n (h x) -> p n x h", x=GE), AX, ALU.add))
        for h in range(2):
            link(v.tensor_scalar(con["scores"][:, 0:HI * GE].rearrange("p (j h x) -> p h j x", h=2, x=GE)[:, h], ad[:, h * TILES:(h + 1) * TILES, :],
                                 1.0 / HEADS, None, ALU.mult))

    st.end()


def fourth_experts(nc, con, X, a):
    experts(nc, con, X, a, "ffn3", 4, 1, ACT.Gelu, scored=con["scores"])



def build(nc, a, out):
    with ExitStack() as ctx:
        padded = ctx.enter_context(nc.sbuf_tensor("X", [P, GC + HALF + GC], F32))
        X = padded[:, GC:GC + HALF]
        consts = ctx.enter_context(nc.sbuf_tensor("consts", [P, 5 * P + 8], F32))
        con = {"consts": consts[:, :], "padded": padded}
        for n, name in enumerate(("ident", "centre", "average", "mean128", "ones")):
            con[name] = consts[:, n * P:(n + 1) * P]
        con["eps"] = consts[:, 5 * P:5 * P + 1]
        keys = ctx.enter_context(nc.sbuf_tensor("keys", [P, EW], F32))
        most = ctx.enter_context(nc.sbuf_tensor("most", [P, 1], I32))
        scores = ctx.enter_context(nc.sbuf_tensor("scores", [P, HI * GE + 2 * TJ * GE], F32))
        con["scores"] = scores[:, :]
        con["keys"], con["most"] = keys[:, :], most[:, :]
        left = ctx.enter_context(nc.sbuf_tensor("left", [P, EW + SIFTED], F32))
        edge_count = ctx.enter_context(nc.sbuf_tensor("edge_count", [P, 1], F32))
        con["left"], con["edge_count"] = left[:, :], edge_count[:, :]
        early = Stage(nc, "routed")
        con["routed"], con["route"] = early.sb("experts", [P, B * ROUTED])[:, :], early.sb("route", [1, B], I32)[:, :]
        con["routed_in"], con["route_in"] = early.sems("experts_in route_in")
        tokenizer(nc, con, X, a)
        stages = STAGE_LIST()
        for n, stage in enumerate(stages):
            if n < STAGES:
                stage(nc, con, X, a)
            if stage is routed_mlp:
                early.end()
        finish(nc, con, X, out)


def STAGE_LIST():
    return [first_attention, first_experts, second_attention, routed_mlp,
            third_attention, third_experts, fourth_attention,
            order_edges, graph_attention, fourth_experts]


def constants(np):
    eye = np.eye(P, dtype=np.float32)
    half = np.kron(np.eye(2), np.ones((D, D))).astype(np.float32) / D
    t = np.arange(P)
    s, u = t[:, None], t[None, :]
    decay = np.where((s // T == u // T) & (s < u), 0.97 ** np.maximum(u - s - 1.0, 0), 0).astype(np.float32)
    tail = np.zeros((P, 8), np.float32)
    tail[:, 0] = EPS
    return {
        "consts": np.concatenate([eye, eye - half, half, np.full((P, P), 1 / P, np.float32), np.ones((P, P), np.float32), tail], 1),
        "decay": np.tile(decay, (1, TJ)),
        "later": np.tile((np.arange(2 * GC) % T != 0).astype(np.float32), (P, 1)),
    }


def kernel(**inputs):
    import numpy as np
    import concourse.bacc as bacc
    from concourse.bass_utils import run_bass_kernel_spmd

    i = {k: np.asarray(v) for k, v in inputs.items()}

    def rows(w):
        z = np.zeros((P, 2) + w.shape[1:], w.dtype)
        z[:D, 0], z[D:, 1] = w, w
        return z

    def cols(w):
        z = np.zeros((w.shape[0], 2, P), w.dtype)
        z[:, 0, :D], z[:, 1, D:] = w, w
        return z

    def both(w):
        n = w.shape[1]
        z = np.zeros((P, 2 * n), w.dtype)
        z[:D, :n], z[D:, n:] = w, w
        return z

    def twice(w):
        return np.concatenate([w, w], 0)

    arrays = constants(np)
    arrays["x"] = i["x"].reshape(TOK, D * 4)
    arrays["tok"] = np.concatenate([i["L0_tok_W"], i["L0_tok_b"][:, None]], 1)
    arrays["dx"] = rows(i["L0_attn_Dx"].T)
    arrays["dy"] = rows(i["L0_attn_Dy"].T)
    e = cols(i["L0_attn_E"].T).reshape(2, P, 2, P)
    arrays["et"] = e.transpose(1, 2, 0, 3)
    def moe(name, w1, b1, w2, b2, wr=None, biases=()):
        E, _, hidden = w1.shape
        hc = hidden // P
        arrays[f"{name}_w1"] = rows(w1.transpose(1, 0, 2))
        arrays[f"{name}_w2"] = cols(w2.reshape(E * hidden, D)).reshape(E, hc, P, 2, P).transpose(2, 0, 1, 3, 4)
        arrays[f"{name}_b1"] = b1.reshape(E, hc, P).transpose(2, 0, 1)
        z = np.zeros((2, E, P), np.float32)
        z[0, :, :D], z[1, :, D:] = b2, b2
        arrays[f"{name}_b2"] = z.reshape(2 * E, P)
        if wr is not None:
            arrays[f"{name}_wr"] = both(wr)
            biases = list(biases) + [np.zeros(E, np.float32)] * (2 - len(biases))
            arrays[f"{name}_br"] = np.broadcast_to(np.stack(biases)[None, :, None], (P, 2, 2 * TJ, E))

    moe("ffn0", i["L0_ffn_W1"], i["L0_ffn_b1"], i["L0_ffn_W2"], i["L0_ffn_b2"], i["L0_ffn_Wr"], [i["L0_ffn_br"]])
    arrays["ffn0_scale"], arrays["ffn0_shift"] = twice(i["L0_ffn_ln_g"].T), twice(i["L0_ffn_ln_b"].T)
    moe("ffn2", i["L2_ffn_W1"], i["L2_ffn_b1"], i["L2_ffn_W2"], i["L2_ffn_b2"], i["L2_ffn_Wg"], [i["L2_ffn_bg"], i["L2_ffn_bias"]])
    moe("ffn3", i["L3_ffn_W1"], i["L3_ffn_b1"], i["L3_ffn_W2"], i["L3_ffn_b2"])
    for E in (4, 8):
        z = np.zeros((2, E, E, P), np.float32)
        for e in range(E):
            z[0, e, e, :D], z[1, e, e, D:] = 1, 1
        arrays[f"sel{E}"] = z.reshape(2 * E, E, P)
        arrays[f"index{E}"] = np.broadcast_to(np.arange(E, dtype=np.float32), (P, 2 * TJ, E))

    arrays["att1_wq"], arrays["att1_wm"] = both(i["L1_attn_Wq"]), both(i["L1_attn_Wm"])
    arrays["att1_wkv"] = np.concatenate([both(i["L1_attn_Wk"]), both(i["L1_attn_Wv"])], 1)
    arrays["att1_w1x"], arrays["att1_w1m"] = rows(i["L1_attn_W1"][:D]), rows(i["L1_attn_W1"][D:])
    arrays["att1_w2"] = cols(i["L1_attn_W2"])
    arrays["att1_gb"] = twice(np.stack([i[f"L1_attn_{n}"] for n in ("g1", "b1", "g2", "b2")], 1))
    arrays["att1_heads"] = np.broadcast_to(np.tile(np.kron(np.eye(8), np.ones((8, 8))), (2, 1)).astype(np.float32)[:, None], (P, GB, D))
    arrays["ffn1_wi"], arrays["ffn1_wo"] = rows(i["L1_ffn_Wi"].T), cols(i["L1_ffn_Wo"].T)
    arrays["ffn1_bi"], arrays["ffn1_bo"] = i["L1_ffn_bi"][:, None], twice(i["L1_ffn_bo"][:, None])
    arrays["ffn1_bs"] = i["L1_ffn_bs"][:, 0].T
    arrays["ffn1_ws"] = i["L1_ffn_Ws"][:, 0].transpose(2, 0, 1)
    arrays["route"] = i["L1_ffn_route_id"][None]
    E = i["L1_ffn_Wr"].shape[1]
    arrays["ffn1_experts"] = np.concatenate(
        [i["L1_ffn_Wr"].transpose(3, 1, 0, 2).reshape(P, E, LAYERS * P), i["L1_ffn_br"].transpose(2, 1, 0)], 2).reshape(P, E * ROUTED)
    arrays["att2_c"] = twice(i["L2_attn_c"][0])
    for n in "BCD":
        arrays[f"att3_w{n.lower()}"] = both(i[f"L3_attn_W_{n}"].T)
    arrays["att3_par"] = twice(np.stack([i[f"L3_attn_{n}"] for n in ("a", "b_B", "b_C", "b_D")], 1))
    edges = i["L3_ffn_edge_index"].reshape(2, P, EW)
    arrays["edge_src"], arrays["edge_dst"] = edges[0], edges[1]
    arrays["gat_wg"] = both(i["L3_ffn_W_gat"])
    across = lambda *w: np.broadcast_to(np.stack([x.reshape(GF) for x in w])[None, :, None], (P, len(w), HI, GF))
    arrays["gat_att"] = across(i["L3_ffn_att_src"], i["L3_ffn_att_dst"])
    arrays["gat_norm"] = across(i["L3_ffn_b_gat"], i["L3_ffn_ln_gamma"], i["L3_ffn_ln_beta"])
    arrays["gat_iota"] = np.broadcast_to(np.arange(P, dtype=np.float32), (P, P))
    nc = bacc.Bacc("TRN2", target_bir_lowering=False, num_devices=1)
    arrays = {f"in_{k}": np.ascontiguousarray(v) for k, v in arrays.items()}
    a = {k[3:]: nc.dram_tensor(k, v.shape, mybir.dt.from_np(v.dtype), kind="ExternalInput").ap() for k, v in arrays.items()}
    out = nc.dram_tensor("out", (TOK, D), F32, kind="ExternalOutput").ap()
    build(nc, a, out)
    r = run_bass_kernel_spmd(nc, [arrays], core_ids=[0])
    return r.results[0]["out"].reshape(B, T, D)
```

```python
from contextlib import ExitStack

import concourse.bass as bass
from concourse import mybir
from concourse.alu_op_type import AluOpType as ALU

F32 = mybir.dt.float32
I32 = mybir.dt.int32
U32 = mybir.dt.uint32
ACT = mybir.ActivationFunctionType
AX = mybir.AxisListType.X

P = 128
B, T, D = 64, 64, 64
TOK = B * T
HALF = TOK // 2
GC = 512
G = HALF // GC
TJ = GC // P
GB = GC // T
NH = 256
EPS = 1e-5
PART = 32
LN_EXP = "natural_log_exp_and_others"
STAGES = 99


class Stage:

    def __init__(self, nc, name):
        self.nc, self.name, self.ctx, self.all = nc, name, ExitStack(), []

    def sem(self, what):
        s = self.nc.alloc_semaphore(f"{self.name}_{what}")
        self.all.append(s)
        return s

    def sems(self, names):
        return [self.sem(n) for n in names.split()]

    def sb(self, what, shape, dt=F32):
        return self.ctx.enter_context(self.nc.sbuf_tensor(f"{self.name}_{what}", shape, dt))

    def ps(self, what, shape):
        return self.ctx.enter_context(self.nc.psum_tensor(f"{self.name}_{what}", shape, F32))

    def end(self):
        self.ctx.close()
        self.nc.clear_and_free_semaphores(self.all)
        self.nc.all_engine_barrier()


class Norm:

    def __init__(self, st, name, con, centred_ps, var_ps, sq, std, switch=False):
        self.switch = switch
        self.con, self.cp, self.vp, self.sq, self.std = con, centred_ps, var_ps, sq, std
        self.centred, self.squared, self.averaged, self.rooted, self.inverted, self.normed = st.sems(
            " ".join(f"{name}_{x}" for x in "centred squared averaged rooted inverted normed".split()))

    def of(self, buffers, g):
        return buffers[g] if isinstance(buffers, list) else buffers

    def tensor_centre(self, pe, src, src_ready, g):
        pe.wait_ge(src_ready, g + 1)
        pe.matmul(self.of(self.cp, g), self.con["centre"], src, start=True, stop=True).then_inc(self.centred, 1)

    def tensor_average(self, pe, g):
        pe.wait_ge(self.squared, g + 1)
        pe.matmul(self.of(self.vp, g), self.con["average"], self.of(self.sq, g), start=True, stop=True).then_inc(self.averaged, 1)

    def scalar(self, act, g):
        self.scalar_square(act, g)
        self.scalar_root(act, g)

    def scalar_square(self, act, g):
        act.wait_ge(self.centred, g + 1)
        act.activation(self.of(self.sq, g), self.of(self.cp, g), ACT.Square).then_inc(self.squared, 1)

    def scalar_root(self, act, g):
        if self.switch:
            act.preload_act_table_set(LN_EXP)
        act.wait_ge(self.averaged, g + 1)
        std = self.of(self.std, g)
        act.activation(std, self.of(self.vp, g), ACT.Ln, bias=self.con["eps"]).then_inc(self.rooted, 1)
        act.wait_ge(self.rooted, g + 1)
        act.activation(std, std, ACT.Exp, scale=-0.5).then_inc(self.inverted, 1)

    def vector(self, v, out, g):
        v.wait_ge(self.inverted, g + 1)
        v.tensor_tensor(out, self.of(self.cp, g), self.of(self.std, g), ALU.mult).then_inc(self.normed, 1)

    def tensor_all(self, pe, srcs, src_ready):
        for g in range(G + 1):
            if g < G:
                self.tensor_centre(pe, srcs[g], src_ready, g)
            if g:
                self.tensor_average(pe, g - 1)

    def scalar_all(self, act):
        for g in range(G + 1):
            if g < G:
                self.scalar_square(act, g)
            if g:
                self.scalar_root(act, g - 1)


def padded_group(con, g):
    return con["padded"][:, bass.ds((g + 1) * GC, GC)]


def group(t, g):
    return t[:, bass.ds(g * GC, GC)]


def tokenizer(nc, con, X, a):
    st = Stage(nc, "tok")
    F = 4
    wb = st.sb("wb", [P, F + 1])
    mean = st.sb("mean", [P, F + 1])
    xin = [st.sb(f"xin{k}", [P, TJ, 2, D * F]) for k in range(G)]
    tm = [st.sb(f"tm{k}", [P, GC]) for k in range(G)]
    mean_ps = st.ps("mean_ps", [P, F + 1])
    turn_ps = [st.ps(f"turn_ps{k}", [P, GC]) for k in range(G)]
    consts_in, w_in, meaned, mean_kept, summed, turned, kept = st.sems(
        "consts_in w_in meaned mean_kept summed turned kept")
    x_in = [st.sem(f"x_in{k}") for k in range(G)]
    edge_src, edge_dst = st.sb("edge_src", [P, EW], I32), st.sb("edge_dst", [P, EW], I32)
    inside = st.sb("inside", [P, EW])
    src_in, dst_in, capped, keyed, marked = st.sems("src_in dst_in capped keyed marked")
    xr = a["x"].rearrange("(h k j p) c -> k p j h c", h=2, k=G, j=TJ, p=P)
    block = st.ctx.enter_context(nc.Block())

    @block.sync
    def _(sp):
        sp.dma_start(con["consts"], a["consts"]).then_inc(consts_in, 16)
        sp.dma_start(wb[:, :], a["tok"]).then_inc(w_in, 16)
        for k in range(G):
            for j in range(TJ):
                sp.dma_start(xin[k][:, j, :, :], xr[k][:, j, :, :]).then_inc(x_in[k], 16)
        sp.dma_start(edge_src[:, :], a["edge_src"]).then_inc(src_in, 16)
        sp.dma_start(edge_dst[:, :], a["edge_dst"]).then_inc(dst_in, 16)

    @block.tensor
    def _(pe):
        pe.wait_ge(consts_in, 16)
        pe.wait_ge(w_in, 16)
        pe.matmul(mean_ps[:, :], con["mean128"], wb[:, :], start=True, stop=True).then_inc(meaned, 1)
        for k in range(G):
            pe.wait_ge(summed, F * k + F)
            for j in range(TJ):
                mm = pe.transpose(turn_ps[k][:, j * P:(j + 1) * P], tm[k][:, j * P:(j + 1) * P], con["ident"])
            mm.then_inc(turned, 1)

    @block.vector
    def _(v):
        v.wait_ge(meaned, 1)
        v.tensor_copy(mean[:, :], mean_ps[:, :]).then_inc(mean_kept, 1)
        v.wait_ge(mean_kept, 1)
        for k in range(G):
            v.wait_ge(x_in[k], 16 * TJ)
            xf = xin[k][:, :, :, :].rearrange("p j h (d f) -> p (j h d) f", f=F)
            v.tensor_scalar(tm[k][:, :], xf[:, :, 0], mean[:, 0:1], mean[:, F:F + 1], ALU.mult,
                            ALU.add).then_inc(summed, 1)
            for f in range(1, F):
                v.wait_ge(summed, F * k + f)
                v.scalar_tensor_tensor(tm[k][:, :], xf[:, :, f], mean[:, f:f + 1], tm[k][:, :],
                                       ALU.mult, ALU.add).then_inc(summed, 1)
        key = con["left"][:, 0:EW]
        v.memset(con["keys"], 0.0)
        v.memset(con["padded"][:, GC + HALF:], 0.0)
        v.memset(con["scores"], 0.0)
        v.wait_ge(src_in, 16)
        v.tensor_scalar(inside[:, :], edge_src[:, :], float(TOK - 1), 1.0, ALU.min, ALU.add).then_inc(capped, 1)
        v.wait_ge(capped, 1)
        v.wait_ge(dst_in, 16)
        v.scalar_tensor_tensor(key, edge_dst[:, :], float(TOK), inside[:, :], ALU.mult, ALU.add).then_inc(keyed, 1)
        v.wait_ge(keyed, 1)
        v.tensor_scalar(inside[:, :], edge_dst[:, :], float(TOK), None, ALU.is_lt).then_inc(marked, 1)
        v.wait_ge(marked, 1)
        v.tensor_tensor(key, key, inside[:, :], ALU.mult)
        v.tensor_reduce(con["edge_count"], inside[:, :], AX, ALU.add)

    @block.scalar
    def _(act):
        for k in range(G):
            act.wait_ge(turned, k + 1)
            act.activation(X[:, k * GC:(k + 1) * GC], turn_ps[k][:, :], ACT.Copy).then_inc(kept, 1)

    st.end()


def first_attention(nc, con, X, a):
    st = Stage(nc, "att0")
    NB = 2 * GB
    A = 0.97
    BIG = 1e12
    dx = st.sb("dx", [P, 2, NH])
    dy = st.sb("dy", [P, 2, NH])
    e_rows, et = st.sb("e_rows", [P, 2, 2, P]), st.sb("et", [P, 4, P])
    decay = st.sb("decay", [P, GC])
    later = st.sb("later", [P, 2 * GC])
    into_row = st.sb("into_row", [P, NB, NB])
    own = st.sb("own", [NB, NB, T])
    keep = st.sb("keep", [P, 2 * GC])
    xg, nv, u = st.sb("xg", [P, GC]), st.sb("nv", [P, GC]), st.sb("u", [P, 4, GC])
    sq, std = st.sb("sq", [P, GC]), st.sb("std", [P, GC])
    run, q, sig, r, total = [st.sb(n, [NB, T]) for n in ("run", "q", "sig", "r", "total")]
    ur, xs = st.sb("ur", [P, 4, GC]), st.sb("xs", [P, 4, GC])
    gm, nvt = st.sb("gm", [P, 2, GC]), st.sb("nvt", [P, GC])
    an, asum, y, vs, hsum = st.sb("an", [P, GC]), st.sb("asum", [P, GC]), st.sb("y", [P, 4, GC]), st.sb("vs", [P, GC]), st.sb("hsum", [P, GC])
    big = st.ps("big", [P, 4, GC])
    sums = st.ps("sums", [P, 2, GC])
    cp, vp = st.ps("cp", [P, GC]), st.ps("vp", [P, GC])
    dx_in, e_in, e_centred, e_kept, weights_in, grouped, u_made, u_kept, u_summed = st.sems("dx_in e_in e_centred e_kept weights_in grouped u_made u_kept u_summed")
    total_kept, placed, r_spread, ran, capped, q_raw, q_first, q_made, s_raw, s_first, sig_made = st.sems("total_kept placed r_spread ran capped q_raw q_first q_made s_raw s_first sig_made")
    raw, raw_first, guarded, inverted, kept, scaled, scanned = st.sems("raw raw_first guarded inverted kept scaled scanned")
    grams, masked, v_turned, v_kept, attended, a_kept, y_made, gated, added = st.sems(
        "grams masked v_turned v_kept attended a_kept y_made gated added")
    n_v = Norm(st, "nv", con, cp[:, :], vp[:, :], sq[:, :], std[:, :])
    n_a = Norm(st, "na", con, cp[:, :], vp[:, :], sq[:, :], std[:, :])
    n_s = Norm(st, "ns", con, sums[:, 0, :], vp[:, :], sq[:, :], std[:, :])
    n_o = Norm(st, "no", con, cp[:, :], vp[:, :], sq[:, :], std[:, :])
    block = st.ctx.enter_context(nc.Block())

    @block.sync
    def _(sp):
        sp.dma_start(dx[:, :, :], a["dx"]).then_inc(dx_in, 16)
        sp.dma_start(e_rows[:, :, :, :], a["e_rows"]).then_inc(e_in, 16)
        for dst, src in ((dy[:, :, :], "dy"),
                         (decay[:, :], "decay"), (later[:, :], "later"), (into_row[:, :, :], "into_row")):
            sp.dma_start(dst, a[src]).then_inc(weights_in, 16)

    @block.tensor
    def _(pe):
        pe.wait_ge(dx_in, 16)
        pe.wait_ge(e_in, 16)
        for n in range(4):
            mm = pe.matmul(sums[:, 0, n * P:(n + 1) * P], e_rows[:, n // 2, n % 2, :], con["centre"], start=True, stop=True)
        mm.then_inc(e_centred, 1)

        def units(g, h):
            pe.wait_ge(grouped, g + 1)
            for c in range(2):
                mm = pe.matmul(big[:, 2 * h + c, :], dx[:, h, c * P:(c + 1) * P], xg[:, :], start=True, stop=True)
            mm.then_inc(u_made, 1)

        units(0, 0)
        units(0, 1)
        n_v.tensor_centre(pe, xg[:, :], grouped, 0)
        with pe.Fori(0, G) as g:
            n_v.tensor_average(pe, g)
            pe.wait_ge(u_kept, 2 * g + 2)
            pe.wait_ge(weights_in, 16 * 4)
            for b in range(NB):
                for c in range(2):
                    mm = pe.matmul(big[0:NB, 0, 0:T], into_row[:, b, :], u[:, 2 * (b // GB) + c, b % GB * T:(b % GB + 1) * T],
                                   start=b + c == 0, stop=b == NB - 1 and c == 1)
            mm.then_inc(u_summed, 1)
            pe.wait_ge(n_v.normed, g + 1)
            for j in range(TJ):
                mm = pe.transpose(big[:, 2, j * P:(j + 1) * P], nv[:, j * P:(j + 1) * P], con["ident"])
            mm.then_inc(v_turned, 1)
            pe.wait_ge(e_kept, 1)
            pe.wait_ge(placed, g + 1)
            for h in range(2):
                mm = pe.matmul(sums[:, h, :], con["ones"][0:NB, :], own[:, h * GB:(h + 1) * GB, :].rearrange("p b t -> p (b t)"),
                               start=True, stop=True)
            mm.then_inc(r_spread, 1)
            for h in range(2):
                pe.wait_ge(scanned, 4 * g + 2 * h + 2)
                for j in range(TJ):
                    for c in range(2):
                        xt = xs[:, 2 * h + c, j * P:(j + 1) * P]
                        mm = pe.matmul(big[:, h, j * P:(j + 1) * P], xt, xt, start=c == 0, stop=c == 1)
            mm.then_inc(grams, 1)
            pe.wait_ge(masked, g + 1)
            pe.wait_ge(v_kept, g + 1)
            for h in range(2):
                for j in range(TJ):
                    mm = pe.matmul(big[h * D:(h + 1) * D, 3, j * P:(j + 1) * P], nvt[:, j * P + h * D:j * P + (h + 1) * D],
                                   gm[:, h, j * P:(j + 1) * P], start=True, stop=True)
            mm.then_inc(attended, 1)
            n_a.tensor_centre(pe, asum[:, :], a_kept, g)
            n_a.tensor_average(pe, g)
            pe.wait_ge(n_a.normed, g + 1)
            for h in range(2):
                for c in range(2):
                    pe.matmul(big[:, 2 * h + c, :], dy[:, h, c * P:(c + 1) * P], an[:, :], start=True, stop=True).then_inc(y_made, 1)
            for n in range(4):
                pe.wait_ge(gated, 4 * g + n + 1)
                mm = pe.matmul(sums[:, 0, :], et[:, n, :], y[:, n, :], start=n == 0, stop=n == 3)
            mm.then_inc(n_s.centred, 1)
            n_s.tensor_average(pe, g)
            n_o.tensor_centre(pe, hsum[:, :], added, g)
            units(g + 1, 0)
            n_o.tensor_average(pe, g)
            units(g + 1, 1)
            pe.wait_ge(n_o.normed, g + 1)
            n_v.tensor_centre(pe, xg[:, :], grouped, g + 1)

    @block.scalar
    def _(act):
        act.preload_act_table_set(LN_EXP)
        act.wait_ge(e_centred, 1)
        act.activation(et[:, :, :].rearrange("p n c -> p (n c)"), sums[:, 0, :], ACT.Copy).then_inc(e_kept, 1)
        with act.Fori(0, G) as g:
            for h in range(2):
                act.wait_ge(u_made, 2 * g + h + 1)
                act.activation(u[:, 2 * h:2 * h + 2, :], big[:, 2 * h:2 * h + 2, :], ACT.Relu).then_inc(u_kept, 1)
            n_v.scalar(act, g)
            act.wait_ge(v_turned, g + 1)
            act.activation(nvt[:, :], big[:, 2, :], ACT.Copy).then_inc(v_kept, 1)
            act.wait_ge(attended, g + 1)
            act.activation(asum[:, :], big[:, 3, :], ACT.Copy).then_inc(a_kept, 1)
            n_a.scalar(act, g)
            n_s.scalar(act, g)
            n_o.scalar(act, g)

    @block.vector
    def _(v):
        v.tensor_copy(xg[:, :], X[:, 0:GC]).then_inc(grouped, 1)
        with v.Fori(0, G) as g:
            n_v.vector(v, nv[:, :], g)
            v.wait_ge(weights_in, 16 * 4)
            v.wait_ge(u_summed, g + 1)
            v.tensor_copy(total[:, :], big[0:NB, 0, 0:T]).then_inc(total_kept, 1)
            v.wait_ge(total_kept, g + 1)
            v.tensor_tensor_scan(run[:, :], later[0:NB, 0:T], total[:, :], 0.0, ALU.mult, ALU.max).then_inc(ran, 1)
            v.wait_ge(ran, g + 1)
            v.tensor_scalar(run[:, :], run[:, :], BIG, 1.0, ALU.mult, ALU.min).then_inc(capped, 1)
            v.wait_ge(capped, g + 1)
            v.tensor_copy(q[:, 0:1], run[:, 0:1]).then_inc(q_first, 1)
            v.scalar_tensor_tensor(q[:, 1:T], run[:, 0:T - 1], A * BIG, run[:, 1:T], ALU.mult, ALU.add).then_inc(q_raw, 1)
            v.wait_ge(q_first, g + 1)
            v.wait_ge(q_raw, g + 1)
            v.tensor_scalar(q[:, :], q[:, :], 1.0, None, ALU.min).then_inc(q_made, 1)
            v.wait_ge(q_made, g + 1)
            v.tensor_copy(sig[:, 0:1], run[:, 0:1]).then_inc(s_first, 1)
            v.scalar_tensor_tensor(sig[:, 1:T], q[:, 0:T - 1], A * BIG, run[:, 1:T], ALU.mult, ALU.add).then_inc(s_raw, 1)
            v.wait_ge(s_first, g + 1)
            v.wait_ge(s_raw, g + 1)
            v.tensor_scalar(sig[:, :], sig[:, :], 1.0, None, ALU.min).then_inc(sig_made, 1)
            v.wait_ge(sig_made, g + 1)
            v.tensor_copy(r[:, 0:1], total[:, 0:1]).then_inc(raw_first, 1)
            v.scalar_tensor_tensor(r[:, 1:T], sig[:, 0:T - 1], A, total[:, 1:T], ALU.mult, ALU.add).then_inc(raw, 1)
            v.wait_ge(raw_first, g + 1)
            v.wait_ge(raw, g + 1)
            v.tensor_scalar(r[:, :], r[:, :], 1.0 / BIG, None, ALU.max).then_inc(guarded, 1)
            v.wait_ge(guarded, g + 1)
            v.reciprocal(r[:, :], r[:, :]).then_inc(inverted, 1)
            v.wait_ge(inverted, g + 1)
            v.tensor_tensor(own[:, :, :], r[:, None, :].to_broadcast((NB, NB, T)),
                            con["ident"][0:NB, 0:NB][:, :, None].to_broadcast((NB, NB, T)), ALU.mult).then_inc(placed, 1)
            v.wait_ge(r_spread, g + 1)
            for h in range(2):
                half = slice(h * GC, (h + 1) * GC)
                v.scalar_tensor_tensor(keep[:, half], sums[:, h, :], A, later[:, half], ALU.mult, ALU.mult).then_inc(kept, 1)
                for n in (2 * h, 2 * h + 1):
                    v.tensor_tensor(ur[:, n, :], u[:, n, :], sums[:, h, :], ALU.mult).then_inc(scaled, 1)
                v.wait_ge(kept, 2 * g + h + 1)
                for n in (2 * h, 2 * h + 1):
                    v.wait_ge(scaled, 4 * g + n + 1)
                    v.tensor_tensor_scan(xs[:, n, :], keep[:, half], ur[:, n, :], 0.0, ALU.mult, ALU.add).then_inc(scanned, 1)
            v.wait_ge(grams, g + 1)
            for h in range(2):
                ins = v.tensor_tensor(gm[:, h, :], big[:, h, :], decay[:, :], ALU.mult)
            ins.then_inc(masked, 1)
            n_a.vector(v, an[:, :], g)
            for n in range(4):
                v.wait_ge(y_made, 4 * g + n + 1)
                v.scalar_tensor_tensor(y[:, n, :], big[:, n, :], 0.0, xs[:, n, :], ALU.max, ALU.mult).then_inc(gated, 1)
            n_s.vector(v, vs[:, :], g)
            v.wait_ge(n_s.normed, g + 1)
            v.tensor_tensor(hsum[:, :], xg[:, :], vs[:, :], ALU.add).then_inc(added, 1)
            v.wait_ge(added, g + 1)
            v.tensor_copy(xg[:, :], padded_group(con, g + 1)).then_inc(grouped, 1)
            n_o.vector(v, group(X, g), g)

    st.end()


def finish(nc, con, X, out):
    st = Stage(nc, "out")
    rows = [st.sb(f"rows{k}", [P, TJ, P]) for k in range(G)]
    turn_ps = [st.ps(f"turn_ps{k}", [P, GC]) for k in range(G)]
    turned, kept = st.sems("turned kept")
    stored = [st.sem(f"stored{k}") for k in range(G)]
    ov = out.rearrange("(h k j p) d -> k h p j d", h=2, k=G, j=TJ, p=P)
    block = st.ctx.enter_context(nc.Block())

    @block.tensor
    def _(pe):
        for k in range(G):
            for j in range(TJ):
                c = k * GC + j * P
                mm = pe.transpose(turn_ps[k][:, j * P:(j + 1) * P], X[:, c:c + P], con["ident"])
            mm.then_inc(turned, 1)

    @block.vector
    def _(v):
        for k in range(G):
            v.wait_ge(turned, k + 1)
            v.tensor_copy(rows[k][:, :, :].rearrange("p j c -> p (j c)"), turn_ps[k][:, :]).then_inc(kept, 1)

    @block.sync
    def _(sp):
        for k in range(G):
            sp.wait_ge(kept, k + 1)
            for h in range(2):
                sp.dma_start(ov[k][h], rows[k][:, :, h * D:(h + 1) * D]).then_inc(stored[k], 16)
        for k in range(G):
            sp.wait_ge(stored[k], 32)

    st.end()

def experts(nc, con, X, a, name, E, HC, act_fn, scored=None, prenorm=False, background=None, spare_work=None):
    st = Stage(nc, name)
    BF16 = mybir.dt.bfloat16
    TH = TJ * 2
    N = E * 2 * HC
    state = lambda g: padded_group(con, g)
    if E == 8:
        at = dict(leave_centre=0, leave_average=1, leave_root=3, leave_scale=3 if HC == 2 else 4, enter=0, route=1, best=2,
                  exp=3, gate=4, centre=4, average=5, root=5, turn=6, turn_keep=5, scale=6, bias=6, start=6)
    else:
        at = dict(leave_centre=0, leave_average=1, leave_root=1, leave_scale=2, enter=0, route=None, best=0,
                  exp=1, gate=1, centre=None, average=None, root=None, turn=2, turn_keep=2, scale=None, bias=3, start=3)
    w1 = st.sb("w1", [P, 2, E, HC * P])
    w2 = st.sb("w2", [P, E, HC, 2, P])
    b1 = st.sb("b1", [P, E, HC])
    b2 = st.sb("b2", [3 * PART, P])
    sel, sel_b = st.sb("sel", [3 * PART, E, P]), st.sb("sel_b", [3 * PART, E, P], BF16)
    index = st.sb("index", [P, TH, E])
    loads = [(b1[:, :, :], "b1"), (b2[:, :], "b2"), (sel[:, :, :], "sel"), (index[:, :, :], "index")]
    if scored is None:
        wr = st.sb("wr", [P, 2 * E])
        br = st.sb("br", [P, 2, TH, E])
        loads += [(wr[:, :], "wr"), (br[:, :, :, :], "br")]
    if prenorm:
        scale, shift = st.sb("scale", [P, E]), st.sb("shift", [P, E])
        loads += [(scale[:, :], "scale"), (shift[:, :], "shift")]
    sq, std, xn = [st.sb(n, [P, GC]) for n in ("sq", "std", "xn")]
    xg, acc, xe, hid, part = [[st.sb(f"{n}{k}", [P, GC]) for k in range(2)] for n in ("xg", "acc", "xe", "hid", "part")]
    spread = [st.sb(f"spread{k}", [P, GC]) for k in range(4)]
    gt, gt_b = st.sb("gt", [3 * PART, GC]), [st.sb(f"gt_b{k}", [3 * PART, GC], BF16) for k in range(2)]
    part0, part1 = [st.sb(n, [P, TH, E], BF16) for n in ("part_0", "part_1")]
    rest, parts = st.sb("rest", [P, TH, E]), st.sb("parts", [P, TJ, 3, PART])
    lo, eq, low, m1, m2, gate = [st.sb(n, [P, TH, E]) for n in ("lo", "eq", "low", "m1", "m2", "gate")]
    top1, top2, first, e2, den, wgt1, wgt2 = [st.sb(n, [P, TH]) for n in ("top1", "top2", "first", "e2", "den", "wgt1", "wgt2")]
    misc, spread_ps, cp, vp = [st.ps(n, [P, GC]) for n in ("misc", "spread_ps", "cp", "vp")]
    hid_ps, out_ps = [[st.ps(f"{n}{k}", [P, GC]) for k in range(2)] for n in ("hid_ps", "out_ps")]
    weights_in, w1_in, w2_in, grouped, scored_ps, biased1, biased2 = st.sems(
        "weights_in w1_in w2_in grouped scored_ps biased1 biased2")
    best1, is1, cand1, first1, mark1, masked, best2, is2, cand2, first2, mark2, diff, exped = st.sems(
        "best1 is1 cand1 first1 mark1 masked best2 is2 cand2 first2 mark2 diff exped")
    summed, weight1, weight2, half_gate, gate2, gated, turned, turned_kept, bias_out, bias_kept = st.sems(
        "summed weight1 weight2 half_gate gate2 gated turned turned_kept bias_out bias_kept")
    sel_kept, gate_made, part0_made, rest_made, part1_made, laid, turned_kept2 = st.sems(
        "sel_kept gate_made part0_made rest_made part1_made laid turned_kept2")
    hidden, activated, spread_made, spread_kept, out_made, weighed, accumulated, added, tuned = st.sems(
        "hidden activated spread_made spread_kept out_made weighed accumulated added tuned")
    gelu = act_fn == ACT.Gelu
    n_i = Norm(st, "ni", con, cp[:, :], vp[:, :], sq[:, :], std[:, :], gelu) if prenorm else None
    n_o = Norm(st, "no", con, cp[:, :], vp[:, :], sq[:, :], std[:, :], gelu)
    bc = lambda t: t[:, :, None].to_broadcast((P, TH, E))
    runs = spare_work(st) if spare_work else [(0, G // 2, None)]
    block = st.ctx.enter_context(nc.Block())

    @block.sync
    def _(sp):
        for dst, src in loads:
            sp.dma_start(dst, a[f"{name}_{src}" if src not in ("sel", "index") else f"{src}{E}"]).then_inc(weights_in, 16)
        sp.dma_start(w1[:, :, :, :], a[f"{name}_w1"]).then_inc(w1_in, 16)
        sp.dma_start(w2[:, :, :, :, :], a[f"{name}_w2"]).then_inc(w2_in, 16)
        if background is not None:
            background(sp)

    @block.tensor
    def _(pe):
        def route(g, k):
            if scored is None:
                pe.wait_ge(grouped, g + 1)
                pe.wait_ge(bias_kept, g)
                for j in range(TJ):
                    mm = pe.matmul(misc[:, j * 2 * E:(j + 1) * 2 * E], xg[k][:, j * P:(j + 1) * P], wr[:, :], start=True, stop=True)
                mm.then_inc(scored_ps, 1)

        def enter_centre(g, k):
            if prenorm:
                pe.wait_ge(n_o.normed, g)
                n_i.tensor_centre(pe, xg[k][:, :], grouped, g)

        def enter_average(g):
            if prenorm:
                n_i.tensor_average(pe, g)

        def turn(g):
            pe.wait_ge(gated, g + 1)
            for j in range(TJ):
                mm = pe.transpose(misc[0:3 * PART, j * P:(j + 1) * P], parts[:, j, :, :].rearrange("p w c -> p (w c)"), con["ident"])
            mm.then_inc(turned, 1)

        def bias(g):
            pe.wait_ge(turned_kept2, g + 1)
            pe.matmul(misc[:, :], b2[:, :], gt[:, :], start=True, stop=True).then_inc(bias_out, 1)

        def leave_centre(g, k):
            if prenorm:
                pe.wait_ge(n_i.normed, g + 1)
            n_o.tensor_centre(pe, acc[1 - k][:, :], added, g)

        def hidden_of(g, n, k):
            e, h, c = n // (2 * HC), n // HC % 2, n % HC
            if prenorm:
                pe.wait_ge(tuned, g * E + e + 1)
            else:
                pe.wait_ge(grouped, g + 1)
            src = xe[e % 2] if prenorm else xg[k]
            pe.matmul(hid_ps[n % 2][:, :], w1[:, h, e, c * P:(c + 1) * P], src[:, :], start=True, stop=True).then_inc(hidden, 1)

        def output_of(g, n):
            e, h, c = n // (2 * HC), n // HC % 2, n % HC
            if n % (2 * HC) == 0:
                pe.wait_ge(weighed, g * E + e + 1)
            pe.wait_ge(activated, g * N + n + 1)
            mm = pe.matmul(out_ps[e % 2][:, :], w2[:, e, c, h, :], hid[n % 2][:, :],
                           start=n % (2 * HC) == 0, stop=n % (2 * HC) == 2 * HC - 1)
            if n % (2 * HC) == 2 * HC - 1:
                mm.then_inc(out_made, 1)

        def spread_of(g, e, k):
            if e == 0:
                pe.wait_ge(turned_kept, g + 1)
            pe.wait_ge(spread_kept, g * E + e)
            pe.matmul(spread_ps[:, :], sel_b[:, e, :], gt_b[k][:, :], start=True, stop=True).then_inc(spread_made, 1)

        pe.wait_ge(weights_in, 16 * len(loads))
        if scored is None:
            pe.wait_ge(grouped, 1)
            for j in range(TJ):
                mm = pe.matmul(misc[:, j * 2 * E:(j + 1) * 2 * E], xg[0][:, j * P:(j + 1) * P], wr[:, :], start=True, stop=True)
            mm.then_inc(scored_ps, 1)
        if prenorm:
            n_i.tensor_centre(pe, xg[0][:, :], grouped, 0)
            enter_average(0)
        pe.wait_ge(w1_in, 16)
        hidden_of(0, 0, 0)
        hidden_of(0, 1, 0)
        turn(0)
        bias(0)
        pe.wait_ge(sel_kept, 1)
        pe.matmul(spread_ps[:, :], sel_b[:, 0, :], gt_b[0][:, :], start=True, stop=True).then_inc(spread_made, 1)
        pe.wait_ge(w2_in, 16)
        with pe.Fori(0, G // 2) as pair:
            for k in range(2):
                g = pair * 2 + k
                for n in range(N):
                    e = n // (2 * HC)
                    output_of(g, n)
                    hidden_of(g + (n + 2) // N, (n + 2) % N, (k + (n + 2) // N) % 2)
                    if n % (2 * HC) == 0:
                        spread_of(g + (e + 1) // E, (e + 1) % E, (k + (e + 1) // E) % 2)
                    if n % (2 * HC) == (0 if E == 8 else 1) and at["turn"] == e:
                        pe.wait_ge(bias_kept, g + 1)
                        turn(g + 1)
                    if n % (2 * HC) == 1:
                        if at["leave_centre"] == e:
                            leave_centre(g, k)
                        if at["leave_average"] == e:
                            n_o.tensor_average(pe, g)
                        if at["route"] == e:
                            route(g + 1, 1 - k)
                        if at["centre"] == e:
                            enter_centre(g + 1, 1 - k)
                        if at["average"] == e:
                            enter_average(g + 1)
                        if at["bias"] == e:
                            bias(g + 1)
        pe.wait_ge(n_o.normed, G)
        n_o.tensor_centre(pe, acc[1][:, :], added, G)
        n_o.tensor_average(pe, G)

    @block.scalar
    def _(act):
        def exp_gate(g):
            act.wait_ge(diff, g + 1)
            act.activation(e2[:, :], top2[:, :], ACT.Exp).then_inc(exped, 1)

        def spread_copy(g, e):
            act.wait_ge(spread_made, g * E + e + 1)
            act.activation(spread[e % 4][:, :], spread_ps[:, :], ACT.Copy).then_inc(spread_kept, 1)

        act.preload_act_table_set(LN_EXP)
        act.wait_ge(weights_in, 16 * len(loads))
        if prenorm:
            n_i.scalar(act, 0)
        exp_gate(0)
        spread_copy(0, 0)
        with act.Fori(0, G // 2) as pair:
            for k in range(2):
                g = pair * 2 + k
                for n in range(N):
                    e = n // (2 * HC)
                    act.wait_ge(hidden, g * N + n + 1)
                    act.activation(hid[n % 2][:, :], hid_ps[n % 2][:, :], act_fn,
                                   bias=b1[:, e, n % HC:n % HC + 1]).then_inc(activated, 1)
                    if n % (2 * HC) == 1:
                        act.wait_ge(weighed, g * E + e + 1)
                        spread_copy(g + (e + 1) // E, (e + 1) % E)
                    late = n - (3 if HC == 2 else 2)
                    if late % (2 * HC) == 0:
                        e = late // (2 * HC)
                        if at["leave_centre"] == e:
                            n_o.scalar_square(act, g)
                        if at["centre"] == e and prenorm:
                            n_i.scalar_square(act, g + 1)
                        if at["leave_root"] == e:
                            n_o.scalar_root(act, g)
                        if at["exp"] == e:
                            exp_gate(g + 1)
                        if at["root"] == e and prenorm:
                            n_i.scalar_root(act, g + 1)
        n_o.scalar(act, G)

    @block.vector
    def _(v):
        def enter(g, k):
            v.tensor_copy(xg[k][:, :], state(g)).then_inc(grouped, 1)

        def scale_entry(g):
            if prenorm:
                n_i.vector(v, xn[:, :], g)
                v.wait_ge(n_i.normed, g + 1)

        def tune(e):
            v.tensor_scalar(xe[e % 2][:, :], xn[:, :], scale[:, e:e + 1], shift[:, e:e + 1], ALU.mult, ALU.add).then_inc(tuned, 1)

        def best_two(g):
            if scored is None:
                v.wait_ge(scored_ps, g + 1)
                lg = misc[:, 0:TH * E].rearrange("p (t e) -> p t e", e=E)
                v.tensor_tensor(lo[:, :, :], lg, br[:, 0, :, :], ALU.add).then_inc(biased1, 1)
                v.wait_ge(biased1, g + 1)
                v.tensor_tensor(lo[:, :, :], lo[:, :, :], br[:, 1, :, :], ALU.add).then_inc(biased2, 1)
            else:
                v.tensor_copy(lo[:, :, :].rearrange("p t e -> p (t e)"), scored[:, bass.ds(g * TH * E, TH * E)]).then_inc(biased2, 1)
            v.wait_ge(biased2, g + 1)
            v.tensor_reduce(top1[:, :], lo[:, :, :], AX, ALU.max).then_inc(best1, 1)
            v.wait_ge(best1, g + 1)
            v.tensor_tensor(eq[:, :, :], lo[:, :, :], bc(top1), ALU.is_equal).then_inc(is1, 1)
            v.wait_ge(is1, g + 1)
            v.scalar_tensor_tensor(low[:, :, :], eq[:, :, :], -float(E), index[:, :, :], ALU.mult, ALU.add).then_inc(cand1, 1)
            v.wait_ge(cand1, g + 1)
            v.tensor_reduce(first[:, :], low[:, :, :], AX, ALU.min).then_inc(first1, 1)
            v.wait_ge(first1, g + 1)
            v.tensor_tensor(m1[:, :, :], low[:, :, :], bc(first), ALU.is_equal).then_inc(mark1, 1)
            v.wait_ge(mark1, g + 1)
            v.scalar_tensor_tensor(lo[:, :, :], m1[:, :, :], -3.0e38, lo[:, :, :], ALU.mult, ALU.add).then_inc(masked, 1)
            v.wait_ge(masked, g + 1)
            v.tensor_reduce(top2[:, :], lo[:, :, :], AX, ALU.max).then_inc(best2, 1)
            v.wait_ge(best2, g + 1)
            v.tensor_tensor(eq[:, :, :], lo[:, :, :], bc(top2), ALU.is_equal).then_inc(is2, 1)
            v.wait_ge(is2, g + 1)
            v.scalar_tensor_tensor(low[:, :, :], eq[:, :, :], -float(E), index[:, :, :], ALU.mult, ALU.add).then_inc(cand2, 1)
            v.tensor_tensor(top2[:, :], top2[:, :], top1[:, :], ALU.subtract).then_inc(diff, 1)
            v.wait_ge(cand2, g + 1)
            v.tensor_reduce(first[:, :], low[:, :, :], AX, ALU.min).then_inc(first2, 1)
            v.wait_ge(first2, g + 1)
            v.tensor_tensor(m2[:, :, :], low[:, :, :], bc(first), ALU.is_equal).then_inc(mark2, 1)

        def make_gates(g):
            v.wait_ge(exped, g + 1)
            v.tensor_scalar(den[:, :], e2[:, :], 1.0, None, ALU.add).then_inc(summed, 1)
            v.wait_ge(summed, g + 1)
            v.reciprocal(wgt1[:, :], den[:, :]).then_inc(weight1, 1)
            v.wait_ge(weight1, g + 1)
            v.tensor_tensor(wgt2[:, :], e2[:, :], wgt1[:, :], ALU.mult).then_inc(weight2, 1)
            v.tensor_tensor(gate[:, :, :], m1[:, :, :], bc(wgt1), ALU.mult).then_inc(half_gate, 1)
            v.wait_ge(weight2, g + 1)
            v.wait_ge(mark2, g + 1)
            v.tensor_tensor(m2[:, :, :], m2[:, :, :], bc(wgt2), ALU.mult).then_inc(gate2, 1)
            v.wait_ge(half_gate, g + 1)
            v.wait_ge(gate2, g + 1)
            v.tensor_tensor(gate[:, :, :], gate[:, :, :], m2[:, :, :], ALU.add).then_inc(gate_made, 1)
            lay = lambda w: parts[:, :, w, 0:2 * E].rearrange("p j (h e) -> p j h e", e=E)
            four = lambda t: t[:, :, :].rearrange("p (j h) e -> p j h e", h=2)
            v.wait_ge(gate_made, g + 1)
            v.tensor_copy(part0[:, :, :], gate[:, :, :]).then_inc(part0_made, 1)
            v.wait_ge(part0_made, g + 1)
            v.tensor_tensor(rest[:, :, :], gate[:, :, :], part0[:, :, :], ALU.subtract).then_inc(rest_made, 1)
            v.tensor_copy(lay(0), four(part0)).then_inc(laid, 1)
            v.wait_ge(rest_made, g + 1)
            v.tensor_copy(part1[:, :, :], rest[:, :, :]).then_inc(part1_made, 1)
            v.wait_ge(part1_made, g + 1)
            v.tensor_tensor(lay(2), four(rest), four(part1), ALU.subtract).then_inc(laid, 1)
            v.tensor_copy(lay(1), four(part1)).then_inc(gated, 1)

        def keep_turned(g, k):
            v.wait_ge(turned, g + 1)
            v.tensor_copy(gt_b[k][:, :], misc[0:3 * PART, :]).then_inc(turned_kept, 1)
            v.tensor_copy(gt[:, :], misc[0:3 * PART, :]).then_inc(turned_kept2, 1)

        def start_sum(g, k):
            v.wait_ge(bias_out, g + 1)
            v.tensor_tensor(acc[k][:, :], misc[:, :], xg[k][:, :], ALU.add).then_inc(bias_kept, 1)

        v.memset(acc[1][:, :], 0.0).then_inc(added, 1)
        for k in range(2):
            v.memset(part[k][:, :], 0.0).then_inc(weighed, 1)
        v.memset(parts[:, :, :, :], 0.0)
        enter(0, 0)
        v.wait_ge(weights_in, 16 * len(loads))
        v.tensor_copy(sel_b[:, :, :], sel[:, :, :]).then_inc(sel_kept, 1)
        if prenorm:
            scale_entry(0)
            tune(0)
            tune(1)
        best_two(0)
        make_gates(0)
        keep_turned(0, 0)
        start_sum(0, 0)
        for first_pair, end_pair, work in runs:
            with v.Fori(first_pair, end_pair) as pair:
                for k in range(2):
                    g = pair * 2 + k
                    for e in range(E):
                        if e == 0:
                            v.wait_ge(bias_kept, g + 1)
                        v.wait_ge(out_made, g * E + e + 1)
                        v.wait_ge(spread_kept, g * E + e + 1)
                        v.tensor_tensor(part[e % 2][:, :], out_ps[e % 2][:, :], spread[e % 4][:, :], ALU.mult).then_inc(weighed, 1)
                        if at["enter"] == e:
                            enter(g + 1, 1 - k)
                        if at["leave_scale"] == e:
                            n_o.vector(v, state(g - 1), g)
                        if at["scale"] == e and prenorm:
                            v.wait_ge(tuned, g * E + E)
                            scale_entry(g + 1)
                        if prenorm:
                            tune((e + 2) % E)
                        v.wait_ge(weighed, g * E + e + 3)
                        if e:
                            v.wait_ge(accumulated, g * (E - 1) + e)
                        ins = v.tensor_tensor(acc[k][:, :], acc[k][:, :], part[e % 2][:, :], ALU.add)
                        ins.then_inc(accumulated if e < E - 1 else added, 1)
                        if at["best"] == e:
                            best_two(g + 1)
                        if at["gate"] == e:
                            make_gates(g + 1)
                        if at["turn_keep"] == e:
                            keep_turned(g + 1, 1 - k)
                        if at["start"] == e:
                            start_sum(g + 1, 1 - k)
                        if work is not None:
                            work(v, g, e)
        n_o.vector(v, state(G - 1), G)

    st.end()


def first_experts(nc, con, X, a):
    def background(sp):
        sp.dma_start(con["route"], a["route"]).then_inc(con["route_in"], 16)
        sp.wait_ge(con["route_in"], 16)
        fetch_experts(sp, con["routed"], con["route"], a["ffn1_experts"], con["routed_in"])

    experts(nc, con, X, a, "ffn0", 8, 2, ACT.Gelu, prenorm=True, background=background,
            spare_work=lambda st: [(0, 1, sift_edges(con)(st)), (1, G // 2, gather_edges(con, EARLY, G // 2, 0)(st))])


def third_experts(nc, con, X, a):
    experts(nc, con, X, a, "ffn2", 8, 1, ACT.Relu,
            background=lambda sp: load_toeplitz(sp, con, con["taps"]),
            spare_work=lambda st: [(0, G // 2, gather_edges(con, LATE, 0, G // 2 * sum(EARLY))(st))])


def second_attention(nc, con, X, a):
    st = Stage(nc, "att1")
    wq, wkv = st.sb("wq", [P, P]), st.sb("wkv", [P, 2 * P])
    turned_w = st.sb("turned_w", [P, 3, P])
    centred_w = st.sb("centred_w", [P, 3 * P])
    w1x, w1m = st.sb("w1x", [P, 2, P]), st.sb("w1m", [P, 2, P])
    gb = st.sb("gb", [P, 4])
    heads = st.sb("heads", [P, GB, D])
    xg, sq, std, qn, qe, qs = [st.sb(n, [P, GC]) for n in ("xg", "sq", "std", "qn", "qe", "qs")]
    kn, ke, ks = [st.sb(n, [P, TJ, 2, D]) for n in ("kn", "ke", "ks")]
    vo = st.sb("vo", [P, TJ, 2, 2 * D])
    num_w, den_w = st.sb("num_w", [P, GB, P]), st.sb("den_w", [P, GB, P])
    den, msg, m1, relu, m2, hs = [st.sb(n, [P, 2, GC] if n == "relu" else [P, GC]) for n in
                                               ("den", "msg", "m1", "relu", "m2", "hs")]
    q_ps, cp = st.ps("q_ps", [P, GC]), st.ps("cp", [P, GC])
    wide_ps = st.ps("wide_ps", [P, 4 * GC])
    kv_ps = wide_ps[:, 0:2 * GC].rearrange("p (a j w h d) -> p a j w h d", a=2, j=TJ // 2, w=2, h=2)
    sum_ps = wide_ps[:, :].rearrange("p (b j h d) -> p b j h d", b=2, j=TJ, h=2)
    num_ps, den_ps = st.ps("num_ps", [P, GC]), st.ps("den_ps", [P, GC])
    first_in, weights_in, ones_set, zero1, zero2, grouped, q_made, kv_made, q_low, q_exp, q_kept = st.sems(
        "first_in weights_in ones_set zero1 zero2 grouped q_made kv_made q_low q_exp q_kept")
    k_low, k_exp, k_kept, v_kept, summed, num_kept, den_kept, num_made, den_made = st.sems(
        "k_low k_exp k_kept v_kept summed num_kept den_kept num_made den_made")
    guarded, inverted, messaged, w_centred, w_kept, tuned1, mlp1, relued, tuned2, added, added2 = st.sems(
        "guarded inverted messaged w_centred w_kept tuned1 mlp1 relued tuned2 added added2")
    n_1 = Norm(st, "n1", con, cp[:, :], q_ps[:, :], sq[:, :], std[:, :])
    n_2 = Norm(st, "n2", con, cp[:, :], q_ps[:, :], sq[:, :], std[:, :])
    n_o = Norm(st, "no", con, cp[:, :], q_ps[:, :], sq[:, :], std[:, :])
    loads = [(wq[:, :], "wq"), (wkv[:, :], "wkv"), (turned_w[:, :, :], "turned_w"), (w1x[:, :, :], "w1x"), (w1m[:, :, :], "w1m"),
             (gb[:, :], "gb"), (heads[:, :, :], "heads")]
    block = st.ctx.enter_context(nc.Block())

    @block.sync
    def _(sp):
        for n, (dst, src) in enumerate(loads):
            sp.dma_start(dst, a[f"att1_{src}"]).then_inc(first_in if n < 3 else weights_in, 16)

    @block.gpsimd
    def _(pool):
        pool.memset(vo[:, :, :, D:2 * D], 1.0).then_inc(ones_set, 1)
        pool.memset(num_w[:, :, :], 0.0).then_inc(zero1, 1)
        pool.memset(den_w[:, :, :], 0.0).then_inc(zero2, 1)
        pool.memset(con["toeplitz"], 0.0)

    @block.tensor
    def _(pe):
        pe.wait_ge(first_in, 48)
        for n in range(3):
            mm = pe.matmul(cp[:, n * P:(n + 1) * P], turned_w[:, n, :], con["centre"], start=True, stop=True)
        mm.then_inc(w_centred, 1)
        pe.wait_ge(ones_set, 1)

        def keys_values(g):
            pe.wait_ge(grouped, g + 1)
            for j in range(TJ):
                mm = pe.matmul(kv_ps[:, j // 2, j % 2, :, :, :].rearrange("p w h d -> p (w h d)"), xg[:, j * P:(j + 1) * P],
                               wkv[:, :], start=True, stop=True)
            mm.then_inc(kv_made, 1)

        def queries():
            pe.matmul(q_ps[:, :], wq[:, :], xg[:, :], start=True, stop=True).then_inc(q_made, 1)

        keys_values(0)
        queries()
        with pe.Fori(0, G) as g:
            pe.wait_ge(k_kept, g + 1)
            pe.wait_ge(v_kept, g + 1)
            for j in range(TJ):
                for b in range(2):
                    r = slice(b * D, (b + 1) * D)
                    mm = pe.matmul(sum_ps[:, b, j, :, :].rearrange("p h d -> p (h d)"), ks[r, j, :, :].rearrange("p h d -> p (h d)"),
                                   vo[r, j, :, :].rearrange("p h d -> p (h d)"), start=True, stop=True)
            mm.then_inc(summed, 1)
            pe.wait_ge(q_kept, g + 1)
            pe.wait_ge(den_kept, 2 * g + 2)
            for b in range(GB):
                mm = pe.matmul(den_ps[:, b * D:(b + 1) * D], den_w[:, b, :], qs[:, b * D:(b + 1) * D], start=True, stop=True)
            mm.then_inc(den_made, 1)
            pe.wait_ge(num_kept, 2 * g + 2)
            for b in range(GB):
                mm = pe.matmul(num_ps[:, b * D:(b + 1) * D], num_w[:, b, :], qs[:, b * D:(b + 1) * D], start=True, stop=True)
            mm.then_inc(num_made, 1)
            pe.wait_ge(messaged, g + 1)
            pe.wait_ge(weights_in, 16 * (len(loads) - 3))
            pe.wait_ge(w_kept, 1)
            pe.matmul(cp[:, :], centred_w[:, 0:P], msg[:, :], start=True, stop=True).then_inc(n_1.centred, 1)
            n_1.tensor_average(pe, g)
            pe.wait_ge(tuned1, g + 1)
            for h in range(2):
                out = (num_ps, den_ps)[h][:, :]
                pe.matmul(out, w1x[:, h, :], xg[:, :], start=True, stop=False)
                mm = pe.matmul(out, w1m[:, h, :], m1[:, :], start=False, stop=True)
            mm.then_inc(mlp1, 1)
            pe.wait_ge(relued, 2 * g + 2)
            pe.matmul(cp[:, :], centred_w[:, P:2 * P], relu[:, 0, :], start=True, stop=False)
            pe.matmul(cp[:, :], centred_w[:, 2 * P:], relu[:, 1, :], start=False, stop=True).then_inc(n_2.centred, 1)
            n_2.tensor_average(pe, g)
            n_o.tensor_centre(pe, hs[:, :], added2, g)
            keys_values(g + 1)
            n_o.tensor_average(pe, g)
            pe.wait_ge(n_o.rooted, g + 1)
            queries()

    @block.scalar
    def _(act):
        act.preload_act_table_set(LN_EXP)
        act.wait_ge(w_centred, 1)
        act.activation(centred_w[:, :], cp[:, 0:3 * P], ACT.Copy).then_inc(w_kept, 1)
        with act.Fori(0, G) as g:
            act.wait_ge(k_low, g + 1)
            act.activation(ke[:, :, :, :], kn[:, :, :, :], ACT.Exp).then_inc(k_exp, 1)
            act.wait_ge(q_low, g + 1)
            act.activation(qe[:, :], qn[:, :], ACT.Exp).then_inc(q_exp, 1)
            act.wait_ge(k_kept, g + 1)
            for half in range(2):
                ins = act.activation(vo[:, 2 * half:2 * half + 2, :, 0:D], kv_ps[:, half, :, 1, :, :], ACT.Copy, scale=1.0 / T)
            ins.then_inc(v_kept, 1)
            n_1.scalar(act, g)
            act.wait_ge(mlp1, g + 1)
            for h in range(2):
                act.activation(relu[:, h, :], (num_ps, den_ps)[h][:, :], ACT.Relu).then_inc(relued, 1)
            n_2.scalar(act, g)
            n_o.scalar(act, g)

    @block.vector
    def _(v):
        v.tensor_copy(xg[:, :], X[:, 0:GC]).then_inc(grouped, 1)
        with v.Fori(0, G) as g:
            v.wait_ge(kv_made, g + 1)
            for half in range(2):
                ins = v.tensor_scalar(kn[:, 2 * half:2 * half + 2, :, :], kv_ps[:, half, :, 0, :, :], 0.0, None, ALU.min)
            ins.then_inc(k_low, 1)
            v.wait_ge(q_made, g + 1)
            v.tensor_scalar(qn[:, :], q_ps[:, :], 0.0, None, ALU.min).then_inc(q_low, 1)
            v.wait_ge(k_exp, g + 1)
            for half in range(2):
                flat = lambda t: t[:, 2 * half:2 * half + 2, :, :].rearrange("p j h d -> p j (h d)")
                ins = v.scalar_tensor_tensor(flat(ks), kv_ps[:, half, :, 0, :, :].rearrange("p j h d -> p j (h d)"), 0.0,
                                             flat(ke), ALU.max, ALU.add)
            ins.then_inc(k_kept, 1)
            v.wait_ge(q_exp, g + 1)
            v.scalar_tensor_tensor(qs[:, :], q_ps[:, :], 0.0, qe[:, :], ALU.max, ALU.add).then_inc(q_kept, 1)
            v.wait_ge(weights_in, 16 * (len(loads) - 3))
            v.wait_ge(zero1, 1)
            v.wait_ge(zero2, 1)
            v.wait_ge(summed, g + 1)
            for kept, w, o in ((den_kept, den_w, D), (num_kept, num_w, 0)):
                for h in range(2):
                    r = slice(h * D, (h + 1) * D)
                    for b in range(2):
                        ins = v.tensor_tensor(w[r, b::2, r], sum_ps[r, b, :, h, o:o + D], heads[r, 0:TJ, :], ALU.mult)
                    ins.then_inc(kept, 1)
            v.wait_ge(den_made, g + 1)
            v.tensor_scalar(den[:, :], den_ps[:, :], 1e-6, None, ALU.add).then_inc(guarded, 1)
            v.wait_ge(guarded, g + 1)
            v.reciprocal(den[:, :], den[:, :]).then_inc(inverted, 1)
            v.wait_ge(inverted, g + 1)
            v.wait_ge(num_made, g + 1)
            v.scalar_tensor_tensor(msg[:, :], num_ps[:, :], float(T), den[:, :], ALU.mult, ALU.mult).then_inc(messaged, 1)
            n_1.vector(v, m1[:, :], g)
            v.wait_ge(n_1.normed, g + 1)
            v.tensor_scalar(m1[:, :], m1[:, :], gb[:, 0:1], gb[:, 1:2], ALU.mult, ALU.add).then_inc(tuned1, 1)
            n_2.vector(v, m2[:, :], g)
            v.wait_ge(n_2.normed, g + 1)
            v.tensor_scalar(m2[:, :], m2[:, :], gb[:, 2:3], gb[:, 3:4], ALU.mult, ALU.add).then_inc(tuned2, 1)
            v.wait_ge(tuned2, g + 1)
            v.tensor_tensor(m2[:, :], xg[:, :], m2[:, :], ALU.add).then_inc(added, 1)
            v.wait_ge(added, g + 1)
            v.tensor_tensor(hs[:, :], xg[:, :], m2[:, :], ALU.add).then_inc(added2, 1)
            v.wait_ge(added2, g + 1)
            v.tensor_copy(xg[:, :], padded_group(con, g + 1)).then_inc(grouped, 1)
            n_o.vector(v, group(X, g), g)

    st.end()



LAYERS = 2
ROUTED = LAYERS * P + LAYERS


def fetch_experts(sp, routed, route, experts, routed_in):
    with sp.Fori(0, B) as b:
        e = sp.value_load(route[0:1, bass.ds(b, 1)], min_val=0, max_val=15)
        sp.dma_start(routed[:, bass.ds(b * ROUTED, ROUTED)], experts[:, bass.ds(e * ROUTED, ROUTED)]).then_inc(routed_in, 16)


def routed_mlp(nc, con, X, a):
    st = Stage(nc, "ffn1")
    NB = 2 * GB
    RING = 4
    wi, wo = st.sb("wi", [P, 2, P]), st.sb("wo", [P, 2, P])
    bi, bo, bs = st.sb("bi", [P, 1]), st.sb("bo", [P, 1]), st.sb("bs", [P, LAYERS])
    ws = st.sb("ws", [P, LAYERS, P])
    routed, routed_in = con["routed"], con["routed_in"]
    own = [st.sb(f"own{k}", [P, P]) for k in range(RING)]
    xg, sq, std, hs = [st.sb(n, [P, GC]) for n in ("xg", "sq", "std", "hs")]
    hid = [st.sb(f"hid{k}", [P, 2, GC]) for k in range(LAYERS + 1)]
    pre = st.sb("pre", [P, 2, GC])
    hid_ps = [st.ps(f"hid_ps{h}", [P, GC]) for h in range(2)]
    out_ps, cp, vp = st.ps("out_ps", [P, GC]), st.ps("cp", [P, GC]), st.ps("vp", [P, GC])
    weights_in, grouped, entered, copied = st.sems("weights_in grouped entered copied")
    used, residual, biased, layered, left, added = st.sems("used residual biased layered left added")
    n_o = Norm(st, "no", con, cp[:, :], vp[:, :], sq[:, :], std[:, :])
    loads = [(wi[:, :, :], "wi"), (wo[:, :, :], "wo"), (bi[:, :], "bi"), (bo[:, :], "bo"), (bs[:, :], "bs"), (ws[:, :, :], "ws")]
    block = st.ctx.enter_context(nc.Block())

    @block.sync
    def _(sp):
        for dst, src in loads:
            sp.dma_start(dst, a[f"ffn1_{src}"]).then_inc(weights_in, 16)
        load_toeplitz(sp, con, a["att2_c"])

    @block.tensor
    def _(pe):
        pe.wait_ge(weights_in, 16 * len(loads))

        def enter(g):
            pe.wait_ge(grouped, g + 1)
            for h in range(2):
                mm = pe.matmul(hid_ps[h][:, :], wi[:, h, :], xg[:, :], start=True, stop=True)
            mm.then_inc(entered, 1)

        enter(0)
        with pe.Fori(0, G) as g:
            for l in range(LAYERS):
                pe.wait_ge(layered, g * 2 * (LAYERS + 1) + 2 * l + 2)
                for h in range(2):
                    pe.matmul(hid_ps[h][:, :], ws[:, l, :], hid[l][:, h, :], start=True, stop=False)
                for n in range(NB):
                    h, b = n // GB, n % GB
                    m = l * NB + n
                    pe.wait_ge(copied, g * LAYERS * NB + m + 1)
                    cols = slice(b * T, (b + 1) * T)
                    pe.matmul(hid_ps[h][:, cols], own[m % RING][:, :], hid[l][:, h, cols], start=False,
                              stop=b == GB - 1).then_inc(used, 1)
            pe.wait_ge(layered, (g + 1) * 2 * (LAYERS + 1))
            for h in range(2):
                mm = pe.matmul(out_ps[:, :], wo[:, h, :], hid[LAYERS][:, h, :], start=h == 0, stop=h == 1)
            mm.then_inc(left, 1)
            n_o.tensor_centre(pe, hs[:, :], added, g)
            enter(g + 1)
            n_o.tensor_average(pe, g)

    @block.scalar
    def _(act):
        act.wait_ge(weights_in, 16 * len(loads))
        act.wait_ge(routed_in, 16 * B)
        act.preload_act_table_set(LN_EXP)
        with act.Fori(0, G) as g:
            def copy(m):
                l, h, b = m // NB, m % NB // GB, m % GB
                if m >= RING:
                    act.wait_ge(used, g * LAYERS * NB + m - RING + 1)
                src = routed[:, bass.ds(((h * G * GB + b) * ROUTED + l * P) + g * (GB * ROUTED), P)]
                act.activation(own[m % RING][:, :], src, ACT.Copy).then_inc(copied, 1)

            act.wait_ge(entered, g + 1)
            for h in range(2):
                act.activation(hid[0][:, h, :], hid_ps[h][:, :], ACT.Relu, bias=bi[:, 0:1]).then_inc(layered, 1)
            for l in range(LAYERS):
                for n in range(NB):
                    copy(l * NB + n)
                for h in range(2):
                    act.wait_ge(biased, g * 2 * LAYERS + 2 * l + h + 1)
                    act.activation(hid[l + 1][:, h, :], pre[:, h, :], ACT.Relu, bias=bs[:, l:l + 1]).then_inc(layered, 1)
            n_o.scalar(act, g)

    @block.vector
    def _(v):
        v.wait_ge(weights_in, 16 * len(loads))
        v.wait_ge(routed_in, 16 * B)
        v.tensor_copy(xg[:, :], X[:, 0:GC]).then_inc(grouped, 1)
        with v.Fori(0, G) as g:
            for l in range(LAYERS):
                for h in range(2):
                    k = g * 2 * LAYERS + 2 * l + h + 1
                    v.wait_ge(used, g * LAYERS * NB + (l * 2 + h + 1) * GB)
                    v.tensor_tensor(pre[:, h, :], hid_ps[h][:, :], hid[l][:, h, :], ALU.add).then_inc(residual, 1)
                    v.wait_ge(residual, k)
                    own_bias = routed[:, bass.ds((h * G * GB * ROUTED) + g * (GB * ROUTED), GB * ROUTED)].rearrange(
                        "p (b c) -> p b c", c=ROUTED)[:, :, LAYERS * P + l:LAYERS * P + l + 1].to_broadcast((P, GB, T))
                    p3 = pre[:, h, :].rearrange("p (b t) -> p b t", t=T)
                    v.tensor_tensor(p3, p3, own_bias, ALU.add).then_inc(biased, 1)
            v.wait_ge(left, g + 1)
            v.scalar_tensor_tensor(hs[:, :], out_ps[:, :], bo[:, 0:1], xg[:, :], ALU.add, ALU.add).then_inc(added, 1)
            v.wait_ge(added, g + 1)
            v.tensor_copy(xg[:, :], padded_group(con, g + 1)).then_inc(grouped, 1)
            n_o.vector(v, group(X, g), g)

    st.end()


class Convolution:

    def __init__(self, st, con):
        self.con = con
        self.xt, self.yt = st.sb("xt", [P, HALF]), st.sb("yt", [P, HALF])
        self.back_ps, self.conv_ps = st.ps("back_ps", [P, HALF]), st.ps("conv_ps", [P, HALF])
        self.turned, self.kept, self.made, self.made_kept, self.back = st.sems("turned kept made made_kept back")

    def banks(self, ps):
        return [ps[:, k * GC:(k + 1) * GC] for k in range(G)]

    def tensor(self, pe, src, src_ready, matrices):
        for q in range(G):
            if src_ready is not None:
                pe.wait_ge(src_ready, q + 1)
            for c in range(q * GC, (q + 1) * GC, P):
                mm = pe.transpose(self.back_ps[:, c:c + P], src[:, c:c + P], self.con["ident"])
            mm.then_inc(self.turned, 1)
        pe.wait_ge(self.con["toeplitz_in"], 32 * matrices)
        pe.wait_ge(self.kept, G)
        cols = self.xt[:, :].rearrange("p (n f) -> p f n", f=D)
        N = HALF // D
        for q in range(G):
            for f in range(q * D // G, (q + 1) * D // G):
                mm = pe.matmul(self.conv_ps[:, f * N:(f + 1) * N], self.con["toeplitz"][:, f, :], cols[:, f, :], start=True, stop=True)
            mm.then_inc(self.made, 1)
        pe.wait_ge(self.made_kept, G)
        for q in range(G):
            for c in range(q * GC, (q + 1) * GC, P):
                mm = pe.matmul(self.back_ps[:, c:c + P], self.yt[:, c:c + P], self.con["flip"], start=True, stop=True)
            mm.then_inc(self.back, 1)

    def scalar(self, act):
        for q in range(G):
            act.wait_ge(self.turned, q + 1)
            act.activation(self.xt[:, q * GC:(q + 1) * GC], self.back_ps[:, q * GC:(q + 1) * GC], ACT.Copy).then_inc(self.kept, 1)

    def vector(self, v):
        rows = self.yt[:, :].rearrange("p (n f) -> p n f", f=D)
        for q in range(G):
            v.wait_ge(self.made, q + 1)
            v.tensor_copy(rows[:, :, q * D // G:(q + 1) * D // G],
                          self.conv_ps[:, q * GC:(q + 1) * GC].rearrange("p (f n) -> p n f", f=D // G)).then_inc(self.made_kept, 1)


def load_toeplitz(sp, con, reversed_taps):
    skewed = bass.AP(reversed_taps.tensor, reversed_taps.offset, [[1, T], [2 * T, D], [1, T]])
    for b in range(2):
        sp.dma_start(con["toeplitz"][b * T:(b + 1) * T, :, b * T:(b + 1) * T], skewed).then_inc(con["toeplitz_in"], 16)


def third_attention(nc, con, X, a):
    st = Stage(nc, "att2")
    DT = 1.0 / T
    par = st.sb("par", [P, 4])
    rx, rz = st.sb("rx", [P, T]), st.sb("rz", [P, T])
    rz_turned, taps = st.sb("rz_turned", [T, P]), st.sb("taps", [P, 2 * T])
    tx, tz = st.sb("tx", [P, T // 2]), st.sb("tz", [P, T // 2])
    p_, q_, aq, t1, t2 = [st.sb(n, [P, 1]) for n in ("p_", "q_", "aq", "t1", "t2")]
    hs, sq, std = [[st.sb(f"{n}{k}", [P, GC])[:, :] for k in range(G)] for n in ("hs", "sq", "std")]
    par_in, chained, added, responded, turned, turned_kept, flipped, taps_kept, stored = st.sems(
        "par_in chained added responded response_turned response_kept flipped taps_kept stored")
    conv = Convolution(st, con)
    n_o = Norm(st, "no", con, conv.banks(conv.conv_ps), conv.banks(conv.back_ps), sq, std)
    block = st.ctx.enter_context(nc.Block())

    @block.sync
    def _(sp):
        sp.dma_start(par[:, :], a["att3_par"]).then_inc(par_in, 16)
        sp.wait_ge(taps_kept, 1)
        sp.dma_start(con["taps"], taps[0:D, :]).then_inc(stored, 16)
        sp.wait_ge(stored, 16)

    @block.tensor
    def _(pe):
        conv.tensor(pe, X, None, 1)
        n_o.tensor_all(pe, hs, added)
        pe.wait_ge(responded, 1)
        pe.transpose(conv.back_ps[0:T, 0:P], rz[:, :], con["ident"]).then_inc(turned, 1)
        pe.wait_ge(turned_kept, 1)
        pe.matmul(conv.back_ps[:, GC:GC + T], rz_turned[:, :], con["flip"][0:T, 0:T], start=True, stop=True).then_inc(flipped, 1)

    @block.scalar
    def _(act):
        act.preload_act_table_set(LN_EXP)
        conv.scalar(act)
        n_o.scalar_all(act)
        act.wait_ge(turned, 1)
        act.activation(rz_turned[:, :], conv.back_ps[0:T, 0:P], ACT.Copy).then_inc(turned_kept, 1)

    @block.vector
    def _(v):
        count = 0

        def link(ins):
            nonlocal count
            count += 1
            ins.then_inc(chained, 1)
            v.wait_ge(chained, count)

        acol, h = par[:, 0:1], rz[:, :]

        def start_response():
            link(v.tensor_scalar(t1[:, :], acol, DT * DT, 1.0, ALU.mult, ALU.add))
            link(v.reciprocal(p_[:, :], t1[:, :]))
            link(v.tensor_scalar(q_[:, :], p_[:, :], DT, None, ALU.mult))
            link(v.tensor_copy(rx[:, 0:1], q_[:, :]))
            link(v.tensor_scalar(h[:, 0:1], q_[:, :], DT, None, ALU.mult))

        def double_response(m):
            link(v.tensor_tensor(aq[:, :], acol, q_[:, :], ALU.mult))
            link(v.tensor_scalar(tx[:, 0:m], h[:, 0:m], aq[:, 0:1], None, ALU.mult))
            link(v.tensor_scalar(tz[:, 0:m], h[:, 0:m], p_[:, 0:1], None, ALU.mult))
            link(v.scalar_tensor_tensor(h[:, m:2 * m], rx[:, 0:m], q_[:, 0:1], tz[:, 0:m], ALU.mult, ALU.add))
            link(v.scalar_tensor_tensor(rx[:, m:2 * m], rx[:, 0:m], p_[:, 0:1], tx[:, 0:m], ALU.mult, ALU.subtract))
            link(v.tensor_tensor(t1[:, :], aq[:, :], q_[:, :], ALU.mult))
            link(v.tensor_scalar(t2[:, :], p_[:, :], q_[:, 0:1], 2.0, ALU.mult, ALU.mult))
            link(v.scalar_tensor_tensor(p_[:, :], p_[:, :], p_[:, 0:1], t1[:, :], ALU.mult, ALU.subtract))
            link(v.tensor_copy(q_[:, :], t2[:, :]))

        v.memset(taps[:, T:2 * T], 0.0)
        v.wait_ge(par_in, 16)
        start_response()
        double_response(1)
        conv.vector(v)
        for g in range(G):
            v.wait_ge(conv.back, g + 1)
            v.tensor_tensor(hs[g], X[:, g * GC:(g + 1) * GC], conv.back_ps[:, g * GC:(g + 1) * GC], ALU.add).then_inc(added, 1)
        for g in range(G):
            double_response(2 << g)
            n_o.vector(v, X[:, g * GC:(g + 1) * GC], g)
        double_response(32)
        v.nop().then_inc(responded, 1)
        v.wait_ge(flipped, 1)
        v.tensor_copy(taps[:, 0:T], conv.back_ps[:, GC:GC + T]).then_inc(taps_kept, 1)

    st.end()


def fourth_attention(nc, con, X, a):
    st = Stage(nc, "att3")
    wb, wc, wd = st.sb("wb", [P, P]), st.sb("wc", [P, P]), st.sb("wd", [P, P])
    par = st.sb("par", [P, 4])
    bcd = st.sb("bcd", [P, 1])
    u, y = st.sb("u", [P, HALF]), st.sb("y", [P, HALF])
    gx, xs, sg, hs = [[st.sb(f"{n}{k}", [P, GC])[:, :] for k in range(G)] for n in ("gx", "xs", "sg", "hs")]
    weights_in, u_made, u_kept, y_kept, biased, out_made, gelued, sigmoided = st.sems(
        "weights_in u_made u_kept y_kept biased out_made gelued sigmoided")
    gated, added, added2 = st.sems("gated added added2")
    conv = Convolution(st, con)
    bank = conv.banks(conv.conv_ps)
    n_o = Norm(st, "no", con, bank, conv.banks(conv.back_ps), xs, sg, False)
    loads = [(wb[:, :], "wb"), (wc[:, :], "wc"), (wd[:, :], "wd"), (par[:, :], "par")]
    block = st.ctx.enter_context(nc.Block())

    @block.sync
    def _(sp):
        for dst, src in loads:
            sp.dma_start(dst, a[f"att3_{src}"]).then_inc(weights_in, 16)

    @block.tensor
    def _(pe):
        pe.wait_ge(weights_in, 16 * len(loads))
        for k in range(G):
            pe.matmul(bank[k], wb[:, :], X[:, k * GC:(k + 1) * GC], start=True, stop=True).then_inc(u_made, 1)
        conv.tensor(pe, u, u_kept, 2)
        for g in range(G):
            cols = slice(g * GC, (g + 1) * GC)
            pe.wait_ge(y_kept, g + 1)
            pe.matmul(bank[g], wc[:, :], y[:, cols], start=True, stop=False)
            pe.matmul(bank[g], wd[:, :], X[:, cols], start=False, stop=True).then_inc(out_made, 1)
        n_o.tensor_all(pe, hs, added2)

    @block.scalar
    def _(act):
        act.wait_ge(weights_in, 16 * len(loads))
        for k in range(G):
            act.wait_ge(u_made, k + 1)
            act.activation(u[:, k * GC:(k + 1) * GC], bank[k], ACT.Identity, bias=par[:, 1:2]).then_inc(u_kept, 1)
        conv.scalar(act)
        act.wait_ge(biased, 1)
        for g in range(G):
            act.wait_ge(out_made, g + 1)
            act.activation(gx[g], bank[g], ACT.Gelu, bias=bcd[:, 0:1]).then_inc(gelued, 1)
        for g in range(G):
            act.wait_ge(gelued, g + 1)
            act.activation(sg[g], gx[g], ACT.Sigmoid).then_inc(sigmoided, 1)
        act.preload_act_table_set(LN_EXP)
        n_o.scalar_all(act)

    @block.vector
    def _(v):
        v.wait_ge(weights_in, 16 * len(loads))
        v.tensor_tensor(bcd[:, :], par[:, 2:3], par[:, 3:4], ALU.add).then_inc(biased, 1)
        conv.vector(v)
        for q in range(G):
            v.wait_ge(conv.back, q + 1)
            v.tensor_copy(y[:, q * GC:(q + 1) * GC], conv.back_ps[:, q * GC:(q + 1) * GC]).then_inc(y_kept, 1)
        for g in range(G):
            x = X[:, g * GC:(g + 1) * GC]
            v.wait_ge(sigmoided, g + 1)
            v.tensor_tensor(xs[g], gx[g], sg[g], ALU.mult).then_inc(gated, 1)
            v.wait_ge(gated, g + 1)
            v.tensor_tensor(xs[g], xs[g], x, ALU.add).then_inc(added, 1)
            v.wait_ge(added, g + 1)
            v.tensor_tensor(hs[g], xs[g], x, ALU.add).then_inc(added2, 1)
        for g in range(G):
            n_o.vector(v, X[:, g * GC:(g + 1) * GC], g)

    st.end()


EDGES = 262144
EW = EDGES // P
CH = 8
CHUNKS = EW // CH
STEPS = 4
EIGHTH = EW // 8
SIFT_ROUNDS = 3
SIFTED = 8 * 2 * SIFT_ROUNDS * 2 * CH
EARLY = (3, 2) * 4
LATE = (1,) * 8
FIXED_ROUNDS = G // 2 * sum(EARLY) + G * sum(LATE)


def sift_edges(con):
    PAIR = 2 * CH

    def work_of(st):
        top, carrier = st.sb("sift_top", [P, PAIR]), st.sb("sift_carrier", [P, PAIR])
        topped, taken, stored = st.sems("sift_topped sift_taken sift_stored")

        def work(v, g, e):
            for j in range(SIFT_ROUNDS):
                want = g * (8 * SIFT_ROUNDS) + e * SIFT_ROUNDS + j + 1
                parts = [con["left"][:, q * EIGHTH:(q + 1) * EIGHTH] for q in (e, (e + 4) % 8)]
                for w, part in enumerate(parts):
                    ins = v.max(top[:, w * CH:(w + 1) * CH], part)
                ins.then_inc(topped, 1)
                v.wait_ge(topped, want)
                v.tensor_copy(carrier[:, :], top[:, :])
                for w, part in enumerate(parts):
                    ins = v.match_replace(part, top[:, w * CH:(w + 1) * CH], part, 0.0)
                ins.then_inc(taken, 1)
                v.tensor_copy(con["left"][:, bass.ds(g * (8 * SIFT_ROUNDS * PAIR) + (EW + (e * SIFT_ROUNDS + j) * PAIR), PAIR)],
                              top[:, :]).then_inc(stored, 1)
                v.wait_ge(taken, want)
                v.wait_ge(stored, want)
                v.memset(carrier[:, 0:1], 0.0)

        return work

    return work_of


def gather_edges(con, rounds, first_group, done):
    def work_of(st):
        top, carrier = st.sb("take_top", [P, CH]), st.sb("take_carrier", [P, CH])
        topped, taken, stored = st.sems("take_topped take_taken take_stored")
        sifted = con["left"][:, EW:EW + SIFTED]

        def work(v, g, e):
            for j in range(rounds[e]):
                n = g * sum(rounds) + (sum(rounds[:e]) + j - first_group * sum(rounds))
                v.max(top[:, :], sifted).then_inc(topped, 1)
                v.wait_ge(topped, n + 1)
                v.tensor_copy(carrier[:, :], top[:, :])
                v.match_replace(sifted, top[:, :], sifted, 0.0).then_inc(taken, 1)
                v.tensor_copy(con["keys"][:, bass.ds(n * CH + done * CH, CH)], top[:, :]).then_inc(stored, 1)
                v.wait_ge(taken, n + 1)
                v.wait_ge(stored, n + 1)
                v.memset(carrier[:, 0:1], 0.0)

        return work

    return work_of


class LeftEdges:

    def __init__(self, st, con):
        self.con = con
        self.inside = st.sb("inside", [P, EW + SIFTED])
        self.top, self.spare = st.sb("left_top", [P, CH]), st.sb("left_spare", [P, CH])
        self.most, self.most_i = st.sb("left_most", [P, 4]), st.sb("left_most_i", [P, 4], I32)
        self.number = st.sb("left_number", [P, 4])
        self.counted, self.maxed, self.most_kept, self.topped, self.taken, self.stored = st.sems(
            "left_counted left_maxed left_most_kept left_topped left_taken left_stored")

    def pool(self, pool):
        pool.wait_ge(self.counted, 1)
        pool.partition_all_reduce(self.most[:, :], self.number[:, :], P, bass.bass_isa.ReduceOp.max).then_inc(self.maxed, 1)

    def vector(self, v, link):
        FRONT = FIXED_ROUNDS * CH
        left, inside, number, most, most_i, top, spare = (
            self.con["left"], self.inside, self.number, self.most, self.most_i, self.top, self.spare)
        link(v.tensor_scalar(inside[:, :], left, 0.0, None, ALU.is_gt))
        link(v.tensor_reduce(number[:, 1:2], inside[:, :], AX, ALU.add))
        link(v.tensor_scalar(number[:, 0:1], number[:, 1:2], 1.0, float(FRONT), ALU.min, ALU.mult))
        link(v.tensor_tensor(number[:, 0:1], number[:, 0:1], number[:, 1:2], ALU.add))
        link(v.tensor_tensor(spare[:, 0:1], self.con["edge_count"], number[:, 1:2], ALU.subtract))
        link(v.tensor_tensor(number[:, 0:1], number[:, 0:1], spare[:, 0:1], ALU.max))
        link(v.tensor_scalar(inside[:, 0:FRONT], self.con["keys"][:, 0:FRONT], float(TOK * TOK // 2), None, ALU.is_gt))
        link(v.tensor_reduce(number[:, 2:3], inside[:, 0:FRONT], AX, ALU.add))
        link(v.tensor_scalar(number[:, 3:4], number[:, 2:3], -1.0, None, ALU.mult))
        link(v.tensor_scalar(spare[:, 1:2], number[:, 1:2], 1.0, float(EW), ALU.min, ALU.mult))
        v.tensor_scalar(number[:, 2:4], number[:, 2:4], spare[:, 1:2], None, ALU.add).then_inc(self.counted, 1)
        v.wait_ge(self.maxed, 1)
        link(v.tensor_scalar(most[:, 2:3], most[:, 2:3], float(EW), None, ALU.min))
        link(v.tensor_scalar(most[:, 3:4], most[:, 3:4], -1.0, 0.0, ALU.mult, ALU.max))
        link(v.tensor_copy(most_i[:, :], most[:, :]))
        v.tensor_copy(self.con["most"], most_i[:, :]).then_inc(self.most_kept, 1)
        n = v.value_load(most_i[0:1, 1:2], min_val=0, max_val=EW)
        with v.If(n > 0):
            with v.Fori(0, (CHUNKS - FIXED_ROUNDS) // STEPS) as k:
                with v.If(n > k * (CH * STEPS)):
                    for j in range(STEPS):
                        v.max(top[:, :], left).then_inc(self.topped, 1)
                        v.wait_ge(self.topped, k * STEPS + j + 1)
                        v.tensor_copy(spare[:, :], top[:, :])
                        v.match_replace(left, top[:, :], left, 0.0).then_inc(self.taken, 1)
                        v.tensor_copy(self.con["keys"][:, bass.ds(k * (CH * STEPS) + (j * CH + FRONT), CH)], top[:, :]).then_inc(self.stored, 1)
                        v.wait_ge(self.taken, k * STEPS + j + 1)
                        v.wait_ge(self.stored, k * STEPS + j + 1)
                        v.memset(spare[:, 0:1], 0.0)


HEADS, GE = 4, 4
GF = HEADS * GE
NF = GF + HEADS
HI = TOK // P
AHEAD = 4
RUN = 8


def graph_attention(nc, con, X, a):
    st = Stage(nc, "gat")
    TILES = HALF // P
    BF16 = mybir.dt.bfloat16
    rows_dram = nc.dram_tensor("gat_rows", (TOK, NF), F32, kind="Internal").ap()
    wg = st.sb("wg", [P, 2 * GF])
    att = st.sb("att", [P, 2, HI, GF])
    norm_par = st.sb("norm_par", [P, 3, HI, GF])
    iota = st.sb("iota", [P, P])
    rowt = st.sb("rowt", [P, HI, NF])
    prod = st.sb("prod", [P, 2, HI, GF])
    ad, shift, selfw = [st.sb(n, [P, HI, HEADS]) for n in ("ad", "shift", "selfw")]
    amax1, amax = st.sb("amax1", [P, HEADS]), st.sb("amax", [P, HEADS])
    rest = st.sb("rest", [P, 2, HI, HEADS])
    adp = st.sb("adp", [P, 3, HI * HEADS], BF16)
    words = [st.sb(f"words{k}", [P, EW + CH * AHEAD], I32) for k in range(2)]
    srci = st.sb("srci", [P, EW + CH * AHEAD], U32)
    low, high = st.sb("low", [P, EW + CH * AHEAD]), st.sb("high", [P, EW + CH * AHEAD])
    index = [st.sb(f"index{k}", [P, CH], U32) for k in range(AHEAD)]
    rows = [st.sb(f"rows{k}", [P, CH, NF]) for k in range(AHEAD)]
    oh_low = [st.sb(f"oh_low{k}", [P, CH, P]) for k in range(AHEAD)]
    oh_high = [st.sb(f"oh_high{k}", [P, CH, HI]) for k in range(AHEAD)]
    turned_b = st.sb("turned_b", [P, CH * P], BF16)
    picked = st.sb("picked", [P, CH, HI, HEADS])
    ade, edge, bound = [st.sb(n, [P, CH, HEADS]) for n in ("ade", "edge", "bound")]
    value = [st.sb(f"value{k}", [P, CH, NF]) for k in range(AHEAD)]
    spread = [st.sb(f"spread{k}", [P, CH, HI, NF]) for k in range(2)]
    zeros, spare = st.sb("zeros", [P, GC]), st.sb("spare", [P, 2])
    std_t = st.sb("std", [P, HI])
    std = std_t[:, :]
    feat_ps = st.ps("feat_ps", [P, TILES, 2, GF])
    turn_ps = st.ps("turn_ps", [P, CH * P])
    gat_ps = st.ps("gat_ps", [P, CH, HI * HEADS])
    sum_ps = st.ps("sum_ps", [P, 2, GC])
    HB = HI // 2
    weights_in, chained, featured, tables, maxed, self_ready, self_done, rows_out, zero_set = st.sems(
        "weights_in chained featured tables maxed self_ready self_done rows_out zero_set")
    staged, onehot, turned, turned_kept, target_out, target_read = st.sems(
        "staged onehot turned turned_kept target_out target_read")
    scored, weighted, valued, spreaded, scattered, indexed, prepared, reduced, step1, step2, step3, step4, all_done = st.sems(
        "scored weighted valued spreaded scattered indexed prepared reduced step1 step2 step3 step4 all_done")
    rooted, rooted_in, carried = st.sems("rooted rooted_in carried")
    gathered = [st.sem(f"gathered{k}") for k in range(AHEAD)]
    loads = [(wg[:, :], "wg"), (att[:, :, :, :], "att"), (norm_par[:, :, :, :], "norm"), (iota[:, :], "iota")]
    block = st.ctx.enter_context(nc.Block())

    edges = LeftEdges(st, con)

    def chunks(eng, body, by_half=False):
        eng.wait_ge(edges.most_kept, 1)
        n = eng.value_load(con["most"][0:1, 0:1], min_val=0, max_val=EW)
        if by_half:
            upper_end = eng.value_load(con["most"][0:1, 2:3], min_val=0, max_val=EW)
            lower_start = eng.value_load(con["most"][0:1, 3:4], min_val=0, max_val=EW)
        with eng.Fori(0, CHUNKS // AHEAD // RUN) as o:
            with eng.If(n > o * (RUN * AHEAD * CH)):
                with eng.Fori(0, RUN) as i:
                    first = o * (RUN * AHEAD * CH) + i * (AHEAD * CH)

                    def step(*halves):
                        for k in range(AHEAD):
                            body(o * (RUN * AHEAD) + i * AHEAD + k, k, o * RUN + i, *halves)

                    with eng.If(n > first):
                        if by_half:
                            with eng.If(lower_start > first + (AHEAD * CH - 1)):
                                step((1,))
                            with eng.If(upper_end > first):
                                with eng.If(lower_start < first + AHEAD * CH):
                                    step((0, 1))
                                eng.nop()
                            with eng.If(upper_end < first + 1):
                                step((0,))
                            eng.nop()
                        else:
                            step()
        return n

    @block.sync
    def _(sp):
        for dst, src in loads:
            sp.dma_start(dst, a[f"gat_{src}"]).then_inc(weights_in, 16)
        sp.wait_ge(tables, 1)
        sp.dma_start(rows_dram.rearrange("(h p) f -> p h f", p=P), rowt[:, :, :]).then_inc(rows_out, 16)
        sp.wait_ge(rows_out, 16)

    @block.gpsimd
    def _(pool):
        pool.memset(spare[:, :], 0.0).then_inc(carried, 1)
        pool.wait_ge(carried, 1)
        edges.pool(pool)
        pool.wait_ge(maxed, 1)
        pool.partition_all_reduce(amax[:, :], amax1[:, :], P, bass.bass_isa.ReduceOp.max).then_inc(maxed, 1)
        pool.wait_ge(rows_out, 16)

        def gather(want, k):
            pool.wait_ge(staged, want)
            pool.wait_ge(carried, want)
            pool.tensor_tensor(spare[:, 1:2], spare[:, 0:1], spare[:, 0:1], ALU.add).then_inc(carried, 1)
            for t in range(CH):
                pool.indirect_dma_start(rows[k][:, t, :], None, rows_dram,
                                        bass.IndirectOffsetOnAxis(ap=index[k][:, t:t + 1], axis=0)).then_inc(gathered[k], 16)

        for c in range(AHEAD):
            gather(c + 1, c)
        chunks(pool, lambda c, k, i: gather(c + AHEAD + 1, k))

    @block.tensor
    def _(pe):
        pe.wait_ge(weights_in, 16 * len(loads))
        for n in range(TILES):
            mm = pe.matmul(feat_ps[:, n, :, :].rearrange("p h f -> p (h f)"), X[:, n * P:(n + 1) * P], wg[:, :], start=True, stop=True)
        mm.then_inc(featured, 1)
        pe.wait_ge(zero_set, 1)
        for w in range(2):
            pe.matmul(sum_ps[:, w, :], zeros[:, 0:P], zeros[:, :], start=True, stop=False,
                      skip_group_check=True).then_inc(scattered, 1)

        def turn(want, k):
            pe.wait_ge(onehot, want)
            for t in range(CH):
                mm = pe.transpose(turn_ps[:, t * P:(t + 1) * P], oh_low[k][:, t, :], con["ident"])
            mm.then_inc(turned, 1)

        def targets(want, k):
            pe.wait_ge(turned_kept, want)
            for t in range(CH):
                for part in range(3):
                    mm = pe.matmul(gat_ps[:, t, :], turned_b[:, t * P:(t + 1) * P], adp[:, part, :], start=part == 0, stop=part == 2)
            mm.then_inc(target_out, 1)

        pe.wait_ge(prepared, 1)
        turn(1, 0)
        targets(1, 0)

        def chunk(c, k, i, halves):
            turn(c + 2, (k + 1) % AHEAD)
            for t in range(CH):
                pe.wait_ge(spreaded, c * CH + t + 1)
                for w in halves:
                    mm = pe.matmul(sum_ps[:, w, 0:HB * NF], oh_low[k][:, t, :],
                                   spread[k % 2][:, t, w * HB:(w + 1) * HB, :].rearrange("p h f -> p (h f)"),
                                   start=False, stop=False, skip_group_check=True)
                if t == 1:
                    pe.wait_ge(target_read, c + 1)
                    targets(c + 2, (k + 1) % AHEAD)
            mm.then_inc(scattered, 1)

        chunks(pe, chunk, by_half=True)
        for w in range(2):
            mm = pe.matmul(sum_ps[:, w, :], zeros[:, 0:P], zeros[:, :], start=False, stop=True, skip_group_check=True)
        mm.then_inc(all_done, 1)

    @block.scalar
    def _(act):
        act.wait_ge(indexed, 1)

        def stage(c, k):
            act.activation(index[k][:, :], srci[:, bass.ds(c * CH, CH)], ACT.Copy).then_inc(staged, 1)

        for c in range(AHEAD):
            stage(c, c)
        act.wait_ge(self_ready, 1)
        act.activation(selfw[:, :, :], selfw[:, :, :], ACT.Exp).then_inc(self_done, 1)

        def turned_copy(want):
            act.wait_ge(turned, want)
            act.activation(turned_b[:, :], turn_ps[:, :], ACT.Copy).then_inc(turned_kept, 1)

        turned_copy(1)

        def chunk(c, k, i):
            act.wait_ge(scored, c + 1)
            act.activation(value[k][:, :, GF:NF], edge[:, :, :], ACT.Exp).then_inc(weighted, 1)
            act.wait_ge(target_out, c + 1)
            turned_copy(c + 2)
            act.wait_ge(valued, c + 1)
            stage(c + AHEAD, k)

        chunks(act, chunk)
        act.wait_ge(rooted_in, 1)
        act.activation(std, std,
                       ACT.Sqrt, bias=con["eps"]).then_inc(rooted, 1)

    @block.vector
    def _(v):
        count = 0

        def link(ins):
            nonlocal count
            count += 1
            ins.then_inc(chained, 1)
            v.wait_ge(chained, count)

        f2 = lambda t: t.rearrange("p h f -> p (h f)")
        v.memset(zeros[:, :], 0.0).then_inc(zero_set, 1)
        edges.vector(v, link)
        for w in words:
            link(v.memset(w[:, EW:EW + CH * AHEAD], -1))
        link(v.tensor_scalar(words[0][:, 0:EW], con["keys"], -1.0, None, ALU.add))
        link(v.tensor_scalar(words[1][:, :], words[0][:, :], TOK - 1, None, ALU.bitwise_and))
        link(v.tensor_copy(srci[:, :], words[1][:, :]))
        v.nop().then_inc(indexed, 1)
        v.wait_ge(weights_in, 16 * len(loads))
        v.wait_ge(featured, 1)
        feats = rowt[:, :, HEADS:NF]
        for h in range(2):
            link(v.tensor_copy(feats[:, h * TILES:(h + 1) * TILES, :], feat_ps[:, :, h, :]))
        for w, dst in ((0, rowt[:, :, 0:HEADS]), (1, ad[:, :, :])):
            link(v.tensor_tensor(prod[:, w, :, :], feats, att[:, w, :, :], ALU.mult))
            link(v.tensor_reduce(dst, prod[:, w, :, :].rearrange("p n (h x) -> p n h x", x=GE), AX, ALU.add))
        v.nop().then_inc(tables, 1)
        v.tensor_reduce(amax1[:, :], rowt[:, :, 0:HEADS].rearrange("p n h -> p h n"), AX, ALU.max).then_inc(maxed, 1)
        link(v.tensor_scalar(words[1][:, :], words[0][:, :], 12, P - 1, ALU.logical_shift_right, ALU.bitwise_and))
        link(v.tensor_copy(low[:, :], words[1][:, :]))
        link(v.tensor_scalar(words[1][:, :], words[0][:, :], 19, None, ALU.arith_shift_right))
        link(v.tensor_copy(high[:, :], words[1][:, :]))
        link(v.tensor_copy(adp[:, 0, :], f2(ad[:, :, :])))
        link(v.tensor_tensor(f2(rest[:, 0, :, :]), f2(ad[:, :, :]), adp[:, 0, :], ALU.subtract))
        link(v.tensor_copy(adp[:, 1, :], f2(rest[:, 0, :, :])))
        link(v.tensor_tensor(f2(rest[:, 1, :, :]), f2(rest[:, 0, :, :]), adp[:, 1, :], ALU.subtract))
        link(v.tensor_copy(adp[:, 2, :], f2(rest[:, 1, :, :])))
        v.nop().then_inc(prepared, 1)

        def leaky(dst, src):
            return v.scalar_tensor_tensor(dst, src, 0.2, src, ALU.mult, ALU.max)

        v.wait_ge(maxed, 2)
        link(v.tensor_tensor(shift[:, :, :], ad[:, :, :], amax[:, None, :].to_broadcast((P, HI, HEADS)), ALU.add))
        link(leaky(shift[:, :, :], shift[:, :, :]))
        link(v.tensor_tensor(selfw[:, :, :], rowt[:, :, 0:HEADS], ad[:, :, :], ALU.add))
        link(leaky(selfw[:, :, :], selfw[:, :, :]))
        v.tensor_tensor(selfw[:, :, :], selfw[:, :, :], shift[:, :, :], ALU.subtract).then_inc(self_ready, 1)

        def high_hot(c, k):
            return v.tensor_tensor(oh_high[k][:, :, :], high[:, bass.ds(c * CH, CH)][:, :, None].to_broadcast((P, CH, HI)),
                                   iota[:, None, 0:HI].to_broadcast((P, CH, HI)), ALU.is_equal)

        def low_hot(c, k):
            v.tensor_tensor(oh_low[k][:, :, :], low[:, bass.ds(c * CH, CH)][:, :, None].to_broadcast((P, CH, P)),
                            iota[:, None, :].to_broadcast((P, CH, P)), ALU.is_equal).then_inc(onehot, 1)

        high_hot(0, 0)
        low_hot(0, 0)

        def chunk(c, k, i, halves):
            highs = slice(halves[0] * HB, (halves[-1] + 1) * HB)
            v.wait_ge(target_out, c + 1)
            v.tensor_tensor(picked[:, :, :, :], gat_ps[:, :, :].rearrange("p c (h x) -> p c h x", x=HEADS),
                            oh_high[k][:, :, :, None].to_broadcast((P, CH, HI, HEADS)), ALU.mult).then_inc(target_read, 1)
            high_hot(c + 1, (k + 1) % AHEAD)
            v.wait_ge(target_read, c + 1)
            v.tensor_reduce(ade[:, :, :], picked[:, :, :, :].rearrange("p c h x -> p c x h"), AX, ALU.add).then_inc(reduced, 1)
            v.wait_ge(gathered[k], (i + 1) * (16 * CH))
            v.wait_ge(reduced, c + 1)
            v.tensor_tensor(edge[:, :, :], rows[k][:, :, 0:HEADS], ade[:, :, :], ALU.add).then_inc(step1, 1)
            v.tensor_tensor(bound[:, :, :], ade[:, :, :], amax[:, None, :].to_broadcast((P, CH, HEADS)), ALU.add).then_inc(step2, 1)
            v.wait_ge(step1, c + 1)
            leaky(edge[:, :, :], edge[:, :, :]).then_inc(step3, 1)
            v.wait_ge(step2, c + 1)
            leaky(bound[:, :, :], bound[:, :, :]).then_inc(step4, 1)
            v.wait_ge(step3, c + 1)
            v.wait_ge(step4, c + 1)
            v.tensor_tensor(edge[:, :, :], edge[:, :, :], bound[:, :, :], ALU.subtract).then_inc(scored, 1)
            low_hot(c + 1, (k + 1) % AHEAD)
            v.wait_ge(weighted, c + 1)
            v.tensor_tensor(value[k][:, :, 0:GF].rearrange("p c (h x) -> p c h x", x=GE),
                            rows[k][:, :, HEADS:NF].rearrange("p c (h x) -> p c h x", x=GE),
                            value[k][:, :, GF:NF][:, :, :, None].to_broadcast((P, CH, HEADS, GE)), ALU.mult).then_inc(valued, 1)
            v.wait_ge(valued, c + 1)
            v.wait_ge(scattered, c + 1)
            for t in range(CH):
                shape = (P, highs.stop - highs.start, NF)
                v.tensor_tensor(spread[k % 2][:, t, highs, :], oh_high[k][:, t, highs, None].to_broadcast(shape),
                                value[k][:, t, None, :].to_broadcast(shape), ALU.mult).then_inc(spreaded, 1)

        n = chunks(v, chunk, by_half=True)
        v.wait_ge(all_done, 1)
        v.wait_ge(self_done, 1)
        for k in range(AHEAD):
            v.wait_ge(gathered[k], ((n + (AHEAD * CH - 1)) // (AHEAD * CH)) * (16 * CH) + 16 * CH)
        msg, den = prod[:, 0, :, :], shift[:, :, :]
        sums = lambda w: sum_ps[:, w, 0:HB * NF].rearrange("p (h f) -> p h f", f=NF)
        link(v.tensor_tensor(msg.rearrange("p n (h x) -> p n h x", x=GE), feats.rearrange("p n (h x) -> p n h x", x=GE),
                             selfw[:, :, :, None].to_broadcast((P, HI, HEADS, GE)), ALU.mult))
        for w in range(2):
            part = slice(w * HB, (w + 1) * HB)
            link(v.tensor_tensor(msg[:, part, :], msg[:, part, :], sums(w)[:, :, 0:GF], ALU.add))
            link(v.tensor_tensor(den[:, part, :], selfw[:, part, :], sums(w)[:, :, GF:NF], ALU.add))
        link(v.tensor_scalar(den, den, 1e-16, None, ALU.add))
        link(v.reciprocal(den, den))
        link(v.tensor_tensor(msg.rearrange("p n (h x) -> p n h x", x=GE), msg.rearrange("p n (h x) -> p n h x", x=GE),
                             den[:, :, :, None].to_broadcast((P, HI, HEADS, GE)), ALU.mult))
        link(v.tensor_tensor(msg, msg, norm_par[:, 0, :, :], ALU.add))
        mean, cen = ad[:, :, 0], prod[:, 1, :, :]
        link(v.tensor_reduce(mean, msg, AX, ALU.add))
        link(v.tensor_scalar(mean, mean, 1.0 / GF, None, ALU.mult))
        bc = lambda t: t[:, :, None].to_broadcast((P, HI, GF))
        link(v.tensor_tensor(cen, msg, bc(mean), ALU.subtract))
        link(v.tensor_tensor(msg, cen, cen, ALU.mult))
        link(v.tensor_reduce(std, msg, AX, ALU.add))
        v.tensor_scalar(std, std, 1.0 / GF, None, ALU.mult).then_inc(rooted_in, 1)
        v.wait_ge(rooted, 1)
        link(v.reciprocal(std, std))
        link(v.tensor_tensor(cen, cen, bc(std), ALU.mult))
        link(v.tensor_tensor(cen, cen, norm_par[:, 1, :, :], ALU.mult))
        link(v.tensor_tensor(cen, cen, norm_par[:, 2, :, :], ALU.add))
        link(v.tensor_reduce(ad[:, :, :], cen.rearrange("p n (h x) -> p n x h", x=GE), AX, ALU.add))
        for h in range(2):
            link(v.tensor_scalar(con["scores"][:, 0:HI * GE].rearrange("p (j h x) -> p h j x", h=2, x=GE)[:, h], ad[:, h * TILES:(h + 1) * TILES, :],
                                 1.0 / HEADS, None, ALU.mult))

    st.end()


def fourth_experts(nc, con, X, a):
    experts(nc, con, X, a, "ffn3", 4, 1, ACT.Gelu, scored=con["scores"])


def build(nc, a, out):
    with ExitStack() as ctx:
        padded = ctx.enter_context(nc.sbuf_tensor("X", [P, GC + HALF + GC], F32))
        X = padded[:, GC:GC + HALF]
        consts = ctx.enter_context(nc.sbuf_tensor("consts", [P, 6 * P + 8], F32))
        con = {"consts": consts[:, :], "padded": padded}
        for n, name in enumerate(("ident", "centre", "average", "mean128", "ones", "flip")):
            con[name] = consts[:, n * P:(n + 1) * P]
        con["eps"] = consts[:, 6 * P:6 * P + 1]
        keys = ctx.enter_context(nc.sbuf_tensor("keys", [P, EW], F32))
        most = ctx.enter_context(nc.sbuf_tensor("most", [P, 4], I32))
        scores = ctx.enter_context(nc.sbuf_tensor("scores", [P, HI * GE + 2 * TJ * GE], F32))
        con["scores"] = scores[:, :]
        con["keys"], con["most"] = keys[:, :], most[:, :]
        left = ctx.enter_context(nc.sbuf_tensor("left", [P, EW + SIFTED], F32))
        edge_count = ctx.enter_context(nc.sbuf_tensor("edge_count", [P, 1], F32))
        con["left"], con["edge_count"] = left[:, :], edge_count[:, :]
        early = Stage(nc, "routed")
        con["routed"], con["route"] = early.sb("experts", [P, B * ROUTED])[:, :], early.sb("route", [1, B], I32)[:, :]
        con["routed_in"], con["route_in"] = early.sems("experts_in route_in")
        con["taps"] = nc.dram_tensor("taps", (D, 2 * T), F32, kind="Internal").ap()
        tokenizer(nc, con, X, a)
        stages = STAGE_LIST()
        for n, stage in enumerate(stages):
            if n < STAGES:
                stage(nc, con, X, a)
            if stage is first_experts:
                late = Stage(nc, "toeplitz")
                con["toeplitz"] = late.sb("matrices", [P, D, P])[:, :, :]
                con["toeplitz_in"] = late.sem("in")
            if stage is fourth_attention:
                late.end()
                early.end()
        finish(nc, con, X, out)


def STAGE_LIST():
    return [first_attention, first_experts, second_attention, routed_mlp,
            third_attention, third_experts, fourth_attention,
            graph_attention, fourth_experts]


def constants(np):
    eye = np.eye(P, dtype=np.float32)
    half = np.kron(np.eye(2), np.ones((D, D))).astype(np.float32) / D
    t = np.arange(P)
    s, u = t[:, None], t[None, :]
    decay = np.where((s // T == u // T) & (s < u), 0.97 ** np.maximum(u - s - 1.0, 0), 0).astype(np.float32)
    tail = np.zeros((P, 8), np.float32)
    tail[:, 0] = EPS
    return {
        "consts": np.concatenate([eye, eye - half, half, np.full((P, P), 1 / P, np.float32), np.ones((P, P), np.float32),
                                  np.kron(np.eye(2), np.eye(T)[:, ::-1]).astype(np.float32), tail], 1),
        "decay": np.tile(decay, (1, TJ)),
        "later": np.tile((np.arange(2 * GC) % T != 0).astype(np.float32), (P, 1)),
        "into_row": np.broadcast_to(np.eye(2 * GB, dtype=np.float32), (P, 2 * GB, 2 * GB)),
    }


def kernel(**inputs):
    import numpy as np
    import concourse.bacc as bacc
    from concourse.bass_utils import run_bass_kernel_spmd

    i = {k: np.asarray(v) for k, v in inputs.items()}

    def rows(w):
        z = np.zeros((P, 2) + w.shape[1:], w.dtype)
        z[:D, 0], z[D:, 1] = w, w
        return z

    def cols(w):
        z = np.zeros((w.shape[0], 2, P), w.dtype)
        z[:, 0, :D], z[:, 1, D:] = w, w
        return z

    def both(w):
        n = w.shape[1]
        z = np.zeros((P, 2 * n), w.dtype)
        z[:D, :n], z[D:, n:] = w, w
        return z

    def twice(w):
        return np.concatenate([w, w], 0)

    arrays = constants(np)
    arrays["x"] = i["x"].reshape(TOK, D * 4)
    arrays["tok"] = np.concatenate([i["L0_tok_W"], i["L0_tok_b"][:, None]], 1)
    arrays["dx"] = rows(i["L0_attn_Dx"].T)
    arrays["dy"] = rows(i["L0_attn_Dy"].T)
    arrays["e_rows"] = cols(i["L0_attn_E"].T).reshape(2, P, 2, P).transpose(3, 2, 0, 1)

    def thrice(w):
        z = np.zeros((3, PART) + w.shape[1:], w.dtype)
        z[:, :w.shape[0]] = w
        return z.reshape((3 * PART,) + w.shape[1:])

    def moe(name, w1, b1, w2, b2, wr=None, biases=()):
        E, _, hidden = w1.shape
        hc = hidden // P
        arrays[f"{name}_w1"] = rows(w1.transpose(1, 0, 2))
        arrays[f"{name}_w2"] = cols(w2.reshape(E * hidden, D)).reshape(E, hc, P, 2, P).transpose(2, 0, 1, 3, 4)
        arrays[f"{name}_b1"] = b1.reshape(E, hc, P).transpose(2, 0, 1)
        z = np.zeros((2, E, P), np.float32)
        z[0, :, :D], z[1, :, D:] = b2, b2
        arrays[f"{name}_b2"] = thrice(z.reshape(2 * E, P))
        if wr is not None:
            arrays[f"{name}_wr"] = both(wr)
            biases = list(biases) + [np.zeros(E, np.float32)] * (2 - len(biases))
            arrays[f"{name}_br"] = np.broadcast_to(np.stack(biases)[None, :, None], (P, 2, 2 * TJ, E))

    moe("ffn0", i["L0_ffn_W1"], i["L0_ffn_b1"], i["L0_ffn_W2"], i["L0_ffn_b2"], i["L0_ffn_Wr"], [i["L0_ffn_br"]])
    arrays["ffn0_scale"], arrays["ffn0_shift"] = twice(i["L0_ffn_ln_g"].T), twice(i["L0_ffn_ln_b"].T)
    moe("ffn2", i["L2_ffn_W1"], i["L2_ffn_b1"], i["L2_ffn_W2"], i["L2_ffn_b2"], i["L2_ffn_Wg"], [i["L2_ffn_bg"], i["L2_ffn_bias"]])
    moe("ffn3", i["L3_ffn_W1"], i["L3_ffn_b1"], i["L3_ffn_W2"], i["L3_ffn_b2"])
    for E in (4, 8):
        z = np.zeros((2, E, E, P), np.float32)
        for e in range(E):
            z[0, e, e, :D], z[1, e, e, D:] = 1, 1
        arrays[f"sel{E}"] = thrice(z.reshape(2 * E, E, P))
        arrays[f"index{E}"] = np.broadcast_to(np.arange(E, dtype=np.float32), (P, 2 * TJ, E))

    arrays["att1_wq"] = both(i["L1_attn_Wq"])
    arrays["att1_turned_w"] = np.stack([both(i["L1_attn_Wm"]).T] + list(cols(i["L1_attn_W2"]).transpose(1, 2, 0)), 1)
    arrays["att1_wkv"] = np.concatenate([both(i["L1_attn_Wk"]), both(i["L1_attn_Wv"])], 1)
    arrays["att1_w1x"], arrays["att1_w1m"] = rows(i["L1_attn_W1"][:D]), rows(i["L1_attn_W1"][D:])
    arrays["att1_gb"] = twice(np.stack([i[f"L1_attn_{n}"] for n in ("g1", "b1", "g2", "b2")], 1))
    arrays["att1_heads"] = np.broadcast_to(np.tile(np.kron(np.eye(8), np.ones((8, 8))), (2, 1)).astype(np.float32)[:, None], (P, GB, D))
    arrays["ffn1_wi"], arrays["ffn1_wo"] = rows(i["L1_ffn_Wi"].T), cols(i["L1_ffn_Wo"].T)
    arrays["ffn1_bi"], arrays["ffn1_bo"] = i["L1_ffn_bi"][:, None], twice(i["L1_ffn_bo"][:, None])
    arrays["ffn1_bs"] = i["L1_ffn_bs"][:, 0].T
    arrays["ffn1_ws"] = i["L1_ffn_Ws"][:, 0].transpose(2, 0, 1)
    arrays["route"] = i["L1_ffn_route_id"][None]
    E = i["L1_ffn_Wr"].shape[1]
    arrays["ffn1_experts"] = np.concatenate(
        [i["L1_ffn_Wr"].transpose(3, 1, 0, 2).reshape(P, E, LAYERS * P), i["L1_ffn_br"].transpose(2, 1, 0)], 2).reshape(P, E * ROUTED)
    arrays["att2_c"] = np.concatenate([i["L2_attn_c"][0][:, ::-1], np.zeros((D, T), np.float32)], 1)
    for n in "BCD":
        arrays[f"att3_w{n.lower()}"] = both(i[f"L3_attn_W_{n}"].T)
    arrays["att3_par"] = twice(np.stack([i[f"L3_attn_{n}"] for n in ("a", "b_B", "b_C", "b_D")], 1))
    edges = i["L3_ffn_edge_index"].reshape(2, P, EW)
    arrays["edge_src"], arrays["edge_dst"] = edges[0], edges[1]
    arrays["gat_wg"] = both(i["L3_ffn_W_gat"])
    across = lambda *w: np.broadcast_to(np.stack([x.reshape(GF) for x in w])[None, :, None], (P, len(w), HI, GF))
    arrays["gat_att"] = across(i["L3_ffn_att_src"], i["L3_ffn_att_dst"])
    arrays["gat_norm"] = across(i["L3_ffn_b_gat"], i["L3_ffn_ln_gamma"], i["L3_ffn_ln_beta"])
    arrays["gat_iota"] = np.broadcast_to(np.arange(P, dtype=np.float32), (P, P))
    nc = bacc.Bacc("TRN2", target_bir_lowering=False, num_devices=1)
    arrays = {f"in_{k}": np.ascontiguousarray(v) for k, v in arrays.items()}
    a = {k[3:]: nc.dram_tensor(k, v.shape, mybir.dt.from_np(v.dtype), kind="ExternalInput").ap() for k, v in arrays.items()}
    out = nc.dram_tensor("out", (TOK, D), F32, kind="ExternalOutput").ap()
    build(nc, a, out)
    r = run_bass_kernel_spmd(nc, [arrays], core_ids=[0])
    return r.results[0]["out"].reshape(B, T, D)
```
